# Optimizing a Trainium2 kernel written in Bass

```python
import numpy as np
import jax
import jax.numpy as jnp

def _softmax(x, axis=-1):
    return jax.nn.softmax(x, axis=axis)

def _gelu(x):
    return jax.nn.gelu(x, approximate=True)

def _silu(x):
    return jax.nn.silu(x)

def _sigmoid(x):
    return jax.nn.sigmoid(x)

def _layernorm(x, axis=-1, eps=1e-05):
    m = jnp.mean(x, axis=axis, keepdims=True)
    v = jnp.var(x, axis=axis, keepdims=True)
    return (x - m) / jnp.sqrt(v + eps)

def _scatter_add(tgt, idx, src, axis=0):
    return tgt.at[idx].add(src)

def _segment_sum(src, seg, n):
    return jax.ops.segment_sum(src, seg, n)
kernel_name = 'mk_recurrent_d1_jaxref_r8_66a63f'

def setup_inputs(seed: int=0):
    np.random.seed(seed)
    _w = jnp.asarray

    def _L0_attn_setup():
        import jax, jax.numpy as jnp
        import numpy as np
        H, HKV, D, BS, NSEL, WIN = (32, 8, 64, 64, 16, 64)
        N_REP = H // HKV

        def precompute_freqs(dim, max_seq_len, theta=10000.0):
            inv = 1.0 / theta ** (np.arange(0, dim, 2, dtype=np.float32) / dim)
            t = np.arange(max_seq_len, dtype=np.float32)
            return jnp.asarray(np.outer(t, inv))

        def apply_rope(x, freqs):
            T = x.shape[1]
            xr = x.reshape(x.shape[:-1] + (-1, 2))
            cos = jnp.cos(freqs[:T])[None, :, None, :]
            sin = jnp.sin(freqs[:T])[None, :, None, :]
            x0, x1 = (xr[..., 0], xr[..., 1])
            out = jnp.stack([x0 * cos - x1 * sin, x0 * sin + x1 * cos], axis=-1)
            return out.reshape(x.shape)
        key = jax.random.key(seed)
        ks = jax.random.split(key, 9)
        d_model = 256
        s = lambda fan_in: 1.0 / np.sqrt(fan_in)
        return {'x': jax.random.normal(ks[0], (1, 256, d_model), jnp.float32), 'W_q': jax.random.normal(ks[1], (d_model, H * D), jnp.float32) * s(d_model), 'W_k': jax.random.normal(ks[2], (d_model, HKV * D), jnp.float32) * s(d_model), 'W_v': jax.random.normal(ks[3], (d_model, HKV * D), jnp.float32) * s(d_model), 'W_o': jax.random.normal(ks[4], (H * D, d_model), jnp.float32) * s(H * D), 'W_ck': jax.random.normal(ks[5], (BS * D, D), jnp.float32) * s(BS * D), 'W_cv': jax.random.normal(ks[6], (BS * D, D), jnp.float32) * s(BS * D), 'W_imp': jax.random.normal(ks[7], (D, 1), jnp.float32) * s(D), 'W_gate': jax.random.normal(ks[8], (d_model, 3), jnp.float32) * s(d_model)}
    _L0_attn_in = _L0_attn_setup()

    def _L0_ffn_setup():
        import jax, jax.numpy as jnp
        import numpy as np
        BLOCK_SIZE = 32
        HIDDEN_SIZE = 256
        MLP_DIM = 2048
        NVFP4_LUT = jnp.array([0.0, 0.5, 1.0, 1.5, 2.0, 3.0, 4.0, 6.0, 0.0, -0.5, -1.0, -1.5, -2.0, -3.0, -4.0, -6.0], dtype=jnp.float32)

        def dequant_nvfp4(W_packed, scales, block=BLOCK_SIZE):
            N = W_packed.shape[0]
            low = W_packed & 15
            high = W_packed >> 4 & 15
            idx = jnp.stack([low, high], axis=-1).reshape(N, -1)
            vals = NVFP4_LUT[idx]
            K = vals.shape[1]
            vals = vals.reshape(N, K // block, block) * scales[:, :, None]
            return vals.reshape(N, K)
        key = jax.random.key(seed)
        ks = jax.random.split(key, 7)
        x = jax.random.normal(ks[0], (4, 32, HIDDEN_SIZE), dtype=jnp.float32)
        gate_W_packed = jax.random.randint(ks[1], (MLP_DIM, HIDDEN_SIZE // 2), 0, 32, dtype=jnp.int32)
        gate_scales = jax.random.uniform(ks[2], (MLP_DIM, HIDDEN_SIZE // BLOCK_SIZE), dtype=jnp.float32) * 0.1 + 0.001
        up_W_packed = jax.random.randint(ks[3], (MLP_DIM, HIDDEN_SIZE // 2), 0, 32, dtype=jnp.int32)
        up_scales = jax.random.uniform(ks[4], (MLP_DIM, HIDDEN_SIZE // BLOCK_SIZE), dtype=jnp.float32) * 0.1 + 0.001
        down_W_packed = jax.random.randint(ks[5], (HIDDEN_SIZE, MLP_DIM // 2), 0, 32, dtype=jnp.int32)
        down_scales = jax.random.uniform(ks[6], (HIDDEN_SIZE, MLP_DIM // BLOCK_SIZE), dtype=jnp.float32) * 0.1 + 0.001
        return {'x': x, 'gate_W_packed': gate_W_packed, 'gate_scales': gate_scales, 'up_W_packed': up_W_packed, 'up_scales': up_scales, 'down_W_packed': down_W_packed, 'down_scales': down_scales}
    _L0_ffn_in = _L0_ffn_setup()
    _d = {'L0_attn_x': _L0_attn_in['x'], 'L0_attn_W_q': _L0_attn_in['W_q'], 'L0_attn_W_k': _L0_attn_in['W_k'], 'L0_attn_W_v': _L0_attn_in['W_v'], 'L0_attn_W_o': _L0_attn_in['W_o'], 'L0_attn_W_ck': _L0_attn_in['W_ck'], 'L0_attn_W_cv': _L0_attn_in['W_cv'], 'L0_attn_W_imp': _L0_attn_in['W_imp'], 'L0_attn_W_gate': _L0_attn_in['W_gate'], 'L0_ffn_gate_W_packed': _L0_ffn_in['gate_W_packed'], 'L0_ffn_gate_scales': _L0_ffn_in['gate_scales'], 'L0_ffn_up_W_packed': _L0_ffn_in['up_W_packed'], 'L0_ffn_up_scales': _L0_ffn_in['up_scales'], 'L0_ffn_down_W_packed': _L0_ffn_in['down_W_packed'], 'L0_ffn_down_scales': _L0_ffn_in['down_scales']}
    _x0 = _d['L0_attn_x']
    _d['L0_attn_x'] = jax.random.normal(jax.random.fold_in(jax.random.key(seed), 1), (2, 1024, 256), dtype=_x0.dtype)
    del _x0
    return _d

def reference(L0_attn_x, L0_attn_W_q, L0_attn_W_k, L0_attn_W_v, L0_attn_W_o, L0_attn_W_ck, L0_attn_W_cv, L0_attn_W_imp, L0_attn_W_gate, L0_ffn_gate_W_packed, L0_ffn_gate_scales, L0_ffn_up_W_packed, L0_ffn_up_scales, L0_ffn_down_W_packed, L0_ffn_down_scales):

    def _L0_attn_ref(x, W_q, W_k, W_v, W_o, W_ck, W_cv, W_imp, W_gate):
        import jax, jax.numpy as jnp
        import numpy as np
        H, HKV, D, BS, NSEL, WIN = (32, 8, 64, 64, 16, 64)
        N_REP = H // HKV

        def precompute_freqs(dim, max_seq_len, theta=10000.0):
            inv = 1.0 / theta ** (np.arange(0, dim, 2, dtype=np.float32) / dim)
            t = np.arange(max_seq_len, dtype=np.float32)
            return jnp.asarray(np.outer(t, inv))

        def apply_rope(x, freqs):
            T = x.shape[1]
            xr = x.reshape(x.shape[:-1] + (-1, 2))
            cos = jnp.cos(freqs[:T])[None, :, None, :]
            sin = jnp.sin(freqs[:T])[None, :, None, :]
            x0, x1 = (xr[..., 0], xr[..., 1])
            out = jnp.stack([x0 * cos - x1 * sin, x0 * sin + x1 * cos], axis=-1)
            return out.reshape(x.shape)
        B, T, _ = x.shape
        S = T
        scale = 1.0 / np.sqrt(D)
        freqs = precompute_freqs(D, T)
        q = apply_rope((x @ W_q).reshape(B, T, H, D), freqs)
        k = apply_rope((x @ W_k).reshape(B, T, HKV, D), freqs)
        v = (x @ W_v).reshape(B, T, HKV, D)
        q = q.transpose(0, 2, 1, 3)
        k = k.transpose(0, 2, 1, 3)
        v = v.transpose(0, 2, 1, 3)
        nb = S // BS
        kb = k[:, :, :nb * BS].reshape(B, HKV, nb, BS * D)
        vb = v[:, :, :nb * BS].reshape(B, HKV, nb, BS * D)
        kc = jnp.repeat(kb @ W_ck, N_REP, axis=1)
        vc = jnp.repeat(vb @ W_cv, N_REP, axis=1)
        a_c = jax.nn.softmax(jnp.einsum('bhtd,bhnd->bhtn', q, kc) * scale, axis=-1)
        out_c = jnp.einsum('bhtn,bhnd->bhtd', a_c, vc)
        kx = jnp.repeat(k, N_REP, axis=1)
        vx = jnp.repeat(v, N_REP, axis=1)
        k_mean = k[:, :, :nb * BS].reshape(B, HKV, nb, BS, D).mean(axis=3)
        scores = (k_mean @ W_imp)[..., 0]
        _top = jax.lax.top_k(scores, NSEL)
        a_s = jax.nn.softmax(jnp.einsum('bhtd,bhsd->bhts', q, kx) * scale, axis=-1)
        out_s = jnp.einsum('bhts,bhsd->bhtd', a_s, vx)
        logits = jnp.einsum('bhtd,bhsd->bhts', q, kx) * scale
        i = jnp.arange(T)[:, None]
        j = jnp.arange(S)[None, :]
        allowed = (j <= S - T + i) & (j >= S - T + i - WIN + 1)
        logits = jnp.where(allowed[None, None], logits, -jnp.inf)
        a_w = jnp.nan_to_num(jax.nn.softmax(logits, axis=-1))
        out_w = jnp.einsum('bhts,bhsd->bhtd', a_w, vx)
        gates = jax.nn.softmax(x @ W_gate, axis=-1)
        stacked = jnp.stack([out_c.transpose(0, 2, 1, 3), out_s.transpose(0, 2, 1, 3), out_w.transpose(0, 2, 1, 3)], axis=3)
        out = (stacked * gates[:, :, None, :, None]).sum(axis=3).reshape(B, T, H * D)
        return out @ W_o

    def _L0_ffn_ref(x, gate_W_packed, gate_scales, up_W_packed, up_scales, down_W_packed, down_scales):
        import jax, jax.numpy as jnp
        import numpy as np
        BLOCK_SIZE = 32
        HIDDEN_SIZE = 256
        MLP_DIM = 2048
        NVFP4_LUT = jnp.array([0.0, 0.5, 1.0, 1.5, 2.0, 3.0, 4.0, 6.0, 0.0, -0.5, -1.0, -1.5, -2.0, -3.0, -4.0, -6.0], dtype=jnp.float32)

        def dequant_nvfp4(W_packed, scales, block=BLOCK_SIZE):
            N = W_packed.shape[0]
            low = W_packed & 15
            high = W_packed >> 4 & 15
            idx = jnp.stack([low, high], axis=-1).reshape(N, -1)
            vals = NVFP4_LUT[idx]
            K = vals.shape[1]
            vals = vals.reshape(N, K // block, block) * scales[:, :, None]
            return vals.reshape(N, K)
        B, S, H = x.shape
        xt = x.reshape(B * S, H)
        Wg = dequant_nvfp4(gate_W_packed, gate_scales)
        Wu = dequant_nvfp4(up_W_packed, up_scales)
        Wd = dequant_nvfp4(down_W_packed, down_scales)
        gate = jnp.einsum('th,nh->tn', xt, Wg)
        up = jnp.einsum('th,nh->tn', xt, Wu)
        gelu = jnp.tanh(0.7978845608028654 * (gate + 0.044715 * gate ** 3)) * gate * 0.5 + gate * 0.5
        inter = gelu * up
        out = jnp.einsum('tn,hn->th', inter, Wd)
        return out.reshape(B, S, H)
    x = L0_attn_x
    xn = _layernorm(x, axis=-1)
    s = _L0_attn_ref(xn, L0_attn_W_q, L0_attn_W_k, L0_attn_W_v, L0_attn_W_o, L0_attn_W_ck, L0_attn_W_cv, L0_attn_W_imp, L0_attn_W_gate)
    g = _silu(_L0_ffn_ref(xn, L0_ffn_gate_W_packed, L0_ffn_gate_scales, L0_ffn_up_W_packed, L0_ffn_up_scales, L0_ffn_down_W_packed, L0_ffn_down_scales))
    x = x + s * g
    return x

_drawn_inputs = setup_inputs


def setup_inputs(seed=0):
    import zlib

    import numpy as np

    out = dict(_drawn_inputs(seed))
    spreads = {}
    factors = {}
    for name, (base, spread) in spreads.items():
        noise = np.random.default_rng([zlib.crc32(name.encode()), seed]).standard_normal(out[name].shape)
        drawn = base * np.exp(spread * noise) if base else spread * noise
        out[name] = jnp.asarray(drawn.astype(out[name].dtype))
    for name, factor in factors.items():
        out[name] = (out[name] * factor).astype(out[name].dtype)
    return out
```

```python
from contextlib import ExitStack

import numpy as np
import concourse.bass as bass
from concourse import mybir

ALU = mybir.AluOpType
ACT = mybir.ActivationFunctionType
X = mybir.AxisListType.X
F32 = mybir.dt.float32
F32R = mybir.dt.float32r
BF16 = mybir.dt.bfloat16
I32 = mybir.dt.int32

P = 128
B, T, DM = 2, 1024, 256
H, HKV, D = 32, 8, 64
REP = H // HKV
BS = 64
NBLK = T // BS
WIN = 64
F = 2048
QB = 32
KT = DM // P
NTOK = B * T
TB = NTOK // P
TJ = T // P
CH = 512
NC = NTOK // CH
WW = P + WIN
NEG = -1.0e30
EPS = 1e-5


class Chain:

    def __init__(self, eng, sem):
        self.eng, self.sem, self.n, self.base = eng, sem, 0, 0

    def link(self, ins):
        ins.then_inc(self.sem, 1)
        self.n += 1
        self.eng.wait_ge(self.sem, self.base + self.n)


def f32(ap):
    return ap.bitcast(F32)


def build(nc, a, out, stop=99):
    main = ExitStack()

    def dram(name, shape, dt):
        return nc.dram_tensor(name, shape, dt).ap()

    q_scr = dram("q_scr", [HKV, B, 2, 2, P, T], F32)
    k_scr = dram("k_scr", [2, B, 2, 2, P, T], F32)
    vt_scr = dram("vt_scr", [4, B, 2, P, T], F32)
    pc_scr = dram("pc_scr", [HKV, P, T], F32)
    vc_scr = dram("vc_scr", [2, P, D], F32)
    o_scr = dram("o_scr", [B, H * D, T], F32)

    def sb(name, shape, dt, ctx=main):
        return ctx.enter_context(nc.sbuf_tensor(name, shape, dt))

    def sem(name, ctx=main):
        return ctx.enter_context(nc.semaphore(name))

    ps = main.enter_context(nc.psum_tensor("ps", [P, 8, CH], F32))
    ident = sb("ident_sb", [P, P], F32)
    gate_c = sb("gate_c", [P, TB], F32)
    ln_gate = sb("ln_gate", [P, 2, TB], F32)
    v_all = sb("v_all", [P, TB, HKV * D], F32)
    g_t = sb("g_t", [P, 2, NTOK], F32)
    kc_all = sb("kc_all", [P, 2, 2, NBLK * B * HKV], F32R)
    dense = ExitStack()
    xh = sb("xh", [P, KT, NTOK], F32R, dense)
    xl = sb("xl", [P, KT, NTOK], F32R, dense)
    x_tok = a["L0_attn_x"].rearrange("b (n p) d -> p (b n) d", p=P)

    def three(kt, wh, wl, xh_ap, xl_ap):
        return [(wh, xh_ap), (wl, xh_ap), (wh, xl_ap)]

    def norm_phase():
        with ExitStack() as c:
            xt = sb("xt", [P, TB, DM], F32, c)
            xn = sb("xn", [P, TB, DM], F32, c)
            st = sb("st", [P, TB, 6], F32, c)
            mv = sb("mv", [P, TB, 2], F32, c)
            rstd = sb("rstd", [P, TB], F32, c)
            wg = sb("wg", [P, KT, 3], F32, c)
            z = sb("z", [P, TB, 3], F32, c)
            ez = sb("ez", [P, TB, 3], F32, c)
            zs = sb("zs", [P, 3, TB], F32, c)
            x_in = [sem(f"x_in{q}", c) for q in range(4)]
            const_in = sem("n_const_in", c)
            stat = sem("n_stat", c)
            var_ready = sem("var_ready", c)
            std_ready = sem("std_ready", c)
            normed = sem("normed", c)
            turned = sem("n_turned", c)
            hi_done = sem("n_hi", c)
            lo_done = sem("n_lo", c)
            z_ready = sem("z_ready", c)
            shifted = sem("z_shifted", c)
            exped = sem("z_exped", c)
            summed = sem("z_summed", c)
            logged = sem("z_logged", c)
            blk = c.enter_context(nc.Block())

            @blk.sync
            def _(sp):
                for q in range(4):
                    sp.dma_start(xt[:, 4 * q:4 * q + 4, :], x_tok[:, 4 * q:4 * q + 4, :]).then_inc(x_in[q], 16)
                sp.dma_start(ident[:], a["ident"]).then_inc(const_in, 16)
                sp.dma_start(wg[:], a["L0_attn_W_gate"].rearrange("(k p) n -> p k n", p=P)).then_inc(const_in, 16)

            @blk.vector
            def _(dve):
                ch = Chain(dve, stat)
                for t in range(TB):
                    if t % 4 == 0:
                        dve.wait_ge(x_in[t // 4], 16)
                    dve.bn_stats(st[:, t, :], xt[:, t, :]).then_inc(stat, 1)
                dve.wait_ge(stat, TB)
                for t in range(TB):
                    dve.bn_aggr(mv[:, t, :], st[:, t, :]).then_inc(stat, 1)
                dve.wait_ge(stat, 2 * TB)
                ch.n = 2 * TB
                dve.tensor_scalar(rstd[:], mv[:, :, 1], EPS, None, ALU.add).then_inc(var_ready, 1)
                dve.wait_ge(std_ready, 1)
                ch.link(dve.reciprocal(rstd[:], rstd[:]))
                for t in range(TB):
                    dve.tensor_scalar(xn[:, t, :], xt[:, t, :], mv[:, t, 0:1], rstd[:, t:t + 1],
                                      ALU.subtract, ALU.mult).then_inc(normed, 1)
                for n in range(8):
                    kt, q = n // 4, n % 4
                    dve.wait_ge(hi_done, n + 1)
                    cols = slice(q * CH, (q + 1) * CH)
                    dve.tensor_tensor(xl[:, kt, cols], ps[:, n, :], f32(xh[:, kt, cols]), ALU.subtract).then_inc(lo_done, 1)
                dve.wait_ge(z_ready, 1)
                zp = ps[:, 0, 0:3 * TB].rearrange("p (t g) -> p t g", g=3)
                ch.link(dve.tensor_reduce(zs[:, 0, :], zp, X, ALU.max))
                dve.tensor_tensor(z[:], zp, zs[:, 0, :].unsqueeze(2).broadcast_to([P, TB, 3]), ALU.subtract).then_inc(shifted, 1)
                dve.wait_ge(exped, 1)
                dve.tensor_reduce(zs[:, 1, :], ez[:], X, ALU.add).then_inc(summed, 1)
                dve.wait_ge(summed, 1)
                ch.link(dve.reciprocal(zs[:, 0, :], zs[:, 1, :]))
                dve.tensor_tensor(gate_c[:], ez[:, :, 0], zs[:, 0, :], ALU.mult)
                dve.wait_ge(logged, 1)
                for br in range(2):
                    dve.tensor_tensor(ln_gate[:, br, :], z[:, :, 1 + br], zs[:, 2, :], ALU.subtract)

            @blk.scalar
            def _(act):
                act.wait_ge(var_ready, 1)
                act.activation(rstd[:], rstd[:], ACT.Sqrt).then_inc(std_ready, 1)
                for n in range(8):
                    kt, q = n // 4, n % 4
                    act.wait_ge(turned, n + 1)
                    act.activation(xh[:, kt, q * CH:(q + 1) * CH], ps[:, n, :], ACT.Copy).then_inc(hi_done, 1)
                act.wait_ge(shifted, 1)
                act.activation(ez[:], z[:], ACT.Exp).then_inc(exped, 1)
                act.wait_ge(summed, 1)
                act.activation(zs[:, 2, :], zs[:, 1, :], ACT.Ln).then_inc(logged, 1)

            @blk.tensor
            def _(pe):
                pe.wait_ge(const_in, 32)
                for n in range(8):
                    kt, q = n // 4, n % 4
                    pe.wait_ge(normed, 4 * q + 4)
                    for t in range(4):
                        ins = pe.transpose(ps[:, n, t * P:(t + 1) * P], xn[:, 4 * q + t, kt * P:(kt + 1) * P], ident[:])
                    ins.then_inc(turned, 1)
                pe.wait_ge(lo_done, 8)
                for t in range(TB):
                    for n, (kt, part) in enumerate((kt, part) for kt in range(KT) for part in (xh, xl)):
                        ins = pe.matmul(ps[:, 0, 3 * t:3 * t + 3], f32(part[:, kt, t * P:(t + 1) * P]), wg[:, kt, :],
                                        start=(n == 0), stop=(n == 3))
                ins.then_inc(z_ready, 1)

    def mlp_phase():
        with ExitStack() as c:
            names = ["gate", "up", "down"]
            NG = P * DM * 16 // P // QB
            hi = [sb(f"w_hi{m}", [P, 32, P], F32R, c) for m in names]
            lo = [sb(f"w_lo{m}", [P, 32, P], F32R, c) for m in names]
            deq = ExitStack()
            scl = sb("scl", [P, 3, P], F32, deq)
            room = v_all[:].rearrange("p t d -> p (t d)").rearrange("p (r n) -> p r n", r=4)
            packed, code, sign = (room[:, r, :].bitcast(I32) for r in range(3))
            u1 = room[:, 3, :]
            u2 = sb("u2", [P, 2048], F32, deq)
            w = sb("w", [P, 2048, 2], F32, deq)
            packed_in = sem("packed_in", c)
            scale_in = sem("scale_in", c)
            dch = sem("deq_chain", c)
            unpacked = sem("unpacked", c)
            w_ready = sem("w_ready", c)
            w_turned = sem("w_turned", c)
            w_hi_done = sem("w_hi_done", c)
            w_lo_done = sem("w_lo_done", c)
            with nc.Block() as blk:
                srcs = [(a[f"L0_ffn_{m}_W_packed"].rearrange("(n p) k -> p n k", p=P),
                         a[f"L0_ffn_{m}_scales"].rearrange("(n p) k -> p n k", p=P)) for m in names]

                @blk.sync
                def _(sp):
                    for m in range(3):
                        n = srcs[m][0].shape[1]
                        if m:
                            sp.wait_ge(unpacked, 4 * m)
                        sp.dma_start(packed.rearrange("p (n k) -> p n k", n=n), srcs[m][0]).then_inc(packed_in, 16)
                        sp.dma_start(scl[:, m, :].rearrange("p (n k) -> p n k", n=n), srcs[m][1]).then_inc(scale_in, 16)

                @blk.vector
                def _(dve):
                    ch = Chain(dve, dch)
                    for m in range(3):
                        dve.wait_ge(packed_in, 16 * (m + 1))
                        dve.wait_ge(scale_in, 16 * (m + 1))
                        ch.link(dve.tensor_scalar(scl[:, m, :], scl[:, m, :], 0.5, None, ALU.mult))
                        for half in range(2):
                            if m or half:
                                dve.wait_ge(w_ready, 2 * m + half)
                            dve.tensor_scalar(code, packed, 4 * half, 7, ALU.logical_shift_right,
                                              ALU.bitwise_and).then_inc(unpacked, 1)
                            dve.tensor_scalar(sign, packed, 3 + 4 * half, 31, ALU.logical_shift_right,
                                              ALU.logical_shift_left).then_inc(unpacked, 1)
                            dve.wait_ge(unpacked, 4 * m + 2 * half + 2)
                            dve.tensor_scalar(u1, code, 2.0, -4.0, ALU.mult, ALU.add)
                            ch.link(dve.tensor_scalar(u2[:], code, 4.0, -16.0, ALU.mult, ALU.add))
                            ch.link(dve.tensor_tensor(u1, u1, code, ALU.max))
                            ch.link(dve.tensor_tensor(u1, u1, u2[:], ALU.max))
                            u_blk = u1.rearrange("p (s k) -> p s k", k=QB // 2)
                            ch.link(dve.tensor_tensor(u_blk, u_blk, scl[:, m, :].unsqueeze(2).broadcast_to([P, P, QB // 2]),
                                                      ALU.mult))
                            if m and half == 0:
                                dve.wait_ge(w_turned, 8 * m)
                            dve.tensor_tensor(w[:, :, half].bitcast(I32), u1.bitcast(I32), sign,
                                              ALU.bitwise_or).then_inc(w_ready, 1)
                        for n in range(8):
                            dve.wait_ge(w_hi_done, 8 * m + n + 1)
                            dve.tensor_tensor(lo[m][:, 4 * n:4 * n + 4, :], ps[:, n, :].rearrange("p (c k) -> p c k", c=4),
                                              f32(hi[m][:, 4 * n:4 * n + 4, :]), ALU.subtract).then_inc(w_lo_done, 1)

                @blk.scalar
                def _(act):
                    for m in range(3):
                        for n in range(8):
                            act.wait_ge(w_turned, 8 * m + n + 1)
                            act.activation(hi[m][:, 4 * n:4 * n + 4, :], ps[:, n, :].rearrange("p (c k) -> p c k", c=4),
                                           ACT.Copy).then_inc(w_hi_done, 1)

                @blk.tensor
                def _(pe):
                    for m in range(3):
                        pe.wait_ge(w_ready, 2 * m + 2)
                        for n in range(8):
                            if m:
                                pe.wait_ge(w_lo_done, 8 * (m - 1) + n + 1)
                            for t in range(4):
                                wt = w[:].rearrange("p k two -> p (k two)")[:, (4 * n + t) * P:(4 * n + t + 1) * P]
                                ins = pe.transpose(ps[:, n, t * P:(t + 1) * P], wt, ident[:])
                            ins.then_inc(w_turned, 1)
            deq.close()

            NT = F // P
            steps = v_all[:].rearrange("p t d -> p (t d)").rearrange("p (r h n) -> p r h n", h=2, n=CH)
            sq, cub, th, hg, it, se = (steps[:, r] for r in range(6))
            ih = sb("ih", [P, 4, CH], F32R, c)
            il = sb("il", [P, 4, CH], F32R, c)
            gu_ready = sem("gu_ready", c)
            sq_ready = sem("sq_ready", c)
            cub_half = sem("cub_half", c)
            cub_ready = sem("cub_ready", c)
            th_ready = sem("th_ready", c)
            hg_ready = sem("hg_ready", c)
            it_ready = sem("it_ready", c)
            ih_ready = sem("ih_ready", c)
            il_ready = sem("il_ready", c)
            down_done = sem("down_done", c)
            se_ready = sem("se_ready", c)
            sch = sem("silu_chain", c)
            g_done = sem("g_done", c)
            with nc.Block() as blk:
                LAGD = 3

                @blk.tensor
                def _(pe):
                    def down(tc, n, first):
                        pe.wait_ge(il_ready, tc * NT + n + 1)
                        if n == 0 and not first:
                            pe.wait_ge(g_done, tc)
                        for ht in range(2):
                            w_i = ht * NT + n
                            prods = three(0, hi[2][:, w_i, :], lo[2][:, w_i, :], ih[:, n % 4, :], il[:, n % 4, :])
                            for k, (wt, xt) in enumerate(prods):
                                ins = pe.matmul(ps[:, 6 + ht, :], wt, xt, start=(n == 0 and k == 0),
                                                stop=(n == NT - 1 and k == 2))
                        ins.then_inc(down_done, 1)

                    def chunk(tc, first):
                        cols = bass.ds(tc * CH, CH)
                        for n in range(NT):
                            if n >= 3:
                                pe.wait_ge(it_ready, tc * NT + n - 2)
                            elif not first:
                                pe.wait_ge(it_ready, tc * NT)
                            for m in range(2):
                                k = 0
                                for kt in range(KT):
                                    w_i = 2 * n + kt
                                    for wt, xt in three(kt, hi[m][:, w_i, :], lo[m][:, w_i, :], xh[:, kt, cols], xl[:, kt, cols]):
                                        ins = pe.matmul(ps[:, 2 * (n % 3) + m, :], wt, xt, start=(k == 0), stop=(k == 5))
                                        k += 1
                            ins.then_inc(gu_ready, 1)
                            if n >= LAGD:
                                down(tc, n - LAGD, first)
                        for n in range(NT - LAGD, NT):
                            down(tc, n, first)

                    chunk(0, True)
                    with pe.Fori(1, NC) as tc:
                        chunk(tc, False)

                @blk.scalar
                def _(act):
                    def chunk(tc, first):
                        for n in range(NT + 2):
                            if n < NT:
                                act.wait_ge(gu_ready, tc * NT + n + 1)
                                if n >= 2:
                                    act.wait_ge(cub_half, tc * NT + n - 1)
                                act.activation(sq[:, n % 2, :], ps[:, 2 * (n % 3), :], ACT.Square).then_inc(sq_ready, 1)
                            if 1 <= n <= NT:
                                act.wait_ge(cub_ready, tc * NT + n)
                                act.activation(th[:, (n - 1) % 2, :], cub[:, (n - 1) % 2, :], ACT.Tanh,
                                               scale=0.7978845608028654).then_inc(th_ready, 1)
                            if n >= 2:
                                act.wait_ge(it_ready, tc * NT + n - 1)
                                if n >= 6:
                                    act.wait_ge(down_done, tc * NT + n - 5)
                                act.activation(ih[:, (n - 2) % 4, :], it[:, n % 2, :], ACT.Copy).then_inc(ih_ready, 1)
                        act.wait_ge(down_done, (tc + 1) * NT)
                        act.activation(se, ps[:, 6:8, :], ACT.Exp, scale=-1.0).then_inc(se_ready, 1)

                    chunk(0, True)
                    with act.Fori(1, NC) as tc:
                        chunk(tc, False)

                @blk.vector
                def _(dve):
                    ch = Chain(dve, sch)
                    def chunk(tc, first):
                        ch.n, ch.base = 0, tc * 2
                        for n in range(NT + 3):
                            if n < NT:
                                gp = ps[:, 2 * (n % 3), :]
                                dve.wait_ge(sq_ready, tc * NT + n + 1)
                                dve.tensor_scalar(sq[:, n % 2, :], sq[:, n % 2, :], 0.044715, 1.0, ALU.mult,
                                                  ALU.add).then_inc(cub_half, 1)
                                dve.wait_ge(cub_half, tc * NT + n + 1)
                                if n >= 2:
                                    dve.wait_ge(th_ready, tc * NT + n - 1)
                                dve.tensor_tensor(cub[:, n % 2, :], gp, sq[:, n % 2, :], ALU.mult).then_inc(cub_ready, 1)
                            if 1 <= n <= NT:
                                m = n - 1
                                dve.wait_ge(th_ready, tc * NT + m + 1)
                                dve.scalar_tensor_tensor(hg[:, m % 2, :], th[:, m % 2, :], 1.0, ps[:, 2 * (m % 3), :],
                                                         ALU.add, ALU.mult).then_inc(hg_ready, 1)
                                dve.wait_ge(hg_ready, tc * NT + m + 1)
                                if m >= 2:
                                    dve.wait_ge(ih_ready, tc * NT + m - 1)
                                dve.scalar_tensor_tensor(it[:, m % 2, :], hg[:, m % 2, :], 0.5, ps[:, 2 * (m % 3) + 1, :],
                                                         ALU.mult, ALU.mult).then_inc(it_ready, 1)
                            if 2 <= n <= NT + 1:
                                m = n - 2
                                dve.wait_ge(ih_ready, tc * NT + m + 1)
                                dve.tensor_tensor(il[:, m % 4, :], it[:, m % 2, :], f32(ih[:, m % 4, :]),
                                                  ALU.subtract).then_inc(il_ready, 1)
                        dve.wait_ge(se_ready, tc + 1)
                        ch.link(dve.tensor_scalar(se, se, 1.0, None, ALU.add))
                        ch.link(dve.reciprocal(se, se))
                        dve.tensor_tensor(g_t[:, :, bass.ds(tc * CH, CH)], ps[:, 6:8, :], se, ALU.mult).then_inc(g_done, 1)

                    chunk(0, True)
                    with dve.Fori(1, NC) as tc:
                        chunk(tc, False)

    def kv_phase():
        with ExitStack() as c:
            raw = sb("kv_raw", [P, 2, KT, HKV * D], F32, c)
            wk = [sb(f"wk{n}", [P, KT, 2, 2, P], F32R, c) for n in ("h", "l")]
            wv = [sb(f"wv{n}", [P, KT, HKV * D], F32R, c) for n in ("h", "l")]
            rot = sb("rot_k_sb", [P, 2, 2, T], F32, c)
            tu = sb("tu", [P, 2, 2, 2, CH], F32, c)
            ab = sb("ab", [P, 2, 2, CH], F32, c)
            kh = sb("kh", [P, 2, 2, CH], F32R, c)
            kl = sb("kl", [P, 2, 2, CH], F32R, c)
            vh = sb("vh", [P, 2, 2, CH], F32R, c)
            vl = sb("vl", [P, 2, 2, CH], F32R, c)
            kv_in = sem("kv_in", c)
            wh_done = sem("wh_done", c)
            wl_done = sem("wl_done", c)
            k_ready = sem("k_ready", c)
            vt_ready = sem("vt_ready", c)
            k_rot = sem("k_rot", c)
            k_sum = sem("k_sum", c)
            k_hi = sem("k_hi", c)
            k_lo = sem("k_lo", c)
            vt_hi = sem("vt_hi", c)
            vt_lo = sem("vt_lo", c)
            k_stored = [sem(f"k_stored{n}", c) for n in range(2)]
            vt_stored = [sem(f"vt_stored{n}", c) for n in range(2)]
            v_ready = sem("v_ready", c)
            v_done = sem("v_done", c)
            blk = c.enter_context(nc.Block())

            def k_view(ap):
                return ap.rearrange("p (g h i e) -> p g e h i", g=2, h=4, e=2)

            @blk.sync
            def _(sp):
                for n, w in enumerate(("W_k", "W_v")):
                    sp.dma_start(raw[:, n], a["L0_attn_" + w].rearrange("(k p) n -> p k n", p=P)).then_inc(kv_in, 16)
                sp.dma_start(rot[:], a["rot_k"]).then_inc(kv_in, 16)
                for b in range(B):
                    for half in range(2):
                        cols = slice(half * CH, (half + 1) * CH)
                        for n in range(2):
                            sp.wait_ge(vt_lo, 4 * b + 2 * half + n + 1)
                            for part, t in ((0, vh), (1, vl)):
                                dst = vt_scr[2 * n:2 * n + 2, b, part, :, cols].rearrange("j p t -> p j t")
                                sp.dma_start(dst, f32(t[:, n])).then_inc(vt_stored[n], 16)
                            sp.wait_ge(k_lo, 4 * b + 2 * half + n + 1)
                            for part, t in ((0, kh), (1, kl)):
                                dst = k_scr[n, b, part, :, :, cols].rearrange("e p t -> p e t")
                                sp.dma_start(dst, f32(t[:, n])).then_inc(k_stored[n], 16)
                for n in range(2):
                    sp.wait_ge(k_stored[n], 2 * 16 * 4)
                    sp.wait_ge(vt_stored[n], 2 * 16 * 4)

            @blk.tensor
            def _(pe):
                pe.wait_ge(wl_done, 6)
                for b in range(B):
                    for half in range(2):
                        cols = slice(b * T + half * CH, b * T + (half + 1) * CH)
                        for n in range(2):
                            if b or half:
                                pe.wait_ge(k_rot, 4 * b + 2 * half + n - 1)
                            for e in range(2):
                                k = 0
                                for kt in range(KT):
                                    for w, x in three(kt, wk[0][:, kt, n, e, :], wk[1][:, kt, n, e, :],
                                                      xh[:, kt, cols], xl[:, kt, cols]):
                                        ins = pe.matmul(ps[:, 2 * n + e, :], w, x, start=(k == 0), stop=(k == 5))
                                        k += 1
                            ins.then_inc(k_ready, 1)
                        for n in range(2):
                            if b or half:
                                pe.wait_ge(vt_lo, 4 * b + 2 * half + n - 1)
                            for e in range(2):
                                k = 0
                                ws = slice((2 * n + e) * P, (2 * n + e + 1) * P)
                                for kt in range(KT):
                                    for w, x in three(kt, wv[0][:, kt, ws], wv[1][:, kt, ws], xh[:, kt, cols], xl[:, kt, cols]):
                                        ins = pe.matmul(ps[:, 4 + 2 * n + e, :], w, x, start=(k == 0), stop=(k == 5))
                                        k += 1
                            ins.then_inc(vt_ready, 1)
                pe.wait_ge(k_rot, 8)
                pe.wait_ge(vt_lo, 8)
                for t in range(TB):
                    if t >= 8:
                        pe.wait_ge(v_done, t - 7)
                    k = 0
                    ts = slice(t * P, (t + 1) * P)
                    for kt in range(KT):
                        for x, w in three(kt, xh[:, kt, ts], xl[:, kt, ts], wv[0][:, kt, :], wv[1][:, kt, :]):
                            ins = pe.matmul(ps[:, t % 8, :], x, w, start=(k == 0), stop=(k == 5))
                            k += 1
                    ins.then_inc(v_ready, 1)

            @blk.scalar
            def _(act):
                act.wait_ge(kv_in, 48)
                for kt in range(KT):
                    for n in range(2):
                        act.activation(wk[0][:, kt, n].rearrange("p e (h i) -> p e h i", h=4), k_view(raw[:, 0, kt, :])[:, n],
                                       ACT.Copy).then_inc(wh_done, 1)
                for kt in range(KT):
                    act.activation(wv[0][:, kt, :], raw[:, 1, kt, :], ACT.Copy).then_inc(wh_done, 1)
                for b in range(B):
                    for half in range(2):
                        for n in range(2):
                            act.wait_ge(vt_ready, 4 * b + 2 * half + n + 1)
                            if b or half:
                                act.wait_ge(vt_stored[n], 64 * b + 32 * half)
                            act.activation(vh[:, n], ps[:, 4 + 2 * n:6 + 2 * n, :], ACT.Copy).then_inc(vt_hi, 1)
                            act.wait_ge(k_sum, 4 * b + 2 * half + n + 1)
                            if b or half:
                                act.wait_ge(k_stored[n], 64 * b + 32 * half)
                            act.activation(kh[:, n], ab[:, n], ACT.Copy).then_inc(k_hi, 1)
                for t in range(TB):
                    act.wait_ge(v_ready, t + 1)
                    act.activation(v_all[:, t, :], ps[:, t % 8, :], ACT.Copy).then_inc(v_done, 1)

            @blk.gpsimd
            def _(pool):
                for b in range(B):
                    for half in range(2):
                        for n in range(2):
                            pool.wait_ge(k_rot, 4 * b + 2 * half + n + 1)
                            if b or half:
                                pool.wait_ge(k_lo, 4 * b + 2 * half + n - 1)
                            pool.tensor_tensor(ab[:, n], tu[:, n, 0], tu[:, n, 1], ALU.add).then_inc(k_sum, 1)

            @blk.vector
            def _(dve):
                for kt in range(KT):
                    for n in range(2):
                        dve.wait_ge(wh_done, 2 * kt + n + 1)
                        dve.tensor_tensor(wk[1][:, kt, n].rearrange("p e (h i) -> p e h i", h=4),
                                          k_view(raw[:, 0, kt, :])[:, n],
                                          f32(wk[0][:, kt, n]).rearrange("p e (h i) -> p e h i", h=4),
                                          ALU.subtract).then_inc(wl_done, 1)
                for kt in range(KT):
                    dve.wait_ge(wh_done, 5 + kt)
                    dve.tensor_tensor(wv[1][:, kt, :], raw[:, 1, kt, :], f32(wv[0][:, kt, :]), ALU.subtract).then_inc(wl_done, 1)
                for b in range(B):
                    for half in range(2):
                        cols = slice(half * CH, (half + 1) * CH)
                        for n in range(2):
                            dve.wait_ge(k_ready, 4 * b + 2 * half + n + 1)
                            if b or half:
                                dve.wait_ge(k_sum, 4 * b + 2 * half + n - 1)
                            for e in range(2):
                                ins = dve.tensor_tensor(tu[:, n, e], ps[:, 2 * n + e, :].unsqueeze(1).broadcast_to([P, 2, CH]),
                                                        rot[:, e, :, cols], ALU.mult)
                            ins.then_inc(k_rot, 1)
                        for n in range(2):
                            dve.wait_ge(vt_hi, 4 * b + 2 * half + n + 1)
                            dve.tensor_tensor(vl[:, n], ps[:, 4 + 2 * n:6 + 2 * n, :], f32(vh[:, n]), ALU.subtract).then_inc(vt_lo, 1)
                            dve.wait_ge(k_hi, 4 * b + 2 * half + n + 1)
                            dve.tensor_tensor(kl[:, n], ab[:, n], f32(kh[:, n]), ALU.subtract).then_inc(k_lo, 1)

    def compress_phase():
        NK = NBLK * B * HKV
        with ExitStack() as c:
            kx = sb("kx", [P, B * HKV, T], F32R, c)
            raw = sb("wc_raw", [P, BS, D], F32, c)
            wc = [sb(f"wc{n}", [P, BS, D], F32R, c) for n in ("h", "l")]
            vct = sb("vct", [D, NK], F32, c)
            vcn = sb("vcn", [P, 2, D], F32, c)
            x_in = [sem(f"kx_in{n}", c) for n in range(2)]
            w_in = sem("wc_in", c)
            wch_done = sem("wch_done", c)
            wcl_done = sem("wcl_done", c)
            c_done = sem("c_done", c)
            kc_hi = sem("kc_hi", c)
            kc_lo = sem("kc_lo", c)
            vct_done = sem("vct_done", c)
            vc_turned = sem("vc_turned", c)
            vcn_done = sem("vcn_done", c)
            vc_stored = sem("vc_stored", c)
            blk = c.enter_context(nc.Block())
            wck = a["L0_attn_W_ck"].rearrange("(s i e) n -> e i s n", s=BS, e=2)
            wcv = a["L0_attn_W_cv"].rearrange("(s d) n -> d s n", s=BS)

            @blk.sync
            def _(sp):
                for r in range(2):
                    for e in range(2):
                        sp.dma_start(raw[r * 64 + e * 32:r * 64 + e * 32 + 32], wck[e]).then_inc(w_in, 16)
                for g in range(HKV):
                    for b in range(B):
                        src = k_scr[g // 4, b, :, :, 32 * (g % 4):32 * (g % 4) + 32, :].rearrange("l e i t -> (l e) i t")
                        sp.dma_start(f32(kx[:, 2 * g + b, :]), src).then_inc(x_in[0], 16)
                sp.wait_ge(wcl_done, 1)
                for r in range(2):
                    sp.dma_start(raw[r * 64:r * 64 + 64], wcv).then_inc(w_in, 16)
                sp.wait_ge(c_done, 1)
                for g in range(HKV):
                    for b in range(B):
                        src = vt_scr[g // 2, b, :, 64 * (g % 2):64 * (g % 2) + 64, :]
                        sp.dma_start(f32(kx[:, 2 * g + b, :]), src).then_inc(x_in[1], 16)
                sp.wait_ge(vcn_done, 1)
                sp.dma_start(vc_scr.rearrange("m p d -> p m d"), vcn[:]).then_inc(vc_stored, 16)
                sp.wait_ge(vc_stored, 16)

            @blk.tensor
            def _(pe):
                for m in range(2):
                    pe.wait_ge(wcl_done, m + 1)
                    pe.wait_ge(x_in[m], 16 * B * HKV)
                    for s in range(BS):
                        xs = kx[:].rearrange("p g (n s) -> p (g n) s", s=BS)[:, :, s]
                        for n in range(2):
                            ins = pe.matmul(ps[0:D, m, 0:NK], wc[n][:, s, :], xs, start=(s == 0 and n == 0),
                                            stop=(s == BS - 1 and n == 1))
                    ins.then_inc(c_done, 1)
                pe.wait_ge(vct_done, 1)
                for n in range(2):
                    ins = pe.transpose(ps[:, 2, n * D:(n + 1) * D], vct[:, n * P:(n + 1) * P], ident[0:D, 0:D])
                ins.then_inc(vc_turned, 1)

            @blk.scalar
            def _(act):
                for m in range(2):
                    act.wait_ge(w_in, 64 + 32 * m)
                    if m == 0:
                        src = raw[:].rearrange("p s (i e) -> p s e i", e=2)
                        for n in range(BS // 16):
                            rows = slice(16 * n, 16 * n + 16)
                            act.activation(wc[0][:, rows].rearrange("p s (e i) -> p s e i", e=2), src[:, rows], ACT.Copy)\
                                .then_inc(wch_done, 1)
                    else:
                        act.wait_ge(c_done, 1)
                        act.activation(wc[0][:], raw[:], ACT.Copy).then_inc(wch_done, 1)
                act.wait_ge(c_done, 2)
                act.activation(vct[:], ps[0:D, 1, 0:NK], ACT.Copy).then_inc(vct_done, 1)
                act.wait_ge(vc_turned, 1)
                act.activation(vcn[:], ps[:, 2, 0:2 * D].rearrange("p (m d) -> p m d", m=2), ACT.Copy).then_inc(vcn_done, 1)

            @blk.vector
            def _(dve):
                dve.wait_ge(wch_done, 4)
                src = raw[:].rearrange("p s (i e) -> p s e i", e=2)
                for n in range(4):
                    rows = slice(16 * n, 16 * n + 16)
                    ins = dve.tensor_tensor(wc[1][:, rows].rearrange("p s (e i) -> p s e i", e=2), src[:, rows],
                                            f32(wc[0][:, rows]).rearrange("p s (e i) -> p s e i", e=2), ALU.subtract)
                ins.then_inc(wcl_done, 1)
                dve.wait_ge(c_done, 1)
                for e in range(2):
                    for h in range(4):
                        dve.tensor_copy(kc_all[32 * h:32 * h + 32, e, 0, :], ps[32 * e:32 * e + 32, 0, 0:NK]).then_inc(kc_hi, 1)
                for e in range(2):
                    for h in range(4):
                        dve.wait_ge(kc_hi, 4 * e + h + 1)
                        dve.tensor_tensor(kc_all[32 * h:32 * h + 32, e, 1, :], ps[32 * e:32 * e + 32, 0, 0:NK],
                                          f32(kc_all[32 * h:32 * h + 32, e, 0, :]), ALU.subtract).then_inc(kc_lo, 1)
                dve.wait_ge(wch_done, 5)
                dve.tensor_tensor(wc[1][:], raw[:], f32(wc[0][:]), ALU.subtract).then_inc(wcl_done, 1)

    def query_phase():
        NJ = HKV * 4
        with ExitStack() as c:
            raw = sb("wq_raw", [P, KT, H * D], F32, c)
            wq = [sb(f"wq{n}", [P, 2, KT, 2, P], F32R, c) for n in ("h", "l")]
            rot = sb("rot_q_sb", [P, 2, 2, T], F32, c)
            tu = sb("q_tu", [P, 2, 2, 2, CH], F32, c)
            ab = sb("q_ab", [P, 2, 2, CH], F32, c)
            qh = sb("qh", [P, 4, 2, CH], F32R, c)
            ql = sb("ql", [P, 4, 2, CH], F32R, c)
            kcb = sb("kcb", [P, B, 2, 2, D], F32R, c)
            lc = sb("lc", [P, 2, CH], F32, c)
            mc = sb("mc", [P, 3, 16], F32, c)
            ec = sb("ec", [P, 16, 16], F32, c)
            prob_c = sb("prob_c", [P, 2, 4, P], F32, c)
            pc = sb("pc", [D, 2, CH], F32, c)
            q_in = sem("q_in", c)
            zeroed = sem("kcb_zeroed", c)
            wqh_done = sem("wqh_done", c)
            wql_done = sem("wql_done", c)
            q_ready = sem("q_ready", c)
            q_rot = sem("q_rot", c)
            q_sum = sem("q_sum", c)
            q_hi = sem("q_hi", c)
            q_lo = sem("q_lo", c)
            q_stored = [sem(f"q_stored{n}", c) for n in range(4)]
            kcb_ready = sem("kcb_ready", c)
            lc_ready = sem("lc_ready", c)
            lc_out = sem("lc_out", c)
            lt_ready = sem("lt_ready", c)
            c_max = sem("c_max", c)
            c_shift = sem("c_shift", c)
            c_exp = sem("c_exp", c)
            c_chain = sem("c_chain", c)
            c_prob = sem("c_prob", c)
            pt_ready = sem("pt_ready", c)
            pc_out = sem("pc_out", c)
            pc_stored = [sem(f"pc_stored{n}", c) for n in range(2)]
            blk = c.enter_context(nc.Block())
            L_SPLIT, L_COMP, L_MAX, L_PROB, L_BACK = 1, 2, 3, 4, 5

            def steps(eng, step):
                for k in range(8):
                    step(0, k, lambda lag, k=k: k >= lag)
                with eng.Fori(1, NJ // 8) as it:
                    for k in range(8):
                        step(it, k, lambda lag: True)
                for k in range(L_BACK):
                    step(NJ // 8, k, lambda lag, k=k: k < lag)

            def place(it, k, lag):
                j, m = 8 * it + k - lag, (k - lag) % 8
                first = isinstance(it, int) and it == 0
                return j, m, 2 * it + (k - lag) // 4, m // 2 % 2, m % 2, (lambda n: not first or k - lag >= n)

            @blk.sync
            def _(sp):
                sp.dma_start(raw[:], a["L0_attn_W_q"].rearrange("(k p) n -> p k n", p=P)).then_inc(q_in, 16)
                sp.dma_start(rot[:], a["rot_q"]).then_inc(q_in, 16)

                def step(it, k, on):
                    if on(L_SPLIT):
                        j, m, g, b, half, _ = place(it, k, L_SPLIT)
                        cols = slice(half * CH, (half + 1) * CH)
                        for part, t, done in ((0, qh, q_hi), (1, ql, q_lo)):
                            sp.wait_ge(done, j + 1)
                            dst = q_scr[bass.ds(g, 1), b, part, :, :, cols].rearrange("g e p t -> p (g e) t")
                            sp.dma_start(dst, f32(t[:, m % 4])).then_inc(q_stored[m % 4], 16)
                    if on(L_BACK):
                        j, m, g, b, half, _ = place(it, k, L_BACK)
                        sp.wait_ge(pc_out, j + 1)
                        dst = pc_scr[bass.ds(g, 1), D * b:D * b + D, half * CH:(half + 1) * CH].rearrange("g p t -> (g p) t")
                        sp.dma_start(dst, pc[:, m % 2]).then_inc(pc_stored[m % 2], 16)
                steps(sp, step)
                for n in range(4):
                    sp.wait_ge(q_stored[n], 2 * 16 * (NJ // 4))
                for n in range(2):
                    sp.wait_ge(pc_stored[n], 16 * (NJ // 2))

            @blk.tensor
            def _(pe):
                def step(it, k, on):
                    if on(0):
                        j, m, g, b, half, past = place(it, k, 0)
                        if k % 4 == 0:
                            pe.wait_ge(wql_done, g + 1)
                        if past(2):
                            pe.wait_ge(q_rot, j - 1)
                        cols = slice(b * T + half * CH, b * T + (half + 1) * CH)
                        for e in range(2):
                            n = 0
                            for kt in range(KT):
                                for w, x in three(kt, wq[0][:, k // 4, kt, e, :], wq[1][:, k // 4, kt, e, :],
                                                  xh[:, kt, cols], xl[:, kt, cols]):
                                    ins = pe.matmul(ps[:, 2 * (k % 2) + e, :], w, x, start=(n == 0), stop=(n == 5))
                                    n += 1
                        ins.then_inc(q_ready, 1)
                    if on(L_COMP):
                        j, m, g, b, half, past = place(it, k, L_COMP)
                        pe.wait_ge(q_lo, j + 1)
                        pe.wait_ge(kcb_ready, 4 * (4 * it + (k - L_COMP) // 2 + 1))
                        if past(2):
                            pe.wait_ge(lc_out, j - 1)
                        n = 0
                        for e in range(2):
                            for w, x in ((0, qh), (1, qh), (0, ql)):
                                ins = pe.matmul(ps[0:D, 4 + m % 2, :], kcb[:, b, e, w, :], x[:, m % 4, e, :],
                                                start=(n == 0), stop=(n == 5))
                                n += 1
                        ins.then_inc(lc_ready, 1)
                    if on(L_MAX):
                        j, m, g, b, half, past = place(it, k, L_MAX)
                        if not past(1):
                            pe.wait_ge(zeroed, 3)
                        pe.wait_ge(lc_out, j + 1)
                        if past(1):
                            pe.wait_ge(c_shift, j)
                        for t in range(4):
                            ins = pe.transpose(ps[:, 6, t * P:(t + 1) * P], lc[:, m % 2, t * P:(t + 1) * P], ident[:])
                        ins.then_inc(lt_ready, 1)
                    if on(L_BACK):
                        j, m, g, b, half, past = place(it, k, L_BACK)
                        pe.wait_ge(c_prob, j + 1)
                        if past(1):
                            pe.wait_ge(pc_out, j)
                        for t in range(4):
                            ins = pe.transpose(ps[:, 7, t * P:(t + 1) * P], prob_c[:, m % 2, t, :], ident[:])
                        ins.then_inc(pt_ready, 1)
                steps(pe, step)

            @blk.gpsimd
            def _(pool):
                pool.memset(f32(kcb[:]), 0.0).then_inc(zeroed, 1)
                pool.memset(prob_c[:, :, :, D:P], 0.0).then_inc(zeroed, 1)
                pool.wait_ge(zeroed, 2)
                pool.memset(lc[D:P], 0.0).then_inc(zeroed, 1)
                pool.wait_ge(zeroed, 3)

                def step(it, k, on):
                    if not on(0):
                        return
                    j, m, g, b, half, past = place(it, k, 0)
                    if half == 0:
                        if past(4):
                            pool.wait_ge(lc_ready, j - 2)
                        for h in range(4):
                            src = kc_all[32 * h:32 * h + 32, :, :, bass.ds((2 * g + b) * NBLK, NBLK)]
                            pool.tensor_copy(kcb[32 * h:32 * h + 32, b, :, :, NBLK * h:NBLK * h + NBLK], f32(src))\
                                .then_inc(kcb_ready, 1)
                            pool.wait_ge(kcb_ready, 4 * (2 * g + b) + h + 1)
                    pool.wait_ge(q_rot, j + 1)
                    if past(2):
                        pool.wait_ge(q_lo, j - 1)
                    pool.tensor_tensor(ab[:, k % 2], tu[:, k % 2, 0], tu[:, k % 2, 1], ALU.add).then_inc(q_sum, 1)
                steps(pool, step)

            def w_view(g, kt):
                return raw[:, kt, bass.ds(g * REP * D, REP * D)].rearrange("p (h i e) -> p e h i", h=REP, e=2)

            def buffer_free(eng, j, m, n4, past):
                if past(4):
                    eng.wait_ge(q_stored[m % 4], 32 * n4)
                    eng.wait_ge(lc_ready, j - 3)

            @blk.scalar
            def _(act):
                act.wait_ge(q_in, 32)

                def step(it, k, on):
                    if on(0) and k % 4 == 0:
                        j, m, g, b, half, past = place(it, k, 0)
                        if past(8):
                            act.wait_ge(q_ready, j - 4)
                        for kt in range(KT):
                            ins = act.activation(wq[0][:, k // 4, kt].rearrange("p e (h i) -> p e h i", h=REP), w_view(g, kt), ACT.Copy)
                        ins.then_inc(wqh_done, 1)
                    if on(L_COMP):
                        j, m, g, b, half, past = place(it, k, L_COMP)
                        act.wait_ge(lc_ready, j + 1)
                        if past(2):
                            act.wait_ge(lt_ready, j - 1)
                        act.activation(lc[0:D, m % 2], ps[0:D, 4 + m % 2, :], ACT.Copy).then_inc(lc_out, 1)
                    if on(L_SPLIT):
                        j, m, g, b, half, past = place(it, k, L_SPLIT)
                        act.wait_ge(q_sum, j + 1)
                        buffer_free(act, j, m, 2 * it + (k - L_SPLIT) // 4, past)
                        act.activation(qh[:, m % 4], ab[:, m % 2], ACT.Copy).then_inc(q_hi, 1)
                    if on(L_MAX):
                        j, m, g, b, half, past = place(it, k, L_MAX)
                        act.wait_ge(c_shift, j + 1)
                        act.activation(ec[:], ec[:], ACT.Exp).then_inc(c_exp, 1)
                    if on(L_BACK):
                        j, m, g, b, half, past = place(it, k, L_BACK)
                        act.wait_ge(pt_ready, j + 1)
                        if past(2):
                            act.wait_ge(pc_stored[m % 2], 16 * (4 * it + (k - L_BACK) // 2))
                        act.activation(pc[:, m % 2], ps[0:D, 7, :], ACT.Copy).then_inc(pc_out, 1)
                steps(act, step)

            @blk.vector
            def _(dve):
                ch = Chain(dve, c_chain)

                def step(it, k, on):
                    if on(0) and k % 4 == 0:
                        j, m, g, b, half, past = place(it, k, 0)
                        dve.wait_ge(wqh_done, g + 1)
                        for kt in range(KT):
                            ins = dve.tensor_tensor(wq[1][:, k // 4, kt].rearrange("p e (h i) -> p e h i", h=REP), w_view(g, kt),
                                                    f32(wq[0][:, k // 4, kt]).rearrange("p e (h i) -> p e h i", h=REP), ALU.subtract)
                        ins.then_inc(wql_done, 1)
                    if on(L_PROB):
                        j, m, g, b, half, past = place(it, k, L_PROB)
                        dve.wait_ge(c_exp, j + 1)
                        ch.n, ch.base = 0, 3 * j
                        ch.link(dve.tensor_reduce(mc[:, 1, :], ec[:], X, ALU.add))
                        ch.link(dve.reciprocal(mc[:, 2, :], mc[:, 1, :]))
                        gc = gate_c[:, TJ * b + 4 * half:TJ * b + 4 * half + 4].unsqueeze(2).broadcast_to([P, 4, REP])
                        ch.link(dve.tensor_tensor(mc[:, 1, :].rearrange("p (t h) -> p t h", t=4),
                                                  mc[:, 2, :].rearrange("p (t h) -> p t h", t=4), gc, ALU.mult))
                        if past(2):
                            dve.wait_ge(pt_ready, j - 1)
                        dve.tensor_tensor(prob_c[:, m % 2, :, 0:D].rearrange("p t (h n) -> p t h n", h=REP),
                                          ec[:].rearrange("p (t h) n -> p t h n", t=4),
                                          mc[:, 1, :].rearrange("p (t h) -> p t h", t=4).unsqueeze(3).broadcast_to([P, 4, REP, NBLK]),
                                          ALU.mult).then_inc(c_prob, 1)
                    if on(0):
                        j, m, g, b, half, past = place(it, k, 0)
                        dve.wait_ge(q_ready, j + 1)
                        if past(2):
                            dve.wait_ge(q_sum, j - 1)
                        for e in range(2):
                            ins = dve.tensor_tensor(tu[:, k % 2, e], ps[:, 2 * (k % 2) + e, :].unsqueeze(1).broadcast_to([P, 2, CH]),
                                                    rot[:, e, :, half * CH:(half + 1) * CH], ALU.mult)
                        ins.then_inc(q_rot, 1)
                    if on(L_MAX):
                        j, m, g, b, half, past = place(it, k, L_MAX)
                        dve.wait_ge(lt_ready, j + 1)
                        lt = ps[:, 6, :].rearrange("p (t r h n) -> p t r h n", t=4, r=2, h=REP)[:, :, 0]
                        nm = mc[:, 0, :].rearrange("p (t h) -> p t h", t=4)
                        dve.tensor_reduce(nm, lt, X, ALU.max, negate=True).then_inc(c_max, 1)
                        dve.wait_ge(c_max, j + 1)
                        if past(1):
                            dve.wait_ge(c_prob, j)
                        dve.tensor_tensor(ec[:].rearrange("p (t h) n -> p t h n", t=4), lt,
                                          nm.unsqueeze(3).broadcast_to([P, 4, REP, NBLK]), ALU.add).then_inc(c_shift, 1)
                    if on(L_SPLIT):
                        j, m, g, b, half, past = place(it, k, L_SPLIT)
                        dve.wait_ge(q_hi, j + 1)
                        buffer_free(dve, j, m, 2 * it + (k - L_SPLIT) // 4, past)
                        dve.tensor_tensor(ql[:, m % 4], ab[:, m % 2], f32(qh[:, m % 4]), ALU.subtract).then_inc(q_lo, 1)
                steps(dve, step)

    def attention_phase():
        NP = 4 * HKV
        NQ = TJ
        with ExitStack() as c:
            qa = sb("qa", [P, 4, 2, T], F32R, c)
            qb = sb("qb", [P, 2, 2, 2, T], F32R, c)
            k_hh = sb("k_hh", [P, B, T], F32R, c)
            k_ll = sb("k_ll", [P, B, T], F32R, c)
            k_l1 = sb("k_l1", [P, B, T], F32R, c)
            v_s = sb("v_s", [P, B, TJ, D], F32, c)
            pct = sb("pct", [P, T], F32, c)
            vcp = sb("vcp", [P, 4, P], F32, c)
            prob = sb("prob", [P, 2, 2, T], F32, c)
            prob_w = sb("prob_w", [P, 2, 2, WW], F32, c)
            wl = sb("wl", [P, 2, TJ, WW], F32, c)
            junk = sb("junk", [P, T], BF16, c)
            nmax = sb("nmax", [P, 2, 2 * TJ], F32, c)
            sums = sb("sums", [P, 2, 2 * TJ], F32, c)
            lns = sb("lns", [P, 2, 2 * TJ], F32, c)
            shift = sb("shift", [P, 2, 2, 2 * TJ], F32, c)
            shift_r = sb("shift_r", [P, P // (4 * TJ), 2, 2 * TJ], F32R, c)
            o_t = sb("o_t", [P, 2, T], F32, c)
            mask_a = sb("mask_a_sb", [P, WW], F32, c)
            mask_b = sb("mask_b_sb", [P, WW], F32, c)
            mask_bh = sb("mask_bh", [P, WW], BF16, c)
            ident_h = sb("ident_h", [P, P], BF16, c)
            pick = sb("pick_sb", [D, 4, TJ], F32, c)
            const_in = sem("m_const_in", c)
            const_ok = sem("m_const_ok", c)
            ones_ok = sem("ones_ok", c)
            qa_in = [sem(f"qa_in{n}", c) for n in range(4)]
            qb_in = [sem(f"qb_in{n}", c) for n in range(2)]
            k_in = [sem(f"k_in{n}", c) for n in range(2)]
            pc_in = sem("pc_in", c)
            v_ok = sem("v_ok", c)
            a_ready = sem("a_ready", c)
            b_ready = sem("b_ready", c)
            w_ready = sem("w_ready5", c)
            t_ready = sem("t_ready", c)
            pv_done = sem("pv_done", c)
            a_exp = sem("a_exp", c)
            b_exp = sem("b_exp", c)
            wb_exp = sem("wb_exp", c)
            w_exp = sem("w_exp", c)
            ln_done = sem("ln_done", c)
            o_out = sem("o_out", c)
            a_max = sem("a_max", c)
            a_win = sem("a_win", c)
            w_max = sem("w_max", c)
            w_shift = sem("w_shift", c)
            w_sum = sem("w_sum", c)
            m_chain = sem("m_chain", c)
            st_ready = sem("st_ready", c)
            aug_done = sem("aug_done", c)
            o_stored = [sem(f"o_stored{n}", c) for n in range(2)]
            blk = c.enter_context(nc.Block())
            OB = 6

            def stages(stage):
                def run(eng):
                    stage(-1, 3, False, True)
                    for u in range(4):
                        stage(0, u, True, True)
                    with eng.Fori(1, HKV - 1) as it:
                        for u in range(4):
                            stage(it, u, True, True)
                    for u in range(4):
                        stage(HKV - 1, u, True, u < 3)
                return run

            def early(it, u, n):
                return isinstance(it, int) and 4 * it + u < n

            def after(it, u, n=1):
                return it + (u + n) // 4, (u + n) % 4

            def pe_order(cc, b_on, a_on):
                seq = []
                if a_on and b_on:
                    seq = ["A", "B0", "A", "V", "B1", "A", "W", "A"] if cc < 4 else ["B0", "B1", "V", "W"]
                elif b_on:
                    seq = ["B0", "B1", "V", "W"]
                elif cc < 4:
                    seq = ["A"] * 4
                if a_on and cc == 6:
                    seq = seq + ["T"]
                return seq

            @blk.sync
            def _(sp):
                sp.dma_start(mask_a[:], a["mask_a"]).then_inc(const_in, 16)
                sp.dma_start(mask_b[:], a["mask_b"]).then_inc(const_in, 16)
                sp.dma_start(pick[:], a["pick"]).then_inc(const_in, 16)

                def load_k(g, b):
                    def rows(part):
                        src = k_scr[bass.ds(g // 4, 1), b, part, :, bass.ds(32 * (g % 4), 32), :]
                        return src.rearrange("g e i t -> (g e) i t")
                    for dst, part in ((k_hh[0:D, b], 0), (k_hh[D:P, b], 0), (k_ll[0:D, b], 1), (k_ll[D:P, b], 1), (k_l1[0:D, b], 1)):
                        sp.dma_start(f32(dst), rows(part)).then_inc(k_in[b], 16)

                def load_qa(it, u):
                    for h in range(2):
                        r = 32 * (2 * (u % 2) + h)
                        src = q_scr[bass.ds(it, 1), u // 2, :, :, r:r + 32, :].rearrange("g l e i t -> (g l e) i t")
                        sp.dma_start(f32(qa[:, u, h]), src).then_inc(qa_in[u], 16)

                def load_qb(it, u):
                    for br in range(2):
                        for h in range(2):
                            r = 32 * (2 * (u % 2) + h)
                            src = q_scr[bass.ds(it, 1), u // 2, 0, :, r:r + 32, :].rearrange("g e i t -> (g e) i t")
                            sp.dma_start(f32(qb[0:D, u % 2, br, h]), src).then_inc(qb_in[u % 2], 16)

                def load_pc(it):
                    sp.dma_start(pct[:], pc_scr[bass.ds(it, 1)].rearrange("g p t -> (g p) t")).then_inc(pc_in, 16)
                    vc = vc_scr.rearrange("m p d -> (m p) d")
                    for b in range(B):
                        for h in range(REP):
                            r = D * b + NBLK * h
                            sp.dma_start(vcp[r:r + NBLK, 2 * b + h // 2, D * (h % 2):D * (h % 2) + D],
                                         vc[bass.ds((2 * it + b) * NBLK, NBLK), :]).then_inc(pc_in, 16)

                def stage(it, u, b_on, a_on):
                    if not b_on:
                        load_k(0, 0)
                        load_qa(0, 0)
                        load_qb(0, 0)
                        load_qa(0, 1)
                        load_k(0, 1)
                        sp.wait_ge(ones_ok, 3)
                        load_pc(0)
                        load_qb(0, 1)
                        return
                    pr = 4 * it + u
                    last = isinstance(it, int) and it == HKV - 1
                    if u == 0 and not early(it, u, 1):
                        sp.wait_ge(w_ready, 8 * pr)
                        load_k(it, 1)
                    if u == 2 and not last:
                        sp.wait_ge(w_ready, 8 * pr)
                        load_k(it + 1, 0)
                    if not (last and u >= 2):
                        if not early(it, u, 2):
                            sp.wait_ge(w_ready, 8 * (pr - 1))
                        load_qa(*after(it, u, 2))
                    if not early(it, u, 1):
                        store_o(*after(it, u, -1))
                    if u == 3 and not last:
                        sp.wait_ge(pv_done, 8 * pr + 1)
                        load_pc(it + 1)
                    if not (last and u >= 2):
                        sp.wait_ge(w_ready, 8 * (pr + 1))
                        load_qb(*after(it, u, 2))

                def store_o(it, u):
                    sp.wait_ge(o_out, 4 * it + u + 1)
                    b, row = u // 2, (u % 2) * P
                    sp.dma_start(o_scr[b, bass.ds(it * (REP * D) + row, P), :], o_t[:, u % 2]).then_inc(o_stored[u % 2], 16)

                stages(stage)(sp)
                store_o(HKV - 1, 3)
                for n in range(2):
                    sp.wait_ge(o_stored[n], 16 * NP // 2)

            @blk.tensor
            def _(pe):
                pe.wait_ge(ones_ok, 3)
                pe.wait_ge(const_ok, 1)
                ring = {"n": 0, "used": [None] * 3}

                def slot(used):
                    n = ring["n"] % 3
                    if ring["used"][n] is not None:
                        s_, f_ = ring["used"][n]
                        pe.wait_ge(s_, f_)
                    ring["used"][n] = used
                    ring["n"] += 1
                    return 2 * n

                def stage(it, u, b_on, a_on):
                    pr = 4 * it + u
                    ita, ua = after(it, u)
                    x = 4 * ita + ua
                    b, ba = u // 2, ua // 2
                    na = 0

                    def job_a(n):
                        h, j = n // TJ, n % TJ
                        if n == 0:
                            pe.wait_ge(qa_in[ua], 32 * (ita + 1))
                            pe.wait_ge(k_in[ba], 80 * (ita + 1))
                        s0 = slot((a_exp, 16 * x + n + 1))
                        lhs = qa[:, ua, h, j * P:(j + 1) * P]
                        for half in range(2):
                            cols = slice(half * CH, (half + 1) * CH)
                            pe.matmul(ps[:, s0 + half, :], lhs, k_hh[:, ba, cols], start=True, stop=False)
                            ins = pe.matmul(ps[:, s0 + half, :], lhs, k_ll[:, ba, cols], start=False, stop=True)
                        ins.then_inc(a_ready, 1)

                    def job_b(cc, h):
                        if cc == 0:
                            if h == 0:
                                pe.wait_ge(qb_in[u % 2], 64 * (2 * it + u // 2 + 1))
                            pe.wait_ge(aug_done, 4 * pr + h + 1)
                        s0 = slot((b_exp, 16 * pr + 2 * cc + h + 1))
                        ks = slice(cc * P, (cc + 1) * P)
                        for half in range(2):
                            cols = slice(half * CH, (half + 1) * CH)
                            pe.matmul(ps[:, s0 + half, :], k_hh[:, b, ks], qa[:, u, h, cols], start=True, stop=False)
                            ins = pe.matmul(ps[:, s0 + half, :], k_l1[:, b, ks], qb[:, u % 2, 0, h, cols], start=False, stop=True)
                        ins.then_inc(b_ready, 1)

                    def job_w(cc):
                        if cc == 0:
                            pe.wait_ge(aug_done, 4 * pr + 4)
                        n = min(WW, T - cc * P)
                        s0 = slot((wb_exp, 8 * pr + cc + 1))
                        ks, ts = slice(cc * P, (cc + 1) * P), slice(cc * P, cc * P + n)
                        dst = ps[:, s0, 0:2 * n].rearrange("p (h n) -> p h n", h=2)
                        pe.matmul(dst, k_hh[:, b, ks], qa[:, u, :, ts], start=True, stop=False)
                        pe.matmul(dst, k_l1[:, b, ks], qb[:, u % 2, 1, :, ts], start=False, stop=False)
                        pe.matmul(dst, ident_h[:], mask_bh[:, 0:n].unsqueeze(1).broadcast_to([P, 2, n]), start=False, stop=True)\
                            .then_inc(w_ready, 1)

                    def job_t():
                        s0 = slot((aug_done, 4 * x + 4))
                        ring["n"] += 1
                        pe.wait_ge(st_ready, x + 1)
                        pe.transpose(ps[:, s0, 0:P], f32(shift_r[:]).rearrange("p l r n -> p (l r n)"), ident[:]).then_inc(t_ready, 1)

                    def job_v(cc):
                        if cc == 0:
                            pe.wait_ge(pc_in, 144 * (it + 1))
                            pe.wait_ge(v_ok, 2 * it + b + 1)
                            if not early(it, u, 1):
                                pe.wait_ge(o_out, pr)
                            for half in range(2):
                                pe.matmul(ps[:, OB + half, :], vcp[:, u, :], pct[:, half * CH:(half + 1) * CH],
                                          start=True, stop=False, skip_group_check=True)
                        lastc = cc == TJ - 1
                        v = v_s[:, b, cc, :]
                        pe.wait_ge(b_exp, 16 * pr + 2 * cc + 2)
                        for half in range(2):
                            for h in range(2):
                                pe.matmul(ps[D * h:D * h + D, OB + half, :], v, prob[:, cc % 2, h, half * CH:(half + 1) * CH],
                                          start=False, stop=lastc and half == 0, skip_group_check=True)
                        pe.wait_ge(wb_exp, 8 * pr + cc + 1)
                        n = min(WW, T - cc * P)
                        for t0, t1 in ([(0, P), (P, WW)] if cc == 3 else [(0, n)]):
                            t = cc * P + t0
                            for h in range(2):
                                ins = pe.matmul(ps[D * h:D * h + D, OB + t // CH, t % CH:t % CH + t1 - t0], v,
                                                prob_w[:, cc % 2, h, t0:t1], start=False, stop=lastc, skip_group_check=True)
                        ins.then_inc(pv_done, 1)

                    for cc in range(TJ):
                        for what in pe_order(cc, b_on, a_on):
                            if what == "A":
                                job_a(na)
                                na += 1
                            elif what[0] == "B":
                                job_b(cc, int(what[1]))
                            elif what == "W":
                                job_w(cc)
                            elif what == "T":
                                job_t()
                            elif cc > 0:
                                job_v(cc - 1)
                    if b_on:
                        job_v(TJ - 1)

                stage(-1, 3, False, True)
                ring["n"] += -ring["n"] % 3
                for u in range(4):
                    stage(0, u, True, True)
                assert (ring["n"]) % 3 == 0
                with pe.Fori(1, HKV - 1) as it:
                    def moved(entry, by):
                        return (entry[0], entry[1] + (it - 1) * by[entry[0].name])
                    per = {a_exp.name: 64, b_exp.name: 64, wb_exp.name: 32, aug_done.name: 16}
                    ring["used"] = [moved(e, per) for e in ring["used"]]
                    for u in range(4):
                        stage(it, u, True, True)
                ring["used"] = [(s_, {a_exp.name: 16 * 4 * (HKV - 1) + 16, b_exp.name: 64 * (HKV - 1), wb_exp.name: 32 * (HKV - 1),
                                      aug_done.name: 16 * (HKV - 1) + 4}[s_.name]) for s_, _ in ring["used"]]
                for u in range(4):
                    stage(HKV - 1, u, True, u < 3)

            def act_order(cc, b_on, a_on):
                if a_on and b_on:
                    seq = ["B0", "A", "A", "B1", "A", "W", "A"] if cc < 4 else ["B0", "B1", "W"]
                elif b_on:
                    seq = ["B0", "B1", "W"]
                else:
                    seq = ["A"] * 4 if cc < 4 else []
                if a_on:
                    seq = seq + {2: ["X0"], 4: ["X1"], 5: ["L"]}.get(cc, [])
                return seq

            def slots_of(b_on, a_on, n0):
                out, n = {}, n0
                na = 0
                for cc in range(TJ):
                    for what in pe_order(cc, b_on, a_on):
                        if what == "V":
                            continue
                        key = ("A", na) if what == "A" else (what, cc)
                        na += what == "A"
                        out[key] = 2 * (n % 3)
                        n += 1 + (what == "T")
                return out, n

            slot_maps = [slots_of(False, True, 0)[0]]
            n_ = 0
            for u_ in range(4):
                m_, n_ = slots_of(True, True, n_)
                slot_maps.append(m_)
            last3 = slots_of(True, False, slots_of(True, True, slots_of(True, True, slots_of(True, True, 0)[1])[1])[1])[0]

            def slot_map(u, b_on, a_on):
                return slot_maps[0] if not b_on else slot_maps[1 + u] if a_on else last3

            @blk.scalar
            def _(act):
                act.wait_ge(const_in, 48)
                act.activation(mask_bh[:], mask_b[:], ACT.Copy)
                act.activation(ident_h[:], ident[:], ACT.Copy).then_inc(const_ok, 1)

                def stage(it, u, b_on, a_on):
                    pr = 4 * it + u
                    ita, ua = after(it, u)
                    x = 4 * ita + ua
                    first_a = isinstance(it, int) and x == 0
                    where = slot_map(u, b_on, a_on)
                    na = 0
                    if b_on and not early(it, u, 1):
                        out_o(*after(it, u, -1))
                    for cc in range(TJ):
                        for what in act_order(cc, b_on, a_on):
                            if what == "A":
                                n = na
                                na += 1
                                s0 = where[("A", n)]
                                act.wait_ge(a_win, 16 * x + n + 1)
                                if n == 0 and not first_a:
                                    act.wait_ge(ln_done, x)
                                src = ps[:, s0:s0 + 2, :].rearrange("p a n -> p (a n)")
                                if n or not first_a:
                                    act.wait_ge(a_exp, 16 * x + n)
                                act.activation(junk[:], src, ACT.Exp, bias=nmax[:, 0, n:n + 1],
                                               accum_out=sums[:, 0, n:n + 1]).then_inc(a_exp, 1)
                            elif what[0] == "B":
                                h = int(what[1])
                                s0 = where[(what, cc)]
                                act.wait_ge(b_ready, 16 * pr + 2 * cc + h + 1)
                                if not early(it, u, 1) or cc >= 2:
                                    act.wait_ge(pv_done, 8 * pr + cc - 1)
                                act.activation(prob[:, cc % 2, h], ps[:, s0:s0 + 2, :].rearrange("p a n -> p (a n)"), ACT.Exp)\
                                    .then_inc(b_exp, 1)
                            elif what == "W":
                                s0 = where[("W", cc)]
                                n = min(WW, T - cc * P)
                                act.wait_ge(w_ready, 8 * pr + cc + 1)
                                act.activation(prob_w[:, cc % 2, :, 0:n], ps[:, s0, 0:2 * n].rearrange("p (h n) -> p h n", h=2), ACT.Exp)\
                                    .then_inc(wb_exp, 1)
                            elif what[0] == "X":
                                h = int(what[1])
                                act.wait_ge(w_shift, 2 * x + h + 1)
                                act.activation(wl[:, h], wl[:, h], ACT.Exp).then_inc(w_exp, 1)
                            else:
                                act.wait_ge(w_sum, 2 * x + 2)
                                act.wait_ge(a_exp, 16 * x + 16)
                                if not first_a:
                                    act.wait_ge(st_ready, x)
                                act.activation(lns[:], sums[:], ACT.Ln).then_inc(ln_done, 1)

                def out_o(it, u):
                    pr = 4 * it + u
                    act.wait_ge(pv_done, 8 * pr + 8)
                    if not early(it, u, 2):
                        act.wait_ge(o_stored[u % 2], 16 * (2 * it + u // 2))
                    act.activation(o_t[:, u % 2].rearrange("p (a n) -> p a n", a=2), ps[:, OB:OB + 2, :], ACT.Copy).then_inc(o_out, 1)

                stages(stage)(act)
                out_o(HKV - 1, 3)

            @blk.gpsimd
            def _(pool):
                pool.memset(f32(k_l1[D:P]), 1.0).then_inc(ones_ok, 1)
                pool.wait_ge(ones_ok, 1)
                pool.memset(f32(shift_r[:, 2:]), 0.0).then_inc(ones_ok, 1)
                pool.memset(vcp[:], 0.0).then_inc(ones_ok, 1)

                def copy_v(g, b):
                    pool.tensor_copy(v_s[:, b], v_all[:, TJ * b:TJ * b + TJ, bass.ds(g * D, D)]).then_inc(v_ok, 1)

                def stage(it, u, b_on, a_on):
                    ita, ua = after(it, u)
                    x = 4 * ita + ua
                    if a_on:
                        for h in range(2):
                            pool.wait_ge(w_max, 2 * x + h + 1)
                            nm = nmax[:, 1, TJ * h:TJ * h + TJ].unsqueeze(2).broadcast_to([P, TJ, WW])
                            pool.tensor_tensor(wl[:, h], wl[:, h], nm, ALU.add).then_inc(w_shift, 1)
                    if not b_on:
                        copy_v(0, 0)
                        copy_v(0, 1)
                    elif u == 0 and not early(it, u, 1):
                        pool.wait_ge(pv_done, 8 * (4 * it))
                        copy_v(it, 1)
                    elif u == 2 and not (isinstance(it, int) and it == HKV - 1):
                        pool.wait_ge(pv_done, 8 * (4 * it + 2))
                        copy_v(it + 1, 0)
                stages(stage)(pool)

            @blk.vector
            def _(dve):
                ch = Chain(dve, m_chain)
                dve.wait_ge(const_in, 48)

                def stage(it, u, b_on, a_on):
                    if not a_on:
                        return
                    ita, ua = after(it, u)
                    x = 4 * ita + ua
                    first_a = isinstance(it, int) and x == 0
                    ba = ua // 2
                    where = slot_map(u, b_on, a_on)

                    def job_a(n):
                        h, j = n // TJ, n % TJ
                        s0 = where[("A", n)]
                        if j == 0:
                            if not first_a:
                                dve.wait_ge(w_sum, 2 * (x - 1) + h + 1)
                                dve.wait_ge(st_ready, x)
                            dve.memset(wl[:, h, 0, 0:WIN], NEG)
                        dve.wait_ge(a_ready, 16 * x + n + 1)
                        src = ps[:, s0:s0 + 2, :].rearrange("p a n -> p (a n)")
                        dve.tensor_reduce(nmax[:, 0, n:n + 1], src, X, ALU.max, negate=True).then_inc(a_max, 1)
                        lo = WIN if j == 0 else 0
                        dve.tensor_tensor(wl[:, h, j, lo:WW], src[:, P * j - WIN + lo:P * j + P], mask_a[:, lo:WW], ALU.add)\
                            .then_inc(a_win, 1)

                    def win_max(h):
                        dve.wait_ge(a_win, 16 * x + TJ * h + TJ)
                        dve.tensor_reduce(nmax[:, 1, TJ * h:TJ * h + TJ], wl[:, h], X, ALU.max, negate=True).then_inc(w_max, 1)

                    def win_sum(h):
                        dve.wait_ge(w_exp, 2 * x + h + 1)
                        dve.tensor_reduce(sums[:, 1, TJ * h:TJ * h + TJ], wl[:, h], X, ALU.add).then_inc(w_sum, 1)

                    for n in range(TJ):
                        job_a(n)
                    win_max(0)
                    for n in range(TJ, 2 * TJ):
                        job_a(n)
                        if n == TJ + 5:
                            win_sum(0)
                    win_max(1)
                    win_sum(1)
                    dve.wait_ge(ln_done, x + 1)
                    ch.n, ch.base = 0, 3 * x
                    ch.link(dve.tensor_tensor(shift[:, 0], nmax[:], lns[:], ALU.subtract))
                    lg = ln_gate[:, :, TJ * ba:TJ * ba + TJ].unsqueeze(2).broadcast_to([P, 2, 2, TJ])
                    ch.link(dve.tensor_tensor(shift[:, 1].rearrange("p r (h j) -> p r h j", h=2),
                                              shift[:, 0].rearrange("p r (h j) -> p r h j", h=2), lg, ALU.add))
                    ch.link(dve.tensor_copy(shift_r[:, 0], shift[:, 1]))
                    dve.tensor_tensor(shift_r[:, 1], shift[:, 1], f32(shift_r[:, 0]), ALU.subtract).then_inc(st_ready, 1)
                    dve.wait_ge(t_ready, x + 1)
                    s0 = where[("T", 6)]
                    if not early(ita, ua, 2):
                        dve.wait_ge(w_ready, 8 * (x - 1))
                    for br in range(2):
                        for h in range(2):
                            dst = qb[D:P, ua % 2, br, h].rearrange("p (j n) -> p j n", j=TJ)
                            dve.tensor_tensor(dst, ps[0:D, s0, 0:P].unsqueeze(1).broadcast_to([D, TJ, P]),
                                              pick[:, 2 * br + h, :].unsqueeze(2).broadcast_to([D, TJ, P]), ALU.mult)\
                                .then_inc(aug_done, 1)
                stages(stage)(dve)

    def out_phase():
        NH = H * D // P
        with ExitStack() as c:
            raw = sb("wo_raw", [P, NH, DM], F32, c)
            wh = sb("woh", [P, NH, DM], F32R, c)
            wl_ = sb("wol", [P, NH, DM], F32R, c)
            o = sb("o", [P, 4, CH], F32, c)
            oh = sb("oh", [P, 4, CH], F32R, c)
            ol = sb("ol", [P, 4, CH], F32R, c)
            xr = sb("xr", [P, 2, 4, DM], F32, c)
            y = sb("y", [P, 2, CH], F32, c)
            yo = sb("yo", [P, 2, 4, DM], F32, c)
            w_in = sem("wo_in", c)
            o_in = [sem(f"o_in{n}", c) for n in range(4)]
            xr_in = [sem(f"xr_in{n}", c) for n in range(2)]
            woh_done = sem("woh_done", c)
            wol_done = sem("wol_done", c)
            oh_done = sem("oh_done", c)
            ol_done = sem("ol_done", c)
            s_part = sem("s_part", c)
            y_done = sem("y_done", c)
            y_turned = sem("y_turned", c)
            yo_done = sem("yo_done", c)
            stored = [sem(f"stored{n}", c) for n in range(2)]
            blk = c.enter_context(nc.Block())
            out_tok = out.rearrange("b (n p) d -> p (b n) d", p=P)

            @blk.sync
            def _(sp):
                sp.dma_start(raw[:], a["L0_attn_W_o"].rearrange("(k p) n -> p k n", p=P)).then_inc(w_in, 16)
                for tc in range(NC):
                    for n in range(NH):
                        k = tc * NH + n
                        if k >= 4:
                            sp.wait_ge(ol_done, k - 3)
                        sp.dma_start(o[:, n % 4], o_scr[tc // 2, n * P:(n + 1) * P, (tc % 2) * CH:(tc % 2) * CH + CH]).then_inc(o_in[n % 4], 16)
                        if n == 0:
                            if tc >= 2:
                                sp.wait_ge(yo_done, tc - 1)
                            sp.dma_start(xr[:, tc % 2], x_tok[:, 4 * tc:4 * tc + 4, :]).then_inc(xr_in[tc % 2], 16)
                        if n == 13 and tc:
                            sp.wait_ge(yo_done, tc)
                            sp.dma_start(out_tok[:, 4 * tc - 4:4 * tc, :], yo[:, (tc - 1) % 2]).then_inc(stored[(tc - 1) % 2], 16)
                sp.wait_ge(yo_done, NC)
                sp.dma_start(out_tok[:, 4 * NC - 4:4 * NC, :], yo[:, (NC - 1) % 2]).then_inc(stored[(NC - 1) % 2], 16)
                for n in range(2):
                    sp.wait_ge(stored[n], 16 * NC // 2)

            @blk.tensor
            def _(pe):
                pe.wait_ge(wol_done, 1)

                def turn(tc):
                    pe.wait_ge(y_done, tc + 1)
                    for t in range(4):
                        for ht in range(2):
                            ins = pe.transpose(ps[:, 4 + t // 2, (2 * (t % 2) + ht) * P:(2 * (t % 2) + ht + 1) * P],
                                               y[:, ht, t * P:(t + 1) * P], ident[:])
                    ins.then_inc(y_turned, 1)
                for tc in range(NC):
                    if tc >= 2:
                        pe.wait_ge(y_done, tc - 1)
                    for n in range(NH):
                        pe.wait_ge(ol_done, tc * NH + n + 1)
                        for ht in range(2):
                            hs = slice(ht * P, (ht + 1) * P)
                            prods = three(0, wh[:, n, hs], wl_[:, n, hs], oh[:, n % 4], ol[:, n % 4])
                            for k, (w, x) in enumerate(prods):
                                ins = pe.matmul(ps[:, 2 * (tc % 2) + ht, :], w, x, start=(n == 0 and k == 0),
                                                stop=(n == NH - 1 and k == 2))
                        ins.then_inc(s_part, 1)
                        if n == 4 and tc:
                            turn(tc - 1)
                turn(NC - 1)

            @blk.scalar
            def _(act):
                act.wait_ge(w_in, 16)
                act.activation(wh[:], raw[:], ACT.Copy).then_inc(woh_done, 1)
                for k in range(NC * NH):
                    act.wait_ge(o_in[k % 4], 16 * (k // 4 + 1))
                    if k >= 4:
                        act.wait_ge(s_part, k - 3)
                    act.activation(oh[:, k % 4], o[:, k % 4], ACT.Copy).then_inc(oh_done, 1)

            @blk.vector
            def _(dve):
                dve.wait_ge(woh_done, 1)
                dve.tensor_tensor(wl_[:], raw[:], f32(wh[:]), ALU.subtract).then_inc(wol_done, 1)

                def finish(tc):
                    dve.wait_ge(y_turned, tc + 1)
                    dve.wait_ge(xr_in[tc % 2], 16 * (tc // 2 + 1))
                    if tc >= 2:
                        dve.wait_ge(stored[tc % 2], 16 * (tc // 2))
                    yt = ps[:, 4:6, :].rearrange("p a (t d) -> p (a t) d", d=DM)
                    dve.tensor_tensor(yo[:, tc % 2], yt, xr[:, tc % 2], ALU.add).then_inc(yo_done, 1)
                for tc in range(NC):
                    for n in range(NH):
                        k = tc * NH + n
                        dve.wait_ge(oh_done, k + 1)
                        dve.tensor_tensor(ol[:, k % 4], o[:, k % 4], f32(oh[:, k % 4]), ALU.subtract).then_inc(ol_done, 1)
                        if n == 8 and tc:
                            finish(tc - 1)
                    dve.wait_ge(s_part, (tc + 1) * NH)
                    if tc:
                        dve.wait_ge(y_turned, tc)
                    dve.tensor_tensor(y[:], ps[:, 2 * (tc % 2):2 * (tc % 2) + 2, :], g_t[:, :, tc * CH:(tc + 1) * CH], ALU.mult)\
                        .then_inc(y_done, 1)
                finish(NC - 1)

    norm_phase()
    if stop == 2 or stop > 6:
        mlp_phase()
    if stop >= 3:
        kv_phase()
    if stop >= 4:
        compress_phase()
    if stop >= 5:
        query_phase()
    dense.close()
    if stop >= 6:
        attention_phase()
    if stop >= 7:
        out_phase()
    g = dict(locals())
    return g


def constants():
    inv = 1.0 / 10000.0 ** (np.arange(0, D, 2, dtype=np.float32) / D)
    ang = np.outer(np.arange(T, dtype=np.float32), inv).T
    cos, sin = np.tile(np.cos(ang), (4, 1)), np.tile(np.sin(ang), (4, 1))
    rot = np.stack([np.stack([cos, sin], 1), np.stack([-sin, cos], 1)], 1).astype(np.float32)
    row = np.arange(P)[:, None]
    col = np.arange(WW)[None]
    mask_a = np.where((col > row) & (col <= row + WIN), 0.0, NEG).astype(np.float32)
    mask_b = np.where((col >= row) & (col < row + WIN), 0.0, NEG).astype(np.float32)
    pick = np.tile(np.eye(4 * TJ, dtype=np.float32).reshape(4 * TJ, 4, TJ), (2, 1, 1))
    return {"mask_a": mask_a, "mask_b": mask_b, "pick": pick, "ident": np.eye(P, dtype=np.float32), "rot_k": rot, "rot_q": rot * np.float32(0.125)}


_INS = ['L0_attn_x', 'L0_attn_W_q', 'L0_attn_W_k', 'L0_attn_W_v', 'L0_attn_W_o', 'L0_attn_W_ck', 'L0_attn_W_cv',
        'L0_attn_W_gate', 'L0_ffn_gate_W_packed', 'L0_ffn_gate_scales', 'L0_ffn_up_W_packed',
        'L0_ffn_up_scales', 'L0_ffn_down_W_packed', 'L0_ffn_down_scales']


def kernel(**inputs):
    import numpy as _np
    import concourse.bacc as _bacc
    from concourse import mybir as _mybir
    from concourse.bass_utils import run_bass_kernel_spmd as _run

    nc = _bacc.Bacc("TRN2", target_bir_lowering=False, num_devices=1)
    arrays = {name: _np.ascontiguousarray(inputs[name]) for name in _INS}
    arrays.update(constants())
    args = {n: nc.dram_tensor(f"in_{n}", v.shape, _mybir.dt.from_np(v.dtype), kind="ExternalInput").ap()
            for n, v in arrays.items()}
    out = nc.dram_tensor("out_0", (B, T, DM), F32, kind="ExternalOutput").ap()
    build(nc, args, out)
    r = _run(nc, [{f"in_{n}": v for n, v in arrays.items()}], core_ids=[0])
    return r.results[0]["out_0"]
```

```python
from contextlib import ExitStack

import numpy as np
import concourse.bass as bass
from concourse import mybir

ALU = mybir.AluOpType
ACT = mybir.ActivationFunctionType
X = mybir.AxisListType.X
F32 = mybir.dt.float32
F32R = mybir.dt.float32r
BF16 = mybir.dt.bfloat16
I32 = mybir.dt.int32
I16 = mybir.dt.int16

P = 128
B, T, DM = 2, 1024, 256
H, HKV, D = 32, 8, 64
REP = H // HKV
BS = 64
NBLK = T // BS
WIN = 64
F = 2048
QB = 32
KT = DM // P
NTOK = B * T
TB = NTOK // P
TJ = T // P
CH = 512
NC = NTOK // CH
WW = P + WIN
NEG = -1.0e30
EPS = 1e-5


class Chain:

    def __init__(self, eng, sem):
        self.eng, self.sem, self.n, self.base = eng, sem, 0, 0

    def link(self, ins):
        ins.then_inc(self.sem, 1)
        self.n += 1
        self.eng.wait_ge(self.sem, self.base + self.n)


def f32(ap):
    return ap.bitcast(F32)


def build(nc, a, out, stop=99):
    main = ExitStack()

    def dram(name, shape, dt):
        return nc.dram_tensor(name, shape, dt).ap()

    q_scr = dram("q_scr", [HKV, B, 2, 2, P, T], F32)
    k_scr = dram("k_scr", [2, B, 2, 2, P, T], F32)
    vt_scr = dram("vt_scr", [4, B, 2, P, T], F32)
    pc_scr = dram("pc_scr", [HKV, P, T], F32)
    vc_scr = dram("vc_scr", [2, P, D], F32)
    o_scr = dram("o_scr", [B, H * D, T], F32)

    def sb(name, shape, dt, ctx=main):
        return ctx.enter_context(nc.sbuf_tensor(name, shape, dt))

    def sem(name, ctx=main):
        return ctx.enter_context(nc.semaphore(name))

    ps = main.enter_context(nc.psum_tensor("ps", [P, 8, CH], F32))
    ident = sb("ident_sb", [P, P], F32)
    gate_c = sb("gate_c", [P, TB], F32)
    ln_gate = sb("ln_gate", [P, 2, TB], F32)
    v_all = sb("v_all", [P, TB, HKV * D], F32)
    g_t = sb("g_t", [P, 2, NTOK], F32)
    dense = ExitStack()
    kc_all = sb("kc_all", [P, 2, 2, NBLK * B * HKV], F32R, dense)
    xh = sb("xh", [P, KT, NTOK], F32R, dense)
    xl = sb("xl", [P, KT, NTOK], F32R, dense)
    x_tok = a["L0_attn_x"].rearrange("b (n p) d -> p (b n) d", p=P)

    def three(kt, wh, wl, xh_ap, xl_ap):
        return [(wh, xh_ap), (wl, xh_ap), (wh, xl_ap)]

    def norm_and_weights(hi, lo):
        with ExitStack() as c:
            names = ["gate", "up", "down"]
            scl = sb("scl", [P, 3, P], F32, c)
            w = sb("w", [P, 2048, 2], F32, c)
            xt = g_t[:].rearrange("p h (a d) -> p (h a) d", d=DM)
            xn = w[:].rearrange("p k two -> p (k two)").rearrange("p (t d) -> p t d", d=DM)
            room = v_all[:].rearrange("p t d -> p (t d)").rearrange("p (r n) -> p r n", r=4)
            packed = room[:, 0, :].bitcast(I32)
            code, sign = (room[:, 1, :].bitcast(I16).rearrange("p (r n) -> p r n", r=2)[:, r, :] for r in range(2))
            u1, u2 = (room[:, 2, :].bitcast(BF16).rearrange("p (r n) -> p r n", r=2)[:, r, :] for r in range(2))
            low = packed.bitcast(I16).rearrange("p (n two) -> p n two", two=2)[:, :, 0]
            st = sb("st", [P, TB, 6], F32, c)
            mv = sb("mv", [P, TB, 2], F32, c)
            rstd = sb("rstd", [P, TB], F32, c)
            wg = sb("wg", [P, KT, 3], F32, c)
            z = sb("z", [P, TB, 3], F32, c)
            ez = sb("ez", [P, TB, 3], F32, c)
            zs = sb("zs", [P, 3, TB], F32, c)
            x_in = [sem(f"x_in{q}", c) for q in range(4)]
            const_in = sem("n_const_in", c)
            stat = sem("n_stat", c)
            var_ready = sem("var_ready", c)
            std_ready = sem("std_ready", c)
            normed = sem("normed", c)
            turned = sem("n_turned", c)
            hi_done = sem("n_hi", c)
            lo_done = sem("n_lo", c)
            z_ready = sem("z_ready", c)
            shifted = sem("z_shifted", c)
            exped = sem("z_exped", c)
            summed = sem("z_summed", c)
            logged = sem("z_logged", c)
            zch = sem("z_chain", c)
            packed_in = sem("packed_in", c)
            scale_in = sem("scale_in", c)
            dch = sem("deq_chain", c)
            unpacked = sem("unpacked", c)
            w_ready = sem("w_ready", c)
            w_turned = sem("w_turned", c)
            w_hi_done = sem("w_hi_done", c)
            w_lo_done = sem("w_lo_done", c)
            blk = c.enter_context(nc.Block())
            srcs = [(a[f"L0_ffn_{m}_W_packed"].rearrange("(n p) k -> p n k", p=P),
                     a[f"L0_ffn_{m}_scales"].rearrange("(n p) k -> p n k", p=P)) for m in names]

            @blk.sync
            def _(sp):
                for q in range(4):
                    sp.dma_start(xt[:, 4 * q:4 * q + 4, :], x_tok[:, 4 * q:4 * q + 4, :]).then_inc(x_in[q], 16)
                sp.dma_start(ident[:], a["ident"]).then_inc(const_in, 16)
                sp.dma_start(wg[:], a["L0_attn_W_gate"].rearrange("(k p) n -> p k n", p=P)).then_inc(const_in, 16)
                for m in range(3):
                    n = srcs[m][0].shape[1]
                    if m == 0:
                        for k in range(3):
                            dst = scl[:, k, :].rearrange("p (n k) -> p n k", n=srcs[k][0].shape[1])
                            sp.dma_start(dst, srcs[k][1]).then_inc(scale_in, 16)
                    else:
                        sp.wait_ge(unpacked, 4 * m)
                    sp.dma_start(packed.rearrange("p (n k) -> p n k", n=n), srcs[m][0]).then_inc(packed_in, 16)

            @blk.vector
            def _(dve):
                ch = Chain(dve, stat)
                for t in range(TB):
                    if t % 4 == 0:
                        dve.wait_ge(x_in[t // 4], 16)
                    dve.bn_stats(st[:, t, :], xt[:, t, :]).then_inc(stat, 1)
                dve.wait_ge(stat, TB)
                for t in range(TB):
                    dve.bn_aggr(mv[:, t, :], st[:, t, :]).then_inc(stat, 1)
                dve.wait_ge(stat, 2 * TB)
                ch.n = 2 * TB
                dve.tensor_scalar(rstd[:], mv[:, :, 1], EPS, None, ALU.add).then_inc(var_ready, 1)
                dve.wait_ge(std_ready, 1)
                ch.link(dve.reciprocal(rstd[:], rstd[:]))
                for t in range(TB):
                    dve.tensor_scalar(xn[:, t, :], xt[:, t, :], mv[:, t, 0:1], rstd[:, t:t + 1],
                                      ALU.subtract, ALU.mult).then_inc(normed, 1)
                for n in range(8):
                    kt, q = n // 4, n % 4
                    dve.wait_ge(hi_done, n + 1)
                    cols = slice(q * CH, (q + 1) * CH)
                    dve.tensor_tensor(xl[:, kt, cols], ps[:, n, :], f32(xh[:, kt, cols]), ALU.subtract).then_inc(lo_done, 1)

                dc = Chain(dve, dch)

                def weights(m):
                    dve.wait_ge(packed_in, 16 * (m + 1))
                    if m == 0:
                        dve.wait_ge(scale_in, 48)
                        dc.link(dve.tensor_scalar(scl[:], scl[:], 0.5, None, ALU.mult))
                    for half in range(2):
                        if m or half:
                            dve.wait_ge(w_ready, 2 * m + half)
                        dve.tensor_scalar(code, low, 4 * half, 7, ALU.logical_shift_right,
                                          ALU.bitwise_and).then_inc(unpacked, 1)
                        dve.tensor_scalar(sign, low, 12 - 4 * half, -32768, ALU.logical_shift_left,
                                          ALU.bitwise_and).then_inc(unpacked, 1)
                        dve.wait_ge(unpacked, 4 * m + 2 * half + 2)
                        dve.tensor_scalar(u1, code, 2.0, -4.0, ALU.mult, ALU.add)
                        dc.link(dve.tensor_scalar(u2, code, 4.0, -16.0, ALU.mult, ALU.add))
                        dc.link(dve.tensor_tensor(u1, u1, code, ALU.max))
                        dc.link(dve.tensor_tensor(u1, u1, u2, ALU.max))
                        dc.link(dve.tensor_tensor(u2.bitcast(I16), u1.bitcast(I16), sign, ALU.bitwise_or))
                        if m and half == 0:
                            dve.wait_ge(w_turned, 8 * m)
                        elif half == 0:
                            dve.wait_ge(turned, 8)
                        dve.tensor_tensor(w[:, :, half].rearrange("p (s k) -> p s k", k=QB // 2),
                                          u2.rearrange("p (s k) -> p s k", k=QB // 2),
                                          scl[:, m, :].unsqueeze(2).broadcast_to([P, P, QB // 2]), ALU.mult).then_inc(w_ready, 1)

                def split(m):
                    for n in range(8):
                        dve.wait_ge(w_hi_done, 8 * m + n + 1)
                        dve.tensor_tensor(lo[m][:, 4 * n:4 * n + 4, :], ps[:, n, :].rearrange("p (c k) -> p c k", c=4),
                                          f32(hi[m][:, 4 * n:4 * n + 4, :]), ALU.subtract).then_inc(w_lo_done, 1)

                weights(0)
                split(0)
                weights(1)
                zc = Chain(dve, zch)
                dve.wait_ge(z_ready, 1)
                zp = ps[:, 0, 0:3 * TB].rearrange("p (t g) -> p t g", g=3)
                zc.link(dve.tensor_reduce(zs[:, 0, :], zp, X, ALU.max))
                dve.tensor_tensor(z[:], zp, zs[:, 0, :].unsqueeze(2).broadcast_to([P, TB, 3]), ALU.subtract).then_inc(shifted, 1)
                split(1)
                weights(2)
                dve.wait_ge(exped, 1)
                dve.tensor_reduce(zs[:, 1, :], ez[:], X, ALU.add).then_inc(summed, 1)
                dve.wait_ge(summed, 1)
                zc.link(dve.reciprocal(zs[:, 0, :], zs[:, 1, :]))
                dve.tensor_tensor(gate_c[:], ez[:, :, 0], zs[:, 0, :], ALU.mult)
                split(2)
                dve.wait_ge(logged, 1)
                for br in range(2):
                    dve.tensor_tensor(ln_gate[:, br, :], z[:, :, 1 + br], zs[:, 2, :], ALU.subtract)

            @blk.scalar
            def _(act):
                act.wait_ge(var_ready, 1)
                act.activation(rstd[:], rstd[:], ACT.Sqrt).then_inc(std_ready, 1)
                for n in range(8):
                    kt, q = n // 4, n % 4
                    act.wait_ge(turned, n + 1)
                    act.activation(xh[:, kt, q * CH:(q + 1) * CH], ps[:, n, :], ACT.Copy).then_inc(hi_done, 1)
                for m in range(3):
                    for n in range(8):
                        act.wait_ge(w_turned, 8 * m + n + 1)
                        act.activation(hi[m][:, 4 * n:4 * n + 4, :], ps[:, n, :].rearrange("p (c k) -> p c k", c=4),
                                       ACT.Copy).then_inc(w_hi_done, 1)
                    if m == 1:
                        act.wait_ge(shifted, 1)
                        act.activation(ez[:], z[:], ACT.Exp).then_inc(exped, 1)
                act.wait_ge(summed, 1)
                act.activation(zs[:, 2, :], zs[:, 1, :], ACT.Ln).then_inc(logged, 1)

            @blk.tensor
            def _(pe):
                pe.wait_ge(const_in, 32)
                for n in range(8):
                    kt, q = n // 4, n % 4
                    pe.wait_ge(normed, 4 * q + 4)
                    for t in range(4):
                        ins = pe.transpose(ps[:, n, t * P:(t + 1) * P], xn[:, 4 * q + t, kt * P:(kt + 1) * P], ident[:])
                    ins.then_inc(turned, 1)
                pe.wait_ge(lo_done, 8)
                for m in range(3):
                    pe.wait_ge(w_ready, 2 * m + 2)
                    for n in range(8):
                        if m:
                            pe.wait_ge(w_lo_done, 8 * (m - 1) + n + 1)
                        if m == 1 and n == 0:
                            pe.wait_ge(shifted, 1)
                        for t in range(4):
                            wt = w[:].rearrange("p k two -> p (k two)")[:, (4 * n + t) * P:(4 * n + t + 1) * P]
                            ins = pe.transpose(ps[:, n, t * P:(t + 1) * P], wt, ident[:])
                        ins.then_inc(w_turned, 1)
                    if m == 0:
                        pe.wait_ge(w_lo_done, 1)
                        for t in range(TB):
                            for n, (kt, part) in enumerate((kt, part) for kt in range(KT) for part in (xh, xl)):
                                ins = pe.matmul(ps[:, 0, 3 * t:3 * t + 3], f32(part[:, kt, t * P:(t + 1) * P]), wg[:, kt, :],
                                                start=(n == 0), stop=(n == 3))
                        ins.then_inc(z_ready, 1)

    def mlp_phase(hi, lo):
        with ExitStack() as c:
            NT = F // P
            steps = v_all[:].rearrange("p t d -> p (t d)").rearrange("p (r h n) -> p r h n", h=2, n=CH)
            sq, cub, th, hg, it, se, oc = (steps[:, r] for r in range(7))
            ih = sb("ih", [P, 4, CH], F32R, c)
            il = sb("il", [P, 4, CH], F32R, c)
            gu_ready = sem("gu_ready", c)
            sq_ready = sem("sq_ready", c)
            cub_half = sem("cub_half", c)
            cub_ready = sem("cub_ready", c)
            th_ready = sem("th_ready", c)
            hg_ready = sem("hg_ready", c)
            it_ready = sem("it_ready", c)
            ih_ready = sem("ih_ready", c)
            il_ready = sem("il_ready", c)
            down_done = sem("down_done", c)
            o_copied = sem("o_copied", c)
            se_ready = sem("se_ready", c)
            g_done = sem("g_done", c)
            LAGD, PIECES = 3, 4

            def steps_of(step):
                def run(eng):
                    for tc in range(2):
                        for n in range(NT):
                            step(tc, n, True, lambda k, tc=tc, n=n: tc * NT + n - k >= 0)
                    with eng.Fori(2, NC) as tc:
                        for n in range(NT):
                            step(tc, n, True, lambda k: True)
                    for n in range(LAGD + 1):
                        step(NC, n, False, lambda k, n=n: n - k < 0)
                return run

            def slot(n):
                return 2 if n == NT - 1 else 2 * (n % 3)

            with nc.Block() as blk:
                @blk.tensor
                def _(pe):
                    def down(t, n, tc, first):
                        pe.wait_ge(il_ready, t + 1)
                        if n == 0 and not first:
                            pe.wait_ge(o_copied, tc)
                        for ht in range(2):
                            w_i = ht * NT + n
                            prods = three(0, hi[2][:, w_i, :], lo[2][:, w_i, :], ih[:, n % 4, :], il[:, n % 4, :])
                            for k, (wt, xt) in enumerate(prods):
                                ins = pe.matmul(ps[:, 6 + ht, :], wt, xt, start=(n == 0 and k == 0),
                                                stop=(n == NT - 1 and k == 2))
                        ins.then_inc(down_done, 1)

                    def step(tc, n, fresh, have):
                        t = tc * NT + n
                        if fresh:
                            cols = bass.ds(tc * CH, CH)
                            back = {0: 4, 1: 2, NT - 1: 2}.get(n, 3)
                            if have(back):
                                pe.wait_ge(it_ready, t - back + 1)
                            for m in range(2):
                                k = 0
                                for kt in range(KT):
                                    w_i = 2 * n + kt
                                    for wt, xt in three(kt, hi[m][:, w_i, :], lo[m][:, w_i, :], xh[:, kt, cols], xl[:, kt, cols]):
                                        ins = pe.matmul(ps[:, slot(n) + m, :], wt, xt, start=(k == 0), stop=(k == 5))
                                        k += 1
                            ins.then_inc(gu_ready, 1)
                        if have(LAGD):
                            down(t - LAGD, (n - LAGD) % NT, tc, isinstance(tc, int) and tc == 0)
                    steps_of(step)(pe)

                @blk.scalar
                def _(act):
                    def step(tc, n, fresh, have):
                        t = tc * NT + n
                        if n == LAGD and have(n + 1):
                            if not (isinstance(tc, int) and tc == 1):
                                act.wait_ge(g_done, PIECES * (tc - 1))
                            act.wait_ge(down_done, tc * NT)
                            act.activation(oc, ps[:, 6:8, :], ACT.Copy).then_inc(o_copied, 1)
                            act.wait_ge(o_copied, tc)
                            act.activation(se, oc, ACT.Sigmoid).then_inc(se_ready, 1)
                        if fresh:
                            act.wait_ge(gu_ready, t + 1)
                            if have(2):
                                act.wait_ge(cub_half, t - 1)
                            act.activation(sq[:, n % 2, :], ps[:, slot(n), :], ACT.Square).then_inc(sq_ready, 1)
                        if have(1):
                            act.wait_ge(cub_ready, t)
                            act.activation(th[:, (n - 1) % 2, :], cub[:, (n - 1) % 2, :], ACT.Tanh,
                                           scale=0.7978845608028654).then_inc(th_ready, 1)
                        if have(2):
                            act.wait_ge(it_ready, t - 1)
                            if have(6):
                                act.wait_ge(down_done, t - 5)
                            act.activation(ih[:, (n - 2) % 4, :], it[:, n % 2, :], ACT.Copy).then_inc(ih_ready, 1)
                    steps_of(step)(act)

                @blk.vector
                def _(dve):
                    def silu(tc, piece):
                        w = CH // PIECES
                        s = se[:, :, piece * w:(piece + 1) * w]
                        if piece == 0:
                            dve.wait_ge(se_ready, tc)
                        dve.tensor_tensor(g_t[:, :, bass.ds((tc - 1) * CH + piece * w, w)],
                                          oc[:, :, piece * w:(piece + 1) * w], s, ALU.mult).then_inc(g_done, 1)

                    def step(tc, n, fresh, have):
                        t = tc * NT + n
                        if fresh:
                            gp = ps[:, slot(n), :]
                            dve.wait_ge(sq_ready, t + 1)
                            dve.tensor_scalar(sq[:, n % 2, :], sq[:, n % 2, :], 0.044715, 1.0, ALU.mult,
                                              ALU.add).then_inc(cub_half, 1)
                            dve.wait_ge(cub_half, t + 1)
                            if have(2):
                                dve.wait_ge(th_ready, t - 1)
                            dve.tensor_tensor(cub[:, n % 2, :], gp, sq[:, n % 2, :], ALU.mult).then_inc(cub_ready, 1)
                        if have(1):
                            m = (n - 1) % NT
                            dve.wait_ge(th_ready, t)
                            dve.scalar_tensor_tensor(hg[:, m % 2, :], th[:, m % 2, :], 1.0, ps[:, slot(m), :],
                                                     ALU.add, ALU.mult).then_inc(hg_ready, 1)
                            dve.wait_ge(hg_ready, t)
                            if have(3):
                                dve.wait_ge(ih_ready, t - 2)
                            dve.scalar_tensor_tensor(it[:, m % 2, :], hg[:, m % 2, :], 0.5, ps[:, slot(m) + 1, :],
                                                     ALU.mult, ALU.mult).then_inc(it_ready, 1)
                        if have(2):
                            m = (n - 2) % NT
                            dve.wait_ge(ih_ready, t - 1)
                            dve.tensor_tensor(il[:, m % 4, :], it[:, m % 2, :], f32(ih[:, m % 4, :]),
                                              ALU.subtract).then_inc(il_ready, 1)
                        if fresh and LAGD < n <= LAGD + PIECES and have(n + 1):
                            silu(tc, n - LAGD - 1)
                        if not fresh and n == LAGD:
                            for piece in range(PIECES):
                                silu(tc, piece)
                    steps_of(step)(dve)

    def kv_phase():
        with ExitStack() as c:
            raw = sb("kv_raw", [P, 2, KT, HKV * D], F32, c)
            wk = [sb(f"wk{n}", [P, KT, 2, 2, P], F32R, c) for n in ("h", "l")]
            wv = [sb(f"wv{n}", [P, KT, HKV * D], F32R, c) for n in ("h", "l")]
            rot = sb("rot_k_sb", [P, 2, 2, T], F32, c)
            tu = sb("tu", [P, 2, 2, 2, CH], F32, c)
            ab = sb("ab", [P, 2, 2, CH], F32, c)
            kh = sb("kh", [P, 2, 2, CH], F32R, c)
            kl = sb("kl", [P, 2, 2, CH], F32R, c)
            vh = sb("vh", [P, 2, 2, CH], F32R, c)
            vl = sb("vl", [P, 2, 2, CH], F32R, c)
            kv_in = sem("kv_in", c)
            wh_done = sem("wh_done", c)
            wl_done = sem("wl_done", c)
            k_ready = sem("k_ready", c)
            vt_ready = sem("vt_ready", c)
            k_rot = sem("k_rot", c)
            k_sum = sem("k_sum", c)
            k_hi = sem("k_hi", c)
            k_lo = sem("k_lo", c)
            vt_hi = sem("vt_hi", c)
            vt_lo = sem("vt_lo", c)
            k_stored = [sem(f"k_stored{n}", c) for n in range(2)]
            vt_stored = [sem(f"vt_stored{n}", c) for n in range(2)]
            v_ready = sem("v_ready", c)
            v_done = sem("v_done", c)
            blk = c.enter_context(nc.Block())

            def k_view(ap):
                return ap.rearrange("p (g h i e) -> p g e h i", g=2, h=4, e=2)

            @blk.sync
            def _(sp):
                for n, w in enumerate(("W_k", "W_v")):
                    sp.dma_start(raw[:, n], a["L0_attn_" + w].rearrange("(k p) n -> p k n", p=P)).then_inc(kv_in, 16)
                sp.dma_start(rot[:], a["rot_k"]).then_inc(kv_in, 16)
                for b in range(B):
                    for half in range(2):
                        cols = slice(half * CH, (half + 1) * CH)
                        for n in range(2):
                            sp.wait_ge(vt_lo, 4 * b + 2 * half + n + 1)
                            for part, t in ((0, vh), (1, vl)):
                                dst = vt_scr[2 * n:2 * n + 2, b, part, :, cols].rearrange("j p t -> p j t")
                                sp.dma_start(dst, f32(t[:, n])).then_inc(vt_stored[n], 16)
                            sp.wait_ge(k_lo, 4 * b + 2 * half + n + 1)
                            for part, t in ((0, kh), (1, kl)):
                                dst = k_scr[n, b, part, :, :, cols].rearrange("e p t -> p e t")
                                sp.dma_start(dst, f32(t[:, n])).then_inc(k_stored[n], 16)
                for n in range(2):
                    sp.wait_ge(k_stored[n], 2 * 16 * 4)
                    sp.wait_ge(vt_stored[n], 2 * 16 * 4)

            @blk.tensor
            def _(pe):
                pe.wait_ge(wl_done, 6)
                for b in range(B):
                    for half in range(2):
                        cols = slice(b * T + half * CH, b * T + (half + 1) * CH)
                        for n in range(2):
                            if b or half:
                                pe.wait_ge(k_rot, 4 * b + 2 * half + n - 1)
                            for e in range(2):
                                k = 0
                                for kt in range(KT):
                                    for w, x in three(kt, wk[0][:, kt, n, e, :], wk[1][:, kt, n, e, :],
                                                      xh[:, kt, cols], xl[:, kt, cols]):
                                        ins = pe.matmul(ps[:, 2 * n + e, :], w, x, start=(k == 0), stop=(k == 5))
                                        k += 1
                            ins.then_inc(k_ready, 1)
                        for n in range(2):
                            if b or half:
                                pe.wait_ge(vt_lo, 4 * b + 2 * half + n - 1)
                            for e in range(2):
                                k = 0
                                ws = slice((2 * n + e) * P, (2 * n + e + 1) * P)
                                for kt in range(KT):
                                    for w, x in three(kt, wv[0][:, kt, ws], wv[1][:, kt, ws], xh[:, kt, cols], xl[:, kt, cols]):
                                        ins = pe.matmul(ps[:, 4 + 2 * n + e, :], w, x, start=(k == 0), stop=(k == 5))
                                        k += 1
                            ins.then_inc(vt_ready, 1)
                pe.wait_ge(k_rot, 8)
                pe.wait_ge(vt_lo, 8)
                for t in range(TB):
                    if t >= 8:
                        pe.wait_ge(v_done, t - 7)
                    k = 0
                    ts = slice(t * P, (t + 1) * P)
                    for kt in range(KT):
                        for x, w in three(kt, xh[:, kt, ts], xl[:, kt, ts], wv[0][:, kt, :], wv[1][:, kt, :]):
                            ins = pe.matmul(ps[:, t % 8, :], x, w, start=(k == 0), stop=(k == 5))
                            k += 1
                    ins.then_inc(v_ready, 1)

            @blk.scalar
            def _(act):
                act.wait_ge(kv_in, 48)
                for kt in range(KT):
                    for n in range(2):
                        act.activation(wk[0][:, kt, n].rearrange("p e (h i) -> p e h i", h=4), k_view(raw[:, 0, kt, :])[:, n],
                                       ACT.Copy).then_inc(wh_done, 1)
                for kt in range(KT):
                    act.activation(wv[0][:, kt, :], raw[:, 1, kt, :], ACT.Copy).then_inc(wh_done, 1)
                for b in range(B):
                    for half in range(2):
                        for n in range(2):
                            act.wait_ge(vt_ready, 4 * b + 2 * half + n + 1)
                            if b or half:
                                act.wait_ge(vt_stored[n], 64 * b + 32 * half)
                            act.activation(vh[:, n], ps[:, 4 + 2 * n:6 + 2 * n, :], ACT.Copy).then_inc(vt_hi, 1)
                            act.wait_ge(k_sum, 4 * b + 2 * half + n + 1)
                            if b or half:
                                act.wait_ge(k_stored[n], 64 * b + 32 * half)
                            act.activation(kh[:, n], ab[:, n], ACT.Copy).then_inc(k_hi, 1)
                for t in range(TB):
                    act.wait_ge(v_ready, t + 1)
                    act.activation(v_all[:, t, :], ps[:, t % 8, :], ACT.Copy).then_inc(v_done, 1)

            @blk.gpsimd
            def _(pool):
                for b in range(B):
                    for half in range(2):
                        for n in range(2):
                            pool.wait_ge(k_rot, 4 * b + 2 * half + n + 1)
                            if b or half:
                                pool.wait_ge(k_lo, 4 * b + 2 * half + n - 1)
                            pool.tensor_tensor(ab[:, n], tu[:, n, 0], tu[:, n, 1], ALU.add).then_inc(k_sum, 1)

            @blk.vector
            def _(dve):
                for kt in range(KT):
                    for n in range(2):
                        dve.wait_ge(wh_done, 2 * kt + n + 1)
                        dve.tensor_tensor(wk[1][:, kt, n].rearrange("p e (h i) -> p e h i", h=4),
                                          k_view(raw[:, 0, kt, :])[:, n],
                                          f32(wk[0][:, kt, n]).rearrange("p e (h i) -> p e h i", h=4),
                                          ALU.subtract).then_inc(wl_done, 1)
                for kt in range(KT):
                    dve.wait_ge(wh_done, 5 + kt)
                    dve.tensor_tensor(wv[1][:, kt, :], raw[:, 1, kt, :], f32(wv[0][:, kt, :]), ALU.subtract).then_inc(wl_done, 1)
                for b in range(B):
                    for half in range(2):
                        cols = slice(half * CH, (half + 1) * CH)
                        for n in range(2):
                            dve.wait_ge(k_ready, 4 * b + 2 * half + n + 1)
                            if b or half:
                                dve.wait_ge(k_sum, 4 * b + 2 * half + n - 1)
                            for e in range(2):
                                ins = dve.tensor_tensor(tu[:, n, e], ps[:, 2 * n + e, :].unsqueeze(1).broadcast_to([P, 2, CH]),
                                                        rot[:, e, :, cols], ALU.mult)
                            ins.then_inc(k_rot, 1)
                        for n in range(2):
                            dve.wait_ge(vt_hi, 4 * b + 2 * half + n + 1)
                            dve.tensor_tensor(vl[:, n], ps[:, 4 + 2 * n:6 + 2 * n, :], f32(vh[:, n]), ALU.subtract).then_inc(vt_lo, 1)
                            dve.wait_ge(k_hi, 4 * b + 2 * half + n + 1)
                            dve.tensor_tensor(kl[:, n], ab[:, n], f32(kh[:, n]), ALU.subtract).then_inc(k_lo, 1)

    def compress_phase():
        NK = NBLK * B * HKV
        with ExitStack() as c:
            kx = sb("kx", [P, B * HKV, T], F32R, c)
            raw = sb("wc_raw", [P, BS, D], F32, c)
            wc = [sb(f"wc{n}", [P, BS, D], F32R, c) for n in ("h", "l")]
            vct = sb("vct", [D, NK], F32, c)
            vcn = sb("vcn", [P, 2, D], F32, c)
            x_in = [sem(f"kx_in{n}", c) for n in range(2)]
            w_in = sem("wc_in", c)
            wch_done = sem("wch_done", c)
            wcl_done = sem("wcl_done", c)
            c_done = sem("c_done", c)
            kc_hi = sem("kc_hi", c)
            kc_lo = sem("kc_lo", c)
            vct_done = sem("vct_done", c)
            vc_turned = sem("vc_turned", c)
            vcn_done = sem("vcn_done", c)
            vc_stored = sem("vc_stored", c)
            blk = c.enter_context(nc.Block())
            wck = a["L0_attn_W_ck"].rearrange("(s i e) n -> e i s n", s=BS, e=2)
            wcv = a["L0_attn_W_cv"].rearrange("(s d) n -> d s n", s=BS)

            @blk.sync
            def _(sp):
                for r in range(2):
                    for e in range(2):
                        sp.dma_start(raw[r * 64 + e * 32:r * 64 + e * 32 + 32], wck[e]).then_inc(w_in, 16)
                for g in range(HKV):
                    for b in range(B):
                        src = k_scr[g // 4, b, :, :, 32 * (g % 4):32 * (g % 4) + 32, :].rearrange("l e i t -> (l e) i t")
                        sp.dma_start(f32(kx[:, 2 * g + b, :]), src).then_inc(x_in[0], 16)
                sp.wait_ge(wcl_done, 1)
                for r in range(2):
                    sp.dma_start(raw[r * 64:r * 64 + 64], wcv).then_inc(w_in, 16)
                sp.wait_ge(c_done, 1)
                for g in range(HKV):
                    for b in range(B):
                        src = vt_scr[g // 2, b, :, 64 * (g % 2):64 * (g % 2) + 64, :]
                        sp.dma_start(f32(kx[:, 2 * g + b, :]), src).then_inc(x_in[1], 16)
                sp.wait_ge(vcn_done, 1)
                sp.dma_start(vc_scr.rearrange("m p d -> p m d"), vcn[:]).then_inc(vc_stored, 16)
                sp.wait_ge(vc_stored, 16)

            @blk.tensor
            def _(pe):
                for m in range(2):
                    pe.wait_ge(wcl_done, m + 1)
                    pe.wait_ge(x_in[m], 16 * B * HKV)
                    for s in range(BS):
                        xs = kx[:].rearrange("p g (n s) -> p (g n) s", s=BS)[:, :, s]
                        for n in range(2):
                            ins = pe.matmul(ps[0:D, m, 0:NK], wc[n][:, s, :], xs, start=(s == 0 and n == 0),
                                            stop=(s == BS - 1 and n == 1))
                    ins.then_inc(c_done, 1)
                pe.wait_ge(vct_done, 1)
                for n in range(2):
                    ins = pe.transpose(ps[:, 2, n * D:(n + 1) * D], vct[:, n * P:(n + 1) * P], ident[0:D, 0:D])
                ins.then_inc(vc_turned, 1)

            @blk.scalar
            def _(act):
                for m in range(2):
                    act.wait_ge(w_in, 64 + 32 * m)
                    if m == 0:
                        src = raw[:].rearrange("p s (i e) -> p s e i", e=2)
                        for n in range(BS // 16):
                            rows = slice(16 * n, 16 * n + 16)
                            act.activation(wc[0][:, rows].rearrange("p s (e i) -> p s e i", e=2), src[:, rows], ACT.Copy)\
                                .then_inc(wch_done, 1)
                    else:
                        act.wait_ge(c_done, 1)
                        act.activation(wc[0][:], raw[:], ACT.Copy).then_inc(wch_done, 1)
                act.wait_ge(c_done, 2)
                act.activation(vct[:], ps[0:D, 1, 0:NK], ACT.Copy).then_inc(vct_done, 1)
                act.wait_ge(vc_turned, 1)
                act.activation(vcn[:], ps[:, 2, 0:2 * D].rearrange("p (m d) -> p m d", m=2), ACT.Copy).then_inc(vcn_done, 1)

            @blk.vector
            def _(dve):
                dve.wait_ge(wch_done, 4)
                src = raw[:].rearrange("p s (i e) -> p s e i", e=2)
                for n in range(4):
                    rows = slice(16 * n, 16 * n + 16)
                    ins = dve.tensor_tensor(wc[1][:, rows].rearrange("p s (e i) -> p s e i", e=2), src[:, rows],
                                            f32(wc[0][:, rows]).rearrange("p s (e i) -> p s e i", e=2), ALU.subtract)
                ins.then_inc(wcl_done, 1)
                dve.wait_ge(c_done, 1)
                for e in range(2):
                    for h in range(4):
                        dve.tensor_copy(kc_all[32 * h:32 * h + 32, e, 0, :], ps[32 * e:32 * e + 32, 0, 0:NK]).then_inc(kc_hi, 1)
                for e in range(2):
                    for h in range(4):
                        dve.wait_ge(kc_hi, 4 * e + h + 1)
                        dve.tensor_tensor(kc_all[32 * h:32 * h + 32, e, 1, :], ps[32 * e:32 * e + 32, 0, 0:NK],
                                          f32(kc_all[32 * h:32 * h + 32, e, 0, :]), ALU.subtract).then_inc(kc_lo, 1)
                dve.wait_ge(wch_done, 5)
                dve.tensor_tensor(wc[1][:], raw[:], f32(wc[0][:]), ALU.subtract).then_inc(wcl_done, 1)

    def query_phase():
        NJ = HKV * 4
        with ExitStack() as c:
            raw = sb("wq_raw", [P, KT, H * D], F32, c)
            wq = [sb(f"wq{n}", [P, 2, KT, 2, P], F32R, c) for n in ("h", "l")]
            rot = sb("rot_q_sb", [P, 2, 2, T], F32, c)
            tu = sb("q_tu", [P, 2, 2, 2, CH], F32, c)
            ab = sb("q_ab", [P, 2, 2, CH], F32, c)
            qh = sb("qh", [P, 4, 2, CH], F32R, c)
            ql = sb("ql", [P, 4, 2, CH], F32R, c)
            kcb = sb("kcb", [P, B, 2, 2, D], F32R, c)
            lc = sb("lc", [P, 2, CH], F32, c)
            mc = sb("mc", [P, 3, 16], F32, c)
            ec = sb("ec", [P, 16, 16], F32, c)
            prob_c = sb("prob_c", [P, 2, 4, P], F32, c)
            pc = sb("pc", [D, 2, CH], F32, c)
            q_in = sem("q_in", c)
            zeroed = sem("kcb_zeroed", c)
            wqh_done = sem("wqh_done", c)
            wql_done = sem("wql_done", c)
            q_ready = sem("q_ready", c)
            q_rot = sem("q_rot", c)
            q_sum = sem("q_sum", c)
            q_hi = sem("q_hi", c)
            q_lo = sem("q_lo", c)
            q_stored = [sem(f"q_stored{n}", c) for n in range(4)]
            kcb_ready = sem("kcb_ready", c)
            lc_ready = sem("lc_ready", c)
            lc_out = sem("lc_out", c)
            lt_ready = sem("lt_ready", c)
            c_max = sem("c_max", c)
            c_shift = sem("c_shift", c)
            c_exp = sem("c_exp", c)
            c_chain = sem("c_chain", c)
            c_prob = sem("c_prob", c)
            pt_ready = sem("pt_ready", c)
            pc_out = sem("pc_out", c)
            pc_stored = [sem(f"pc_stored{n}", c) for n in range(2)]
            blk = c.enter_context(nc.Block())
            L_SPLIT, L_COMP, L_MAX, L_PROB, L_BACK = 1, 2, 3, 4, 5

            def steps(eng, step):
                for k in range(8):
                    step(0, k, lambda lag, k=k: k >= lag)
                with eng.Fori(1, NJ // 8) as it:
                    for k in range(8):
                        step(it, k, lambda lag: True)
                for k in range(L_BACK):
                    step(NJ // 8, k, lambda lag, k=k: k < lag)

            def place(it, k, lag):
                j, m = 8 * it + k - lag, (k - lag) % 8
                first = isinstance(it, int) and it == 0
                return j, m, 2 * it + (k - lag) // 4, m // 2 % 2, m % 2, (lambda n: not first or k - lag >= n)

            @blk.sync
            def _(sp):
                sp.dma_start(raw[:], a["L0_attn_W_q"].rearrange("(k p) n -> p k n", p=P)).then_inc(q_in, 16)
                sp.dma_start(rot[:], a["rot_q"]).then_inc(q_in, 16)

                def step(it, k, on):
                    if on(L_SPLIT):
                        j, m, g, b, half, _ = place(it, k, L_SPLIT)
                        cols = slice(half * CH, (half + 1) * CH)
                        for part, t, done in ((0, qh, q_hi), (1, ql, q_lo)):
                            sp.wait_ge(done, j + 1)
                            dst = q_scr[bass.ds(g, 1), b, part, :, :, cols].rearrange("g e p t -> p (g e) t")
                            sp.dma_start(dst, f32(t[:, m % 4])).then_inc(q_stored[m % 4], 16)
                    if on(L_BACK):
                        j, m, g, b, half, _ = place(it, k, L_BACK)
                        sp.wait_ge(pc_out, j + 1)
                        dst = pc_scr[bass.ds(g, 1), D * b:D * b + D, half * CH:(half + 1) * CH].rearrange("g p t -> (g p) t")
                        sp.dma_start(dst, pc[:, m % 2]).then_inc(pc_stored[m % 2], 16)
                steps(sp, step)
                for n in range(4):
                    sp.wait_ge(q_stored[n], 2 * 16 * (NJ // 4))
                for n in range(2):
                    sp.wait_ge(pc_stored[n], 16 * (NJ // 2))

            @blk.tensor
            def _(pe):
                def step(it, k, on):
                    if on(0):
                        j, m, g, b, half, past = place(it, k, 0)
                        if k % 4 == 0:
                            pe.wait_ge(wql_done, g + 1)
                        if past(2):
                            pe.wait_ge(q_rot, j - 1)
                        cols = slice(b * T + half * CH, b * T + (half + 1) * CH)
                        for e in range(2):
                            n = 0
                            for kt in range(KT):
                                for w, x in three(kt, wq[0][:, k // 4, kt, e, :], wq[1][:, k // 4, kt, e, :],
                                                  xh[:, kt, cols], xl[:, kt, cols]):
                                    ins = pe.matmul(ps[:, 2 * (k % 2) + e, :], w, x, start=(n == 0), stop=(n == 5))
                                    n += 1
                        ins.then_inc(q_ready, 1)
                    if on(L_COMP):
                        j, m, g, b, half, past = place(it, k, L_COMP)
                        pe.wait_ge(q_lo, j + 1)
                        pe.wait_ge(kcb_ready, 4 * (4 * it + (k - L_COMP) // 2 + 1))
                        if past(2):
                            pe.wait_ge(lc_out, j - 1)
                        n = 0
                        for e in range(2):
                            for w, x in ((0, qh), (1, qh), (0, ql)):
                                ins = pe.matmul(ps[0:D, 4 + m % 2, :], kcb[:, b, e, w, :], x[:, m % 4, e, :],
                                                start=(n == 0), stop=(n == 5))
                                n += 1
                        ins.then_inc(lc_ready, 1)
                    if on(L_MAX):
                        j, m, g, b, half, past = place(it, k, L_MAX)
                        if not past(1):
                            pe.wait_ge(zeroed, 3)
                        pe.wait_ge(lc_out, j + 1)
                        if past(1):
                            pe.wait_ge(c_shift, j)
                        for t in range(4):
                            ins = pe.transpose(ps[:, 6, t * P:(t + 1) * P], lc[:, m % 2, t * P:(t + 1) * P], ident[:])
                        ins.then_inc(lt_ready, 1)
                    if on(L_BACK):
                        j, m, g, b, half, past = place(it, k, L_BACK)
                        pe.wait_ge(c_prob, j + 1)
                        if past(1):
                            pe.wait_ge(pc_out, j)
                        for t in range(4):
                            ins = pe.transpose(ps[:, 7, t * P:(t + 1) * P], prob_c[:, m % 2, t, :], ident[:])
                        ins.then_inc(pt_ready, 1)
                steps(pe, step)

            @blk.gpsimd
            def _(pool):
                pool.memset(f32(kcb[:]), 0.0).then_inc(zeroed, 1)
                pool.memset(prob_c[:, :, :, D:P], 0.0).then_inc(zeroed, 1)
                pool.wait_ge(zeroed, 2)
                pool.memset(lc[D:P], 0.0).then_inc(zeroed, 1)
                pool.wait_ge(zeroed, 3)

                def step(it, k, on):
                    if not on(0):
                        return
                    j, m, g, b, half, past = place(it, k, 0)
                    if half == 0:
                        if past(4):
                            pool.wait_ge(lc_ready, j - 2)
                        for h in range(4):
                            src = kc_all[32 * h:32 * h + 32, :, :, bass.ds((2 * g + b) * NBLK, NBLK)]
                            pool.tensor_copy(kcb[32 * h:32 * h + 32, b, :, :, NBLK * h:NBLK * h + NBLK], f32(src))\
                                .then_inc(kcb_ready, 1)
                            pool.wait_ge(kcb_ready, 4 * (2 * g + b) + h + 1)
                    pool.wait_ge(q_rot, j + 1)
                    if past(2):
                        pool.wait_ge(q_lo, j - 1)
                    pool.tensor_tensor(ab[:, k % 2], tu[:, k % 2, 0], tu[:, k % 2, 1], ALU.add).then_inc(q_sum, 1)
                steps(pool, step)

            def w_view(g, kt):
                return raw[:, kt, bass.ds(g * REP * D, REP * D)].rearrange("p (h i e) -> p e h i", h=REP, e=2)

            def buffer_free(eng, j, m, n4, past):
                if past(4):
                    eng.wait_ge(q_stored[m % 4], 32 * n4)
                    eng.wait_ge(lc_ready, j - 3)

            @blk.scalar
            def _(act):
                act.wait_ge(q_in, 32)

                def step(it, k, on):
                    if on(0) and k % 4 == 0:
                        j, m, g, b, half, past = place(it, k, 0)
                        if past(8):
                            act.wait_ge(q_ready, j - 4)
                        for kt in range(KT):
                            ins = act.activation(wq[0][:, k // 4, kt].rearrange("p e (h i) -> p e h i", h=REP), w_view(g, kt), ACT.Copy)
                        ins.then_inc(wqh_done, 1)
                    if on(L_COMP):
                        j, m, g, b, half, past = place(it, k, L_COMP)
                        act.wait_ge(lc_ready, j + 1)
                        if past(2):
                            act.wait_ge(lt_ready, j - 1)
                        act.activation(lc[0:D, m % 2], ps[0:D, 4 + m % 2, :], ACT.Copy).then_inc(lc_out, 1)
                    if on(L_SPLIT):
                        j, m, g, b, half, past = place(it, k, L_SPLIT)
                        act.wait_ge(q_sum, j + 1)
                        buffer_free(act, j, m, 2 * it + (k - L_SPLIT) // 4, past)
                        act.activation(qh[:, m % 4], ab[:, m % 2], ACT.Copy).then_inc(q_hi, 1)
                    if on(L_MAX):
                        j, m, g, b, half, past = place(it, k, L_MAX)
                        act.wait_ge(c_shift, j + 1)
                        act.activation(ec[:], ec[:], ACT.Exp).then_inc(c_exp, 1)
                    if on(L_BACK):
                        j, m, g, b, half, past = place(it, k, L_BACK)
                        act.wait_ge(pt_ready, j + 1)
                        if past(2):
                            act.wait_ge(pc_stored[m % 2], 16 * (4 * it + (k - L_BACK) // 2))
                        act.activation(pc[:, m % 2], ps[0:D, 7, :], ACT.Copy).then_inc(pc_out, 1)
                steps(act, step)

            @blk.vector
            def _(dve):
                ch = Chain(dve, c_chain)

                def step(it, k, on):
                    if on(0) and k % 4 == 0:
                        j, m, g, b, half, past = place(it, k, 0)
                        dve.wait_ge(wqh_done, g + 1)
                        for kt in range(KT):
                            ins = dve.tensor_tensor(wq[1][:, k // 4, kt].rearrange("p e (h i) -> p e h i", h=REP), w_view(g, kt),
                                                    f32(wq[0][:, k // 4, kt]).rearrange("p e (h i) -> p e h i", h=REP), ALU.subtract)
                        ins.then_inc(wql_done, 1)
                    if on(L_PROB):
                        j, m, g, b, half, past = place(it, k, L_PROB)
                        dve.wait_ge(c_exp, j + 1)
                        ch.n, ch.base = 0, 3 * j
                        ch.link(dve.tensor_reduce(mc[:, 1, :], ec[:], X, ALU.add))
                        ch.link(dve.reciprocal(mc[:, 2, :], mc[:, 1, :]))
                        gc = gate_c[:, TJ * b + 4 * half:TJ * b + 4 * half + 4].unsqueeze(2).broadcast_to([P, 4, REP])
                        ch.link(dve.tensor_tensor(mc[:, 1, :].rearrange("p (t h) -> p t h", t=4),
                                                  mc[:, 2, :].rearrange("p (t h) -> p t h", t=4), gc, ALU.mult))
                        if past(2):
                            dve.wait_ge(pt_ready, j - 1)
                        dve.tensor_tensor(prob_c[:, m % 2, :, 0:D].rearrange("p t (h n) -> p t h n", h=REP),
                                          ec[:].rearrange("p (t h) n -> p t h n", t=4),
                                          mc[:, 1, :].rearrange("p (t h) -> p t h", t=4).unsqueeze(3).broadcast_to([P, 4, REP, NBLK]),
                                          ALU.mult).then_inc(c_prob, 1)
                    if on(0):
                        j, m, g, b, half, past = place(it, k, 0)
                        dve.wait_ge(q_ready, j + 1)
                        if past(2):
                            dve.wait_ge(q_sum, j - 1)
                        for e in range(2):
                            ins = dve.tensor_tensor(tu[:, k % 2, e], ps[:, 2 * (k % 2) + e, :].unsqueeze(1).broadcast_to([P, 2, CH]),
                                                    rot[:, e, :, half * CH:(half + 1) * CH], ALU.mult)
                        ins.then_inc(q_rot, 1)
                    if on(L_MAX):
                        j, m, g, b, half, past = place(it, k, L_MAX)
                        dve.wait_ge(lt_ready, j + 1)
                        lt = ps[:, 6, :].rearrange("p (t r h n) -> p t r h n", t=4, r=2, h=REP)[:, :, 0]
                        nm = mc[:, 0, :].rearrange("p (t h) -> p t h", t=4)
                        dve.tensor_reduce(nm, lt, X, ALU.max, negate=True).then_inc(c_max, 1)
                        dve.wait_ge(c_max, j + 1)
                        if past(1):
                            dve.wait_ge(c_prob, j)
                        dve.tensor_tensor(ec[:].rearrange("p (t h) n -> p t h n", t=4), lt,
                                          nm.unsqueeze(3).broadcast_to([P, 4, REP, NBLK]), ALU.add).then_inc(c_shift, 1)
                    if on(L_SPLIT):
                        j, m, g, b, half, past = place(it, k, L_SPLIT)
                        dve.wait_ge(q_hi, j + 1)
                        buffer_free(dve, j, m, 2 * it + (k - L_SPLIT) // 4, past)
                        dve.tensor_tensor(ql[:, m % 4], ab[:, m % 2], f32(qh[:, m % 4]), ALU.subtract).then_inc(q_lo, 1)
                steps(dve, step)

    def attention_phase():
        NP = 4 * HKV
        NQ = TJ
        with ExitStack() as c:
            qa = sb("qa", [P, 4, 2, T], F32R, c)
            qb = sb("qb", [P, 2, 2, 2, T], F32R, c)
            k_hh = sb("k_hh", [P, B, T], F32R, c)
            k_ll = sb("k_ll", [P, B, T], F32R, c)
            k_l1 = sb("k_l1", [P, B, T], F32R, c)
            v_s = sb("v_s", [P, B, TJ, D], F32, c)
            pct = sb("pct", [P, T], F32, c)
            vcp = sb("vcp", [P, 4, P], F32, c)
            prob = sb("prob", [P, 2, 2, T], F32, c)
            prob_w = sb("prob_w", [P, 2, 2, WW], F32, c)
            wl = sb("wl", [P, 2, TJ, WW], F32, c)
            junk = sb("junk", [P, T], BF16, c)
            nmax = sb("nmax", [P, 2, 2 * TJ], F32, c)
            sums = sb("sums", [P, 2, 2 * TJ], F32, c)
            lns = sb("lns", [P, 2, 2 * TJ], F32, c)
            shift = sb("shift", [P, 2, 2, 2 * TJ], F32, c)
            shift_r = sb("shift_r", [P, P // (4 * TJ), 2, 2 * TJ], F32R, c)
            o_t = sb("o_t", [P, 2, T], F32, c)
            mask_a = sb("mask_a_sb", [P, WW], F32, c)
            mask_b = sb("mask_b_sb", [P, WW], F32, c)
            mask_bh = sb("mask_bh", [P, WW], BF16, c)
            ident_h = sb("ident_h", [P, P], BF16, c)
            pick = sb("pick_sb", [D, 4, TJ], F32, c)
            const_in = sem("m_const_in", c)
            const_ok = sem("m_const_ok", c)
            ones_ok = sem("ones_ok", c)
            qa_in = [sem(f"qa_in{n}", c) for n in range(4)]
            qb_in = [sem(f"qb_in{n}", c) for n in range(2)]
            k_in = [sem(f"k_in{n}", c) for n in range(2)]
            pc_in = sem("pc_in", c)
            v_ok = sem("v_ok", c)
            a_ready = sem("a_ready", c)
            b_ready = sem("b_ready", c)
            w_ready = sem("w_ready5", c)
            t_ready = sem("t_ready", c)
            pv_done = sem("pv_done", c)
            a_exp = sem("a_exp", c)
            b_exp = sem("b_exp", c)
            wb_exp = sem("wb_exp", c)
            w_exp = sem("w_exp", c)
            ln_done = sem("ln_done", c)
            o_out = sem("o_out", c)
            a_max = sem("a_max", c)
            a_win = sem("a_win", c)
            w_max = sem("w_max", c)
            w_shift = sem("w_shift", c)
            w_sum = sem("w_sum", c)
            m_chain = sem("m_chain", c)
            st_ready = sem("st_ready", c)
            aug_done = sem("aug_done", c)
            o_stored = [sem(f"o_stored{n}", c) for n in range(2)]
            blk = c.enter_context(nc.Block())
            OB = 6

            def stages(stage):
                def run(eng):
                    stage(-1, 3, False, True)
                    for u in range(4):
                        stage(0, u, True, True)
                    with eng.Fori(1, HKV - 1) as it:
                        for u in range(4):
                            stage(it, u, True, True)
                    for u in range(4):
                        stage(HKV - 1, u, True, u < 3)
                return run

            def early(it, u, n):
                return isinstance(it, int) and 4 * it + u < n

            def after(it, u, n=1):
                return it + (u + n) // 4, (u + n) % 4

            PE_ORDER = ("B0 B1 A A A V0 W W B0 A B1 A V1 B0 A A V0 B1 A V1 B0 W A A V0 A A A V1 B1 A B0 A V0 W A B1 W V1  "
                        "B0 W V0 B1 B0 V1 B1 W V0 W V1 B0 V0 B1 T V1 V0 V1").split()
            ACT_ORDER = ("B0 B1 O A A A W W B0 B1 A A B0 A B1 A A B0 W A A A A A B1 B0 A A W A B1 W B0 X0 X1 W B1 B0 B1 W  "
                        "L W B0 B1").split()
            DVE_ORDER = ("A A A A A A A A M A A A A A A A A M S S C G G G G").split()

            def jobs(order, b_on, a_on):
                of_b = ("B0", "B1", "W", "V0", "V1", "O")
                seen, seq = {}, []
                for what in order:
                    if b_on if what in of_b else a_on:
                        seq.append((what, seen.setdefault(what, 0)))
                        seen[what] += 1
                return seq

            @blk.sync
            def _(sp):
                sp.dma_start(mask_a[:], a["mask_a"]).then_inc(const_in, 16)
                sp.dma_start(mask_b[:], a["mask_b"]).then_inc(const_in, 16)
                sp.dma_start(pick[:], a["pick"]).then_inc(const_in, 16)

                def load_k(g, b):
                    def rows(part):
                        src = k_scr[bass.ds(g // 4, 1), b, part, :, bass.ds(32 * (g % 4), 32), :]
                        return src.rearrange("g e i t -> (g e) i t")
                    for dst, part in ((k_hh[0:D, b], 0), (k_hh[D:P, b], 0), (k_ll[0:D, b], 1), (k_ll[D:P, b], 1), (k_l1[0:D, b], 1)):
                        sp.dma_start(f32(dst), rows(part)).then_inc(k_in[b], 16)

                def load_qa(it, u):
                    for h in range(2):
                        r = 32 * (2 * (u % 2) + h)
                        src = q_scr[bass.ds(it, 1), u // 2, :, :, r:r + 32, :].rearrange("g l e i t -> (g l e) i t")
                        sp.dma_start(f32(qa[:, u, h]), src).then_inc(qa_in[u], 16)

                def load_qb(it, u):
                    for br in range(2):
                        for h in range(2):
                            r = 32 * (2 * (u % 2) + h)
                            src = q_scr[bass.ds(it, 1), u // 2, 0, :, r:r + 32, :].rearrange("g e i t -> (g e) i t")
                            sp.dma_start(f32(qb[0:D, u % 2, br, h]), src).then_inc(qb_in[u % 2], 16)

                def load_pc(it):
                    sp.dma_start(pct[:], pc_scr[bass.ds(it, 1)].rearrange("g p t -> (g p) t")).then_inc(pc_in, 16)
                    vc = vc_scr.rearrange("m p d -> (m p) d")
                    for b in range(B):
                        for h in range(REP):
                            r = D * b + NBLK * h
                            sp.dma_start(vcp[r:r + NBLK, 2 * b + h // 2, D * (h % 2):D * (h % 2) + D],
                                         vc[bass.ds((2 * it + b) * NBLK, NBLK), :]).then_inc(pc_in, 16)

                def stage(it, u, b_on, a_on):
                    if not b_on:
                        load_k(0, 0)
                        load_qa(0, 0)
                        load_qb(0, 0)
                        load_qa(0, 1)
                        load_k(0, 1)
                        sp.wait_ge(ones_ok, 3)
                        load_pc(0)
                        load_qb(0, 1)
                        sp.dma_start(wo_raw[:], a["L0_attn_W_o"].rearrange("(k p) n -> p k n", p=P)).then_inc(wo_in, 16)
                        return
                    pr = 4 * it + u
                    last = isinstance(it, int) and it == HKV - 1
                    if u == 0 and not early(it, u, 1):
                        sp.wait_ge(pv_done, 8 * pr)
                        load_k(it, 1)
                    if u == 2 and not last:
                        sp.wait_ge(pv_done, 8 * pr)
                        load_k(it + 1, 0)
                    if not (last and u >= 2):
                        if not early(it, u, 2):
                            sp.wait_ge(pv_done, 8 * (pr - 1))
                        load_qa(*after(it, u, 2))
                    if not early(it, u, 1):
                        store_o(*after(it, u, -1))
                    if u == 3 and not last:
                        sp.wait_ge(pv_done, 8 * pr + 1)
                        load_pc(it + 1)
                    if not (last and u >= 2):
                        sp.wait_ge(pv_done, 8 * (pr + 1))
                        load_qb(*after(it, u, 2))

                def store_o(it, u):
                    sp.wait_ge(o_out, 4 * it + u + 1)
                    b, row = u // 2, (u % 2) * P
                    sp.dma_start(o_scr[b, bass.ds(it * (REP * D) + row, P), :], o_t[:, u % 2]).then_inc(o_stored[u % 2], 16)

                stages(stage)(sp)
                store_o(HKV - 1, 3)
                for n in range(2):
                    sp.wait_ge(o_stored[n], 16 * NP // 2)

            @blk.tensor
            def _(pe):
                pe.wait_ge(ones_ok, 3)
                pe.wait_ge(const_ok, 1)
                ring = {"n": 0, "used": [None] * 3}

                def slot(*used):
                    n = ring["n"] % 3
                    if ring["used"][n] is not None:
                        for s_, f_ in ring["used"][n]:
                            pe.wait_ge(s_, f_)
                    ring["used"][n] = used
                    ring["n"] += 1
                    return 2 * n

                def stage(it, u, b_on, a_on):
                    pr = 4 * it + u
                    ita, ua = after(it, u)
                    x = 4 * ita + ua
                    b, ba = u // 2, ua // 2

                    def job_a(n):
                        h, j = n // TJ, n % TJ
                        if n == 0:
                            pe.wait_ge(qa_in[ua], 32 * (ita + 1))
                            pe.wait_ge(k_in[ba], 80 * (ita + 1))
                        s0 = slot((a_exp, 16 * x + n + 1))
                        lhs = qa[:, ua, h, j * P:(j + 1) * P]
                        for half in range(2):
                            cols = slice(half * CH, (half + 1) * CH)
                            pe.matmul(ps[:, s0 + half, :], lhs, k_hh[:, ba, cols], start=True, stop=False)
                            ins = pe.matmul(ps[:, s0 + half, :], lhs, k_ll[:, ba, cols], start=False, stop=True)
                        ins.then_inc(a_ready, 1)

                    def job_b(cc, h):
                        if cc == 0:
                            if h == 0:
                                pe.wait_ge(qb_in[u % 2], 64 * (2 * it + u // 2 + 1))
                            pe.wait_ge(aug_done, 4 * pr + h + 1)
                        s0 = slot((b_exp, 16 * pr + 2 * cc + h + 1))
                        ks = slice(cc * P, (cc + 1) * P)
                        for half in range(2):
                            cols = slice(half * CH, (half + 1) * CH)
                            pe.matmul(ps[:, s0 + half, :], k_hh[:, b, ks], qa[:, u, h, cols], start=True, stop=False)
                            ins = pe.matmul(ps[:, s0 + half, :], k_l1[:, b, ks], qb[:, u % 2, 0, h, cols], start=False, stop=True)
                        ins.then_inc(b_ready, 1)

                    def job_w(cc):
                        if cc == 0:
                            pe.wait_ge(aug_done, 4 * pr + 4)
                        n = min(WW, T - cc * P)
                        s0 = slot((wb_exp, 8 * pr + cc + 1))
                        ks, ts = slice(cc * P, (cc + 1) * P), slice(cc * P, cc * P + n)
                        dst = ps[:, s0, 0:2 * n].rearrange("p (h n) -> p h n", h=2)
                        pe.matmul(dst, k_hh[:, b, ks], qa[:, u, :, ts], start=True, stop=False)
                        pe.matmul(dst, k_l1[:, b, ks], qb[:, u % 2, 1, :, ts], start=False, stop=False)
                        pe.matmul(dst, ident_h[:], mask_bh[:, 0:n].unsqueeze(1).broadcast_to([P, 2, n]), start=False, stop=True)\
                            .then_inc(w_ready, 1)

                    def job_t():
                        s0 = slot((aug_done, 4 * x + 4))
                        ring["n"] += 1
                        pe.wait_ge(st_ready, x + 1)
                        pe.transpose(ps[:, s0, 0:P], f32(shift_r[:]).rearrange("p l r n -> p (l r n)"), ident[:]).then_inc(t_ready, 1)

                    def job_v(cc, half):
                        if cc == 0 and half == 0:
                            pe.wait_ge(pc_in, 144 * (it + 1))
                            pe.wait_ge(v_ok, 2 * it + b + 1)
                            if not early(it, u, 1):
                                pe.wait_ge(o_out, pr)
                            for hf in range(2):
                                pe.matmul(ps[:, OB + hf, :], vcp[:, u, :], pct[:, hf * CH:(hf + 1) * CH],
                                          start=True, stop=False, skip_group_check=True)
                        lastc = cc == TJ - 1
                        v = v_s[:, b, cc, :]
                        if half == 0:
                            pe.wait_ge(b_exp, 16 * pr + 2 * cc + 2)
                        for h in range(2):
                            pe.matmul(ps[D * h:D * h + D, OB + half, :], v, prob[:, cc % 2, h, half * CH:(half + 1) * CH],
                                      start=False, stop=lastc and half == 0, skip_group_check=True)
                        if half == 0:
                            return
                        pe.wait_ge(wb_exp, 8 * pr + cc + 1)
                        n = min(WW, T - cc * P)
                        for t0, t1 in ([(0, P), (P, WW)] if cc == 3 else [(0, n)]):
                            t = cc * P + t0
                            for h in range(2):
                                ins = pe.matmul(ps[D * h:D * h + D, OB + t // CH, t % CH:t % CH + t1 - t0], v,
                                                prob_w[:, cc % 2, h, t0:t1], start=False, stop=lastc, skip_group_check=True)
                        ins.then_inc(pv_done, 1)

                    for what, n in jobs(PE_ORDER, b_on, a_on):
                        if what == "A":
                            job_a(n)
                        elif what[0] == "B":
                            job_b(n, int(what[1]))
                        elif what == "W":
                            job_w(n)
                        elif what == "T":
                            job_t()
                        else:
                            job_v(n, int(what[1]))

                stage(-1, 3, False, True)
                ring["n"] += -ring["n"] % 3
                for u in range(4):
                    stage(0, u, True, True)
                assert (ring["n"]) % 3 == 0
                with pe.Fori(1, HKV - 1) as it:
                    def moved(entry, by):
                        return [(s_, f_ + (it - 1) * by[s_.name]) for s_, f_ in entry]
                    per = {a_exp.name: 64, b_exp.name: 64, wb_exp.name: 32, aug_done.name: 16}
                    ring["used"] = [moved(e, per) for e in ring["used"]]
                    for u in range(4):
                        stage(it, u, True, True)
                total = {a_exp.name: 64 * (HKV - 1) + 16, b_exp.name: 64 * (HKV - 1),
                         wb_exp.name: 32 * (HKV - 1), aug_done.name: 16 * (HKV - 1) + 4}
                ring["used"] = [[(s_, total[s_.name]) for s_, _ in e] for e in ring["used"]]
                for u in range(4):
                    stage(HKV - 1, u, True, u < 3)

            def slots_of(b_on, a_on, n0):
                out, n = {}, n0
                for what, k in jobs(PE_ORDER, b_on, a_on):
                    if what[0] != "V":
                        out[(what, k)] = 2 * (n % 3)
                        n += 1 + (what == "T")
                return out, n

            slot_maps = [slots_of(False, True, 0)[0]]
            n_ = 0
            for u_ in range(4):
                m_, n_ = slots_of(True, True, n_)
                slot_maps.append(m_)
            last3 = slots_of(True, False, slots_of(True, True, slots_of(True, True, slots_of(True, True, 0)[1])[1])[1])[0]

            def slot_map(u, b_on, a_on):
                return slot_maps[0] if not b_on else slot_maps[1 + u] if a_on else last3

            @blk.scalar
            def _(act):
                act.wait_ge(const_in, 48)
                act.activation(mask_bh[:], mask_b[:], ACT.Copy)
                act.activation(ident_h[:], ident[:], ACT.Copy).then_inc(const_ok, 1)

                def stage(it, u, b_on, a_on):
                    pr = 4 * it + u
                    ita, ua = after(it, u)
                    x = 4 * ita + ua
                    first_a = isinstance(it, int) and x == 0
                    where = slot_map(u, b_on, a_on)
                    for what, n in jobs(ACT_ORDER, b_on, a_on):
                        if what == "A":
                            s0 = where[("A", n)]
                            act.wait_ge(a_win, 16 * x + n + 1)
                            if n == 0 and not first_a:
                                act.wait_ge(ln_done, x)
                            src = ps[:, s0:s0 + 2, :].rearrange("p a n -> p (a n)")
                            if n or not first_a:
                                act.wait_ge(a_exp, 16 * x + n)
                            act.activation(junk[:], src, ACT.Exp, bias=nmax[:, 0, n:n + 1],
                                           accum_out=sums[:, 0, n:n + 1]).then_inc(a_exp, 1)
                        elif what[0] == "B":
                            h = int(what[1])
                            s0 = where[(what, n)]
                            act.wait_ge(b_ready, 16 * pr + 2 * n + h + 1)
                            if not early(it, u, 1) or n >= 2:
                                act.wait_ge(pv_done, 8 * pr + n - 1)
                            act.activation(prob[:, n % 2, h], ps[:, s0:s0 + 2, :].rearrange("p a n -> p (a n)"), ACT.Exp)\
                                .then_inc(b_exp, 1)
                        elif what == "W":
                            s0 = where[("W", n)]
                            w = min(WW, T - n * P)
                            act.wait_ge(w_ready, 8 * pr + n + 1)
                            if not early(it, u, 1) or n >= 2:
                                act.wait_ge(pv_done, 8 * pr + n - 1)
                            act.activation(prob_w[:, n % 2, :, 0:w], ps[:, s0, 0:2 * w].rearrange("p (h n) -> p h n", h=2), ACT.Exp)\
                                .then_inc(wb_exp, 1)
                        elif what[0] == "X":
                            h = int(what[1])
                            act.wait_ge(w_shift, 2 * x + h + 1)
                            act.activation(wl[:, h], wl[:, h], ACT.Exp).then_inc(w_exp, 1)
                        elif what == "L":
                            act.wait_ge(w_sum, 2 * x + 2)
                            act.wait_ge(a_exp, 16 * x + 16)
                            if not first_a:
                                act.wait_ge(st_ready, x)
                            act.activation(lns[:], sums[:], ACT.Ln).then_inc(ln_done, 1)
                        elif not early(it, u, 1):
                            out_o(*after(it, u, -1))

                def out_o(it, u):
                    pr = 4 * it + u
                    act.wait_ge(pv_done, 8 * pr + 8)
                    if not early(it, u, 2):
                        act.wait_ge(o_stored[u % 2], 16 * (2 * it + u // 2))
                    act.activation(o_t[:, u % 2].rearrange("p (a n) -> p a n", a=2), ps[:, OB:OB + 2, :], ACT.Copy).then_inc(o_out, 1)

                stages(stage)(act)
                out_o(HKV - 1, 3)

            @blk.gpsimd
            def _(pool):
                pool.memset(f32(k_l1[D:P]), 1.0).then_inc(ones_ok, 1)
                pool.wait_ge(ones_ok, 1)
                pool.memset(f32(shift_r[:, 2:]), 0.0).then_inc(ones_ok, 1)
                pool.memset(vcp[:], 0.0).then_inc(ones_ok, 1)

                def copy_v(g, b):
                    pool.tensor_copy(v_s[:, b], v_all[:, TJ * b:TJ * b + TJ, bass.ds(g * D, D)]).then_inc(v_ok, 1)

                def stage(it, u, b_on, a_on):
                    ita, ua = after(it, u)
                    x = 4 * ita + ua
                    if a_on:
                        for h in range(2):
                            pool.wait_ge(w_max, 2 * x + h + 1)
                            nm = nmax[:, 1, TJ * h:TJ * h + TJ].unsqueeze(2).broadcast_to([P, TJ, WW])
                            pool.tensor_tensor(wl[:, h], wl[:, h], nm, ALU.add).then_inc(w_shift, 1)
                    if not b_on:
                        copy_v(0, 0)
                        copy_v(0, 1)
                    elif u == 0 and not early(it, u, 1):
                        pool.wait_ge(pv_done, 8 * (4 * it))
                        copy_v(it, 1)
                    elif u == 2 and not (isinstance(it, int) and it == HKV - 1):
                        pool.wait_ge(pv_done, 8 * (4 * it + 2))
                        copy_v(it + 1, 0)
                stages(stage)(pool)

            @blk.vector
            def _(dve):
                ch = Chain(dve, m_chain)
                dve.wait_ge(const_in, 48)

                def stage(it, u, b_on, a_on):
                    if not a_on:
                        return
                    ita, ua = after(it, u)
                    x = 4 * ita + ua
                    first_a = isinstance(it, int) and x == 0
                    ba = ua // 2
                    where = slot_map(u, b_on, a_on)

                    def job_a(n):
                        h, j = n // TJ, n % TJ
                        s0 = where[("A", n)]
                        if j == 0:
                            if not first_a:
                                dve.wait_ge(w_sum, 2 * (x - 1) + h + 1)
                                dve.wait_ge(st_ready, x)
                            dve.memset(wl[:, h, 0, 0:WIN], NEG)
                        dve.wait_ge(a_ready, 16 * x + n + 1)
                        src = ps[:, s0:s0 + 2, :].rearrange("p a n -> p (a n)")
                        dve.tensor_reduce(nmax[:, 0, n:n + 1], src, X, ALU.max, negate=True).then_inc(a_max, 1)
                        lo = WIN if j == 0 else 0
                        dve.tensor_tensor(wl[:, h, j, lo:WW], src[:, P * j - WIN + lo:P * j + P], mask_a[:, lo:WW], ALU.add)\
                            .then_inc(a_win, 1)

                    def win_max(h):
                        dve.wait_ge(a_win, 16 * x + TJ * h + TJ)
                        dve.tensor_reduce(nmax[:, 1, TJ * h:TJ * h + TJ], wl[:, h], X, ALU.max, negate=True).then_inc(w_max, 1)

                    def win_sum(h):
                        dve.wait_ge(w_exp, 2 * x + h + 1)
                        dve.tensor_reduce(sums[:, 1, TJ * h:TJ * h + TJ], wl[:, h], X, ALU.add).then_inc(w_sum, 1)

                    def shifts():
                        dve.wait_ge(ln_done, x + 1)
                        ch.n, ch.base = 0, 3 * x
                        ch.link(dve.tensor_tensor(shift[:, 0], nmax[:], lns[:], ALU.subtract))
                        lg = ln_gate[:, :, TJ * ba:TJ * ba + TJ].unsqueeze(2).broadcast_to([P, 2, 2, TJ])
                        ch.link(dve.tensor_tensor(shift[:, 1].rearrange("p r (h j) -> p r h j", h=2),
                                                  shift[:, 0].rearrange("p r (h j) -> p r h j", h=2), lg, ALU.add))
                        ch.link(dve.tensor_copy(shift_r[:, 0], shift[:, 1]))
                        dve.tensor_tensor(shift_r[:, 1], shift[:, 1], f32(shift_r[:, 0]), ALU.subtract).then_inc(st_ready, 1)

                    def aug(n):
                        if n == 0:
                            dve.wait_ge(t_ready, x + 1)
                            if not early(ita, ua, 2):
                                dve.wait_ge(pv_done, 8 * (x - 1))
                        s0 = where[("T", 0)]
                        dst = qb[D:P, ua % 2, n // 2, n % 2].rearrange("p (j n) -> p j n", j=TJ)
                        dve.tensor_tensor(dst, ps[0:D, s0, 0:P].unsqueeze(1).broadcast_to([D, TJ, P]),
                                          pick[:, n, :].unsqueeze(2).broadcast_to([D, TJ, P]), ALU.mult)\
                            .then_inc(aug_done, 1)

                    for what, n in jobs(DVE_ORDER, b_on, a_on):
                        {"A": job_a, "M": win_max, "S": win_sum, "C": lambda _: shifts(), "G": aug}[what](n)
                stages(stage)(dve)

    def out_phase():
        NH = H * D // P
        with ExitStack() as c:
            raw = wo_raw
            wh = sb("woh", [P, NH, DM], F32R, c)
            wl_ = sb("wol", [P, NH, DM], F32R, c)
            o = sb("o", [P, 4, CH], F32, c)
            oh = sb("oh", [P, 4, CH], F32R, c)
            ol = sb("ol", [P, 4, CH], F32R, c)
            xr = sb("xr", [P, 2, 4, DM], F32, c)
            y = sb("y", [P, 2, CH], F32, c)
            yo = sb("yo", [P, 2, 4, DM], F32, c)
            o_in = [sem(f"o_in{n}", c) for n in range(4)]
            xr_in = [sem(f"xr_in{n}", c) for n in range(2)]
            woh_done = sem("woh_done", c)
            wol_done = sem("wol_done", c)
            oh_done = sem("oh_done", c)
            ol_done = sem("ol_done", c)
            s_part = sem("s_part", c)
            y_done = sem("y_done", c)
            y_turned = sem("y_turned", c)
            yo_done = sem("yo_done", c)
            stored = [sem(f"stored{n}", c) for n in range(2)]
            blk = c.enter_context(nc.Block())
            out_tok = out.rearrange("b (n p) d -> p (b n) d", p=P)

            @blk.sync
            def _(sp):
                for tc in range(NC):
                    for n in range(NH):
                        k = tc * NH + n
                        if k >= 4:
                            sp.wait_ge(ol_done, k - 3)
                        sp.dma_start(o[:, n % 4], o_scr[tc // 2, n * P:(n + 1) * P, (tc % 2) * CH:(tc % 2) * CH + CH]).then_inc(o_in[n % 4], 16)
                        if n == 0:
                            if tc >= 2:
                                sp.wait_ge(yo_done, tc - 1)
                            sp.dma_start(xr[:, tc % 2], x_tok[:, 4 * tc:4 * tc + 4, :]).then_inc(xr_in[tc % 2], 16)
                        if n == 13 and tc:
                            sp.wait_ge(yo_done, tc)
                            sp.dma_start(out_tok[:, 4 * tc - 4:4 * tc, :], yo[:, (tc - 1) % 2]).then_inc(stored[(tc - 1) % 2], 16)
                sp.wait_ge(yo_done, NC)
                sp.dma_start(out_tok[:, 4 * NC - 4:4 * NC, :], yo[:, (NC - 1) % 2]).then_inc(stored[(NC - 1) % 2], 16)
                for n in range(2):
                    sp.wait_ge(stored[n], 16 * NC // 2)

            @blk.tensor
            def _(pe):
                pe.wait_ge(wol_done, 1)

                def turn(tc):
                    pe.wait_ge(y_done, tc + 1)
                    for t in range(4):
                        for ht in range(2):
                            ins = pe.transpose(ps[:, 4 + t // 2, (2 * (t % 2) + ht) * P:(2 * (t % 2) + ht + 1) * P],
                                               y[:, ht, t * P:(t + 1) * P], ident[:])
                    ins.then_inc(y_turned, 1)
                for tc in range(NC):
                    if tc >= 2:
                        pe.wait_ge(y_done, tc - 1)
                    for n in range(NH):
                        pe.wait_ge(ol_done, tc * NH + n + 1)
                        for ht in range(2):
                            hs = slice(ht * P, (ht + 1) * P)
                            prods = three(0, wh[:, n, hs], wl_[:, n, hs], oh[:, n % 4], ol[:, n % 4])
                            for k, (w, x) in enumerate(prods):
                                ins = pe.matmul(ps[:, 2 * (tc % 2) + ht, :], w, x, start=(n == 0 and k == 0),
                                                stop=(n == NH - 1 and k == 2))
                        ins.then_inc(s_part, 1)
                        if n == 4 and tc:
                            turn(tc - 1)
                turn(NC - 1)

            @blk.scalar
            def _(act):
                act.wait_ge(wo_in, 16)
                act.activation(wh[:], raw[:], ACT.Copy).then_inc(woh_done, 1)
                for k in range(NC * NH):
                    act.wait_ge(o_in[k % 4], 16 * (k // 4 + 1))
                    if k >= 4:
                        act.wait_ge(s_part, k - 3)
                    act.activation(oh[:, k % 4], o[:, k % 4], ACT.Copy).then_inc(oh_done, 1)

            @blk.vector
            def _(dve):
                dve.wait_ge(woh_done, 1)
                dve.tensor_tensor(wl_[:], raw[:], f32(wh[:]), ALU.subtract).then_inc(wol_done, 1)

                def finish(tc):
                    dve.wait_ge(y_turned, tc + 1)
                    dve.wait_ge(xr_in[tc % 2], 16 * (tc // 2 + 1))
                    if tc >= 2:
                        dve.wait_ge(stored[tc % 2], 16 * (tc // 2))
                    yt = ps[:, 4:6, :].rearrange("p a (t d) -> p (a t) d", d=DM)
                    dve.tensor_tensor(yo[:, tc % 2], yt, xr[:, tc % 2], ALU.add).then_inc(yo_done, 1)
                for tc in range(NC):
                    for n in range(NH):
                        k = tc * NH + n
                        dve.wait_ge(oh_done, k + 1)
                        dve.tensor_tensor(ol[:, k % 4], o[:, k % 4], f32(oh[:, k % 4]), ALU.subtract).then_inc(ol_done, 1)
                        if n == 8 and tc:
                            finish(tc - 1)
                    dve.wait_ge(s_part, (tc + 1) * NH)
                    if tc:
                        dve.wait_ge(y_turned, tc)
                    dve.tensor_tensor(y[:], ps[:, 2 * (tc % 2):2 * (tc % 2) + 2, :], g_t[:, :, tc * CH:(tc + 1) * CH], ALU.mult)\
                        .then_inc(y_done, 1)
                finish(NC - 1)

    with ExitStack() as mlp:
        hi = [mlp.enter_context(nc.sbuf_tensor(f"w_hi{m}", [P, F * DM // P // P, P], F32R)) for m in range(3)]
        lo = [mlp.enter_context(nc.sbuf_tensor(f"w_lo{m}", [P, F * DM // P // P, P], F32R)) for m in range(3)]
        norm_and_weights(hi, lo)
        if stop == 2 or stop > 6:
            mlp_phase(hi, lo)
    if stop >= 3:
        kv_phase()
    if stop >= 4:
        compress_phase()
    if stop >= 5:
        query_phase()
    dense.close()
    wo_raw = sb("wo_raw", [P, H * D // P, DM], F32)
    wo_in = sem("wo_in")
    if stop >= 6:
        attention_phase()
    if stop >= 7:
        out_phase()
    g = dict(locals())
    return g


def constants():
    inv = 1.0 / 10000.0 ** (np.arange(0, D, 2, dtype=np.float32) / D)
    ang = np.outer(np.arange(T, dtype=np.float32), inv).T
    cos, sin = np.tile(np.cos(ang), (4, 1)), np.tile(np.sin(ang), (4, 1))
    rot = np.stack([np.stack([cos, sin], 1), np.stack([-sin, cos], 1)], 1).astype(np.float32)
    row = np.arange(P)[:, None]
    col = np.arange(WW)[None]
    mask_a = np.where((col > row) & (col <= row + WIN), 0.0, NEG).astype(np.float32)
    mask_b = np.where((col >= row) & (col < row + WIN), 0.0, NEG).astype(np.float32)
    pick = np.tile(np.eye(4 * TJ, dtype=np.float32).reshape(4 * TJ, 4, TJ), (2, 1, 1))
    return {"mask_a": mask_a, "mask_b": mask_b, "pick": pick, "ident": np.eye(P, dtype=np.float32), "rot_k": rot, "rot_q": rot * np.float32(0.125)}


_INS = ['L0_attn_x', 'L0_attn_W_q', 'L0_attn_W_k', 'L0_attn_W_v', 'L0_attn_W_o', 'L0_attn_W_ck', 'L0_attn_W_cv',
        'L0_attn_W_gate', 'L0_ffn_gate_W_packed', 'L0_ffn_gate_scales', 'L0_ffn_up_W_packed',
        'L0_ffn_up_scales', 'L0_ffn_down_W_packed', 'L0_ffn_down_scales']


def kernel(**inputs):
    import numpy as _np
    import concourse.bacc as _bacc
    from concourse import mybir as _mybir
    from concourse.bass_utils import run_bass_kernel_spmd as _run

    nc = _bacc.Bacc("TRN2", target_bir_lowering=False, num_devices=1)
    arrays = {name: _np.ascontiguousarray(inputs[name]) for name in _INS}
    arrays.update(constants())
    args = {n: nc.dram_tensor(f"in_{n}", v.shape, _mybir.dt.from_np(v.dtype), kind="ExternalInput").ap()
            for n, v in arrays.items()}
    out = nc.dram_tensor("out_0", (B, T, DM), F32, kind="ExternalOutput").ap()
    build(nc, args, out)
    r = _run(nc, [{f"in_{n}": v for n, v in arrays.items()}], core_ids=[0])
    return r.results[0]["out_0"]
```

```python
from contextlib import ExitStack

import numpy as np
import concourse.bass as bass
from concourse import mybir

ALU = mybir.AluOpType
ACT = mybir.ActivationFunctionType
X = mybir.AxisListType.X
F32 = mybir.dt.float32
F32R = mybir.dt.float32r
BF16 = mybir.dt.bfloat16
I32 = mybir.dt.int32
I16 = mybir.dt.int16

P = 128
B, T, DM = 2, 1024, 256
H, HKV, D = 32, 8, 64
REP = H // HKV
BS = 64
NBLK = T // BS
WIN = 64
F = 2048
QB = 32
KT = DM // P
NTOK = B * T
TB = NTOK // P
TJ = T // P
CH = 512
NC = NTOK // CH
WW = P + WIN
NEG = -1.0e30
EPS = 1e-5


class Chain:

    def __init__(self, eng, sem):
        self.eng, self.sem, self.n, self.base = eng, sem, 0, 0

    def link(self, ins):
        ins.then_inc(self.sem, 1)
        self.n += 1
        self.eng.wait_ge(self.sem, self.base + self.n)


def f32(ap):
    return ap.bitcast(F32)


def build(nc, a, out):
    main = ExitStack()

    def dram(name, shape, dt):
        return nc.dram_tensor(name, shape, dt).ap()

    q_scr = dram("q_scr", [HKV, B, 2, 2, P, T], F32)
    k_scr = dram("k_scr", [2, B, 2, 2, P, T], F32)
    pc_scr = dram("pc_scr", [HKV, P, T], F32)
    vc_scr = dram("vc_scr", [2, P, D], F32)
    o_scr = dram("o_scr", [B, H * D, T], F32)

    def sb(name, shape, dt, ctx=main):
        return ctx.enter_context(nc.sbuf_tensor(name, shape, dt))

    def sem(name, ctx=main):
        return ctx.enter_context(nc.semaphore(name))

    ps = main.enter_context(nc.psum_tensor("ps", [P, 8, CH], F32))
    ident = sb("ident_sb", [P, P], F32)
    gate_c = sb("gate_c", [P, TB], F32)
    ln_gate = sb("ln_gate", [P, 2, TB], F32)
    v_all = sb("v_all", [P, TB, HKV * D], F32)
    g_t = sb("g_t", [P, 2, NTOK], F32)
    dense = ExitStack()
    kc_all = sb("kc_all", [P, 2, 2, NBLK * B * HKV], F32R, dense)
    xh = sb("xh", [P, KT, NTOK], F32R, dense)
    xl = sb("xl", [P, KT, NTOK], F32R, dense)
    early_w = ExitStack()
    kv_raw = sb("kv_raw", [P, 2, KT, HKV * D], F32, early_w)
    kv_in = sem("kv_in")
    wck_in = sem("wck_in")
    wck = a["L0_attn_W_ck"].rearrange("(s i e) n -> e i s n", s=BS, e=2)
    x_tok = a["L0_attn_x"].rearrange("b (n p) d -> p (b n) d", p=P)

    def three(kt, wh, wl, xh_ap, xl_ap):
        return [(wh, xh_ap), (wl, xh_ap), (wh, xl_ap)]

    def norm_and_weights(hi, lo):
        with ExitStack() as c:
            names = ["gate", "up", "down"]
            scl = sb("scl", [P, 3, P], F32, c)
            w = sb("w", [P, 2048, 2], F32, c)
            xt = g_t[:].rearrange("p h (a d) -> p (h a) d", d=DM)
            xn = w[:].rearrange("p k two -> p (k two)").rearrange("p (t d) -> p t d", d=DM)
            room = v_all[:].rearrange("p t d -> p (t d)").rearrange("p (r n) -> p r n", r=4)
            packed = room[:, 0, :].bitcast(I32)
            code, sign = (room[:, 1, :].bitcast(I16).rearrange("p (r n) -> p r n", r=2)[:, r, :] for r in range(2))
            u1, u2 = (room[:, 2, :].bitcast(BF16).rearrange("p (r n) -> p r n", r=2)[:, r, :] for r in range(2))
            low = packed.bitcast(I16).rearrange("p (n two) -> p n two", two=2)[:, :, 0]
            st = sb("st", [P, TB, 6], F32, c)
            mv = sb("mv", [P, TB, 2], F32, c)
            rstd = sb("rstd", [P, TB], F32, c)
            wg = sb("wg", [P, KT, 3], F32, c)
            z = sb("z", [P, TB, 3], F32, c)
            ez = sb("ez", [P, TB, 3], F32, c)
            zs = sb("zs", [P, 3, TB], F32, c)
            x_in = [sem(f"x_in{q}", c) for q in range(4)]
            const_in = sem("n_const_in", c)
            stat = sem("n_stat", c)
            var_ready = sem("var_ready", c)
            std_ready = sem("std_ready", c)
            normed = sem("normed", c)
            turned = sem("n_turned", c)
            hi_done = sem("n_hi", c)
            lo_done = sem("n_lo", c)
            z_ready = sem("z_ready", c)
            shifted = sem("z_shifted", c)
            exped = sem("z_exped", c)
            summed = sem("z_summed", c)
            logged = sem("z_logged", c)
            zch = sem("z_chain", c)
            packed_in = sem("packed_in", c)
            scale_in = sem("scale_in", c)
            dch = sem("deq_chain", c)
            unpacked = sem("unpacked", c)
            w_ready = sem("w_ready", c)
            w_turned = sem("w_turned", c)
            w_hi_done = sem("w_hi_done", c)
            w_lo_done = sem("w_lo_done", c)
            blk = c.enter_context(nc.Block())

            def bank(m, n):
                return 1 + (8 * m + n) % 7

            srcs = [(a[f"L0_ffn_{m}_W_packed"].rearrange("(n p) k -> p n k", p=P),
                     a[f"L0_ffn_{m}_scales"].rearrange("(n p) k -> p n k", p=P)) for m in names]

            @blk.sync
            def _(sp):
                for q in range(4):
                    sp.dma_start(xt[:, 4 * q:4 * q + 4, :], x_tok[:, 4 * q:4 * q + 4, :]).then_inc(x_in[q], 16)
                sp.dma_start(ident[:], a["ident"]).then_inc(const_in, 16)
                sp.dma_start(wg[:], a["L0_attn_W_gate"].rearrange("(k p) n -> p k n", p=P)).then_inc(const_in, 16)
                for m in range(3):
                    n = srcs[m][0].shape[1]
                    if m == 0:
                        for k in range(3):
                            dst = scl[:, k, :].rearrange("p (n k) -> p n k", n=srcs[k][0].shape[1])
                            sp.dma_start(dst, srcs[k][1]).then_inc(scale_in, 16)
                    else:
                        sp.wait_ge(unpacked, 4 * m)
                    sp.dma_start(packed.rearrange("p (n k) -> p n k", n=n), srcs[m][0]).then_inc(packed_in, 16)
                for n, w_kv in enumerate(("W_k", "W_v")):
                    sp.dma_start(kv_raw[:, n], a["L0_attn_" + w_kv].rearrange("(k p) n -> p k n", p=P)).then_inc(kv_in, 16)

            @blk.vector
            def _(dve):
                ch = Chain(dve, stat)
                for t in range(TB):
                    if t % 4 == 0:
                        dve.wait_ge(x_in[t // 4], 16)
                    dve.bn_stats(st[:, t, :], xt[:, t, :]).then_inc(stat, 1)
                dve.wait_ge(stat, TB)
                for t in range(TB):
                    dve.bn_aggr(mv[:, t, :], st[:, t, :]).then_inc(stat, 1)
                dve.wait_ge(stat, 2 * TB)
                ch.n = 2 * TB
                dve.tensor_scalar(rstd[:], mv[:, :, 1], EPS, None, ALU.add).then_inc(var_ready, 1)
                dve.wait_ge(std_ready, 1)
                ch.link(dve.reciprocal(rstd[:], rstd[:]))
                for t in range(TB):
                    dve.tensor_scalar(xn[:, t, :], xt[:, t, :], mv[:, t, 0:1], rstd[:, t:t + 1],
                                      ALU.subtract, ALU.mult).then_inc(normed, 1)
                for n in range(8):
                    kt, q = n // 4, n % 4
                    dve.wait_ge(hi_done, n + 1)
                    cols = slice(q * CH, (q + 1) * CH)
                    dve.tensor_tensor(xl[:, kt, cols], ps[:, n, :], f32(xh[:, kt, cols]), ALU.subtract).then_inc(lo_done, 1)

                dc = Chain(dve, dch)

                def codes(m, half):
                    if m == 0 and half == 0:
                        dve.wait_ge(scale_in, 48)
                        dc.link(dve.tensor_scalar(scl[:], scl[:], 0.5, None, ALU.mult))
                    if half == 0:
                        dve.wait_ge(packed_in, 16 * (m + 1))
                    if m or half:
                        dve.wait_ge(w_ready, 2 * m + half)
                    dve.tensor_scalar(code, low, 4 * half, 7, ALU.logical_shift_right,
                                      ALU.bitwise_and).then_inc(unpacked, 1)
                    dve.tensor_scalar(sign, low, 12 - 4 * half, -32768, ALU.logical_shift_left,
                                      ALU.bitwise_and).then_inc(unpacked, 1)
                    dve.wait_ge(unpacked, 4 * m + 2 * half + 2)
                    dve.tensor_scalar(u1, code, 2.0, -4.0, ALU.mult, ALU.add)
                    dc.link(dve.tensor_scalar(u2, code, 4.0, -16.0, ALU.mult, ALU.add))
                    dc.link(dve.tensor_tensor(u1, u1, code, ALU.max))
                    dc.link(dve.tensor_tensor(u1, u1, u2, ALU.max))
                    dc.link(dve.tensor_tensor(u2.bitcast(I16), u1.bitcast(I16), sign, ALU.bitwise_or))

                def scaled(m, half):
                    if m and half == 0:
                        dve.wait_ge(w_turned, 8 * m)
                    elif half == 0:
                        dve.wait_ge(turned, 8)
                    dve.tensor_tensor(w[:, :, half].rearrange("p (s k) -> p s k", k=QB // 2),
                                      u2.rearrange("p (s k) -> p s k", k=QB // 2),
                                      scl[:, m, :].unsqueeze(2).broadcast_to([P, P, QB // 2]), ALU.mult).then_inc(w_ready, 1)

                def split(m, n):
                    dve.wait_ge(w_hi_done, 8 * m + n + 1)
                    dve.tensor_tensor(lo[m][:, 4 * n:4 * n + 4, :], ps[:, bank(m, n), :].rearrange("p (c k) -> p c k", c=4),
                                      f32(hi[m][:, 4 * n:4 * n + 4, :]), ALU.subtract).then_inc(w_lo_done, 1)

                for m in range(3):
                    codes(m, 0)
                    if m:
                        for n in range(8):
                            split(m - 1, n)
                    scaled(m, 0)
                    codes(m, 1)
                    scaled(m, 1)
                zc = Chain(dve, zch)
                dve.wait_ge(z_ready, 1)
                zp = ps[:, 0, 0:3 * TB].rearrange("p (t g) -> p t g", g=3)
                zc.link(dve.tensor_reduce(zs[:, 0, :], zp, X, ALU.max))
                dve.tensor_tensor(z[:], zp, zs[:, 0, :].unsqueeze(2).broadcast_to([P, TB, 3]), ALU.subtract).then_inc(shifted, 1)
                for n in range(8):
                    split(2, n)
                    if n == 0:
                        dve.wait_ge(exped, 1)
                        dve.tensor_reduce(zs[:, 1, :], ez[:], X, ALU.add).then_inc(summed, 1)
                        dve.wait_ge(summed, 1)
                        zc.link(dve.reciprocal(zs[:, 0, :], zs[:, 1, :]))
                        dve.tensor_tensor(gate_c[:], ez[:, :, 0], zs[:, 0, :], ALU.mult)
                dve.wait_ge(logged, 1)
                for br in range(2):
                    dve.tensor_tensor(ln_gate[:, br, :], z[:, :, 1 + br], zs[:, 2, :], ALU.subtract)

            @blk.scalar
            def _(act):
                act.wait_ge(var_ready, 1)
                act.activation(rstd[:], rstd[:], ACT.Sqrt).then_inc(std_ready, 1)
                for n in range(8):
                    kt, q = n // 4, n % 4
                    act.wait_ge(turned, n + 1)
                    act.activation(xh[:, kt, q * CH:(q + 1) * CH], ps[:, n, :], ACT.Copy).then_inc(hi_done, 1)
                for m in range(3):
                    if m == 2:
                        act.wait_ge(shifted, 1)
                        act.activation(ez[:], z[:], ACT.Exp).then_inc(exped, 1)
                    for n in range(8):
                        act.wait_ge(w_turned, 8 * m + n + 1)
                        act.activation(hi[m][:, 4 * n:4 * n + 4, :], ps[:, bank(m, n), :].rearrange("p (c k) -> p c k", c=4),
                                       ACT.Copy).then_inc(w_hi_done, 1)
                        if m == 2 and n == 3:
                            act.wait_ge(summed, 1)
                            act.activation(zs[:, 2, :], zs[:, 1, :], ACT.Ln).then_inc(logged, 1)

            @blk.tensor
            def _(pe):
                pe.wait_ge(const_in, 32)
                for n in range(8):
                    kt, q = n // 4, n % 4
                    pe.wait_ge(normed, 4 * q + 4)
                    for t in range(4):
                        ins = pe.transpose(ps[:, n, t * P:(t + 1) * P], xn[:, 4 * q + t, kt * P:(kt + 1) * P], ident[:])
                    ins.then_inc(turned, 1)
                pe.wait_ge(lo_done, 8)
                for m in range(3):
                    pe.wait_ge(w_ready, 2 * m + 2)
                    for n in range(8):
                        if 8 * m + n >= 7:
                            pe.wait_ge(w_lo_done, 8 * m + n - 6)
                        for t in range(4):
                            wt = w[:].rearrange("p k two -> p (k two)")[:, (4 * n + t) * P:(4 * n + t + 1) * P]
                            ins = pe.transpose(ps[:, bank(m, n), t * P:(t + 1) * P], wt, ident[:])
                        ins.then_inc(w_turned, 1)
                    if m < 2:
                        for t in range(m * TB // 2, (m + 1) * TB // 2):
                            for n, (kt, part) in enumerate((kt, part) for kt in range(KT) for part in (xh, xl)):
                                ins = pe.matmul(ps[:, 0, 3 * t:3 * t + 3], f32(part[:, kt, t * P:(t + 1) * P]), wg[:, kt, :],
                                                start=(n == 0), stop=(n == 3))
                        if m:
                            ins.then_inc(z_ready, 1)

    def mlp_phase(hi, lo):
        with ExitStack() as c:
            NT = F // P
            steps = v_all[:].rearrange("p t d -> p (t d)").rearrange("p (r h n) -> p r h n", h=2, n=CH)
            sq, cub, th, hg, it, se, oc = (steps[:, r] for r in range(7))
            ih = sb("ih", [P, 4, CH], F32R, c)
            il = sb("il", [P, 4, CH], F32R, c)
            gu_ready = sem("gu_ready", c)
            sq_ready = sem("sq_ready", c)
            cub_half = sem("cub_half", c)
            cub_ready = sem("cub_ready", c)
            th_ready = sem("th_ready", c)
            hg_ready = sem("hg_ready", c)
            it_ready = sem("it_ready", c)
            ih_ready = sem("ih_ready", c)
            il_ready = sem("il_ready", c)
            down_done = sem("down_done", c)
            o_copied = sem("o_copied", c)
            se_ready = sem("se_ready", c)
            g_done = sem("g_done", c)
            LAGD, PIECES = 3, 4

            def steps_of(step):
                def run(eng):
                    for tc in range(2):
                        for n in range(NT):
                            step(tc, n, True, lambda k, tc=tc, n=n: tc * NT + n - k >= 0)
                    with eng.Fori(2, NC) as tc:
                        for n in range(NT):
                            step(tc, n, True, lambda k: True)
                    for n in range(LAGD + 1):
                        step(NC, n, False, lambda k, n=n: n - k < 0)
                return run

            def slot(n):
                return 2 if n == NT - 1 else 2 * (n % 3)

            with nc.Block() as blk:
                @blk.tensor
                def _(pe):
                    def down(t, n, tc, first):
                        pe.wait_ge(il_ready, t + 1)
                        if n == 0 and not first:
                            pe.wait_ge(o_copied, tc)
                        for ht in range(2):
                            w_i = ht * NT + n
                            prods = three(0, hi[2][:, w_i, :], lo[2][:, w_i, :], ih[:, n % 4, :], il[:, n % 4, :])
                            for k, (wt, xt) in enumerate(prods):
                                ins = pe.matmul(ps[:, 6 + ht, :], wt, xt, start=(n == 0 and k == 0),
                                                stop=(n == NT - 1 and k == 2))
                        ins.then_inc(down_done, 1)

                    def step(tc, n, fresh, have):
                        t = tc * NT + n
                        if fresh:
                            cols = bass.ds(tc * CH, CH)
                            back = {0: 4, 1: 2, NT - 1: 2}.get(n, 3)
                            if have(back):
                                pe.wait_ge(it_ready, t - back + 1)
                            for m in range(2):
                                k = 0
                                for kt in range(KT):
                                    w_i = 2 * n + kt
                                    for wt, xt in three(kt, hi[m][:, w_i, :], lo[m][:, w_i, :], xh[:, kt, cols], xl[:, kt, cols]):
                                        ins = pe.matmul(ps[:, slot(n) + m, :], wt, xt, start=(k == 0), stop=(k == 5))
                                        k += 1
                            ins.then_inc(gu_ready, 1)
                        if have(LAGD):
                            down(t - LAGD, (n - LAGD) % NT, tc, isinstance(tc, int) and tc == 0)
                    steps_of(step)(pe)

                @blk.scalar
                def _(act):
                    def step(tc, n, fresh, have):
                        t = tc * NT + n
                        if n == LAGD and have(n + 1):
                            if not (isinstance(tc, int) and tc == 1):
                                act.wait_ge(g_done, PIECES * (tc - 1))
                            act.wait_ge(down_done, tc * NT)
                            act.activation(oc, ps[:, 6:8, :], ACT.Copy).then_inc(o_copied, 1)
                            act.wait_ge(o_copied, tc)
                            act.activation(se, oc, ACT.Sigmoid).then_inc(se_ready, 1)
                        if fresh:
                            act.wait_ge(gu_ready, t + 1)
                            if have(2):
                                act.wait_ge(cub_half, t - 1)
                            act.activation(sq[:, n % 2, :], ps[:, slot(n), :], ACT.Square).then_inc(sq_ready, 1)
                        if have(1):
                            act.wait_ge(cub_ready, t)
                            act.activation(th[:, (n - 1) % 2, :], cub[:, (n - 1) % 2, :], ACT.Tanh,
                                           scale=0.7978845608028654).then_inc(th_ready, 1)
                        if have(2):
                            act.wait_ge(it_ready, t - 1)
                            if have(6):
                                act.wait_ge(down_done, t - 5)
                            act.activation(ih[:, (n - 2) % 4, :], it[:, n % 2, :], ACT.Copy).then_inc(ih_ready, 1)
                    steps_of(step)(act)

                @blk.vector
                def _(dve):
                    def silu(tc, piece):
                        w = CH // PIECES
                        s = se[:, :, piece * w:(piece + 1) * w]
                        if piece == 0:
                            dve.wait_ge(se_ready, tc)
                        dve.tensor_tensor(g_t[:, :, bass.ds((tc - 1) * CH + piece * w, w)],
                                          oc[:, :, piece * w:(piece + 1) * w], s, ALU.mult).then_inc(g_done, 1)

                    def step(tc, n, fresh, have):
                        t = tc * NT + n
                        if fresh:
                            gp = ps[:, slot(n), :]
                            dve.wait_ge(sq_ready, t + 1)
                            dve.tensor_scalar(sq[:, n % 2, :], sq[:, n % 2, :], 0.044715, 1.0, ALU.mult,
                                              ALU.add).then_inc(cub_half, 1)
                            dve.wait_ge(cub_half, t + 1)
                            if have(2):
                                dve.wait_ge(th_ready, t - 1)
                            dve.tensor_tensor(cub[:, n % 2, :], gp, sq[:, n % 2, :], ALU.mult).then_inc(cub_ready, 1)
                        if have(1):
                            m = (n - 1) % NT
                            dve.wait_ge(th_ready, t)
                            dve.scalar_tensor_tensor(hg[:, m % 2, :], th[:, m % 2, :], 1.0, ps[:, slot(m), :],
                                                     ALU.add, ALU.mult).then_inc(hg_ready, 1)
                            dve.wait_ge(hg_ready, t)
                            if have(3):
                                dve.wait_ge(ih_ready, t - 2)
                            dve.scalar_tensor_tensor(it[:, m % 2, :], hg[:, m % 2, :], 0.5, ps[:, slot(m) + 1, :],
                                                     ALU.mult, ALU.mult).then_inc(it_ready, 1)
                        if have(2):
                            m = (n - 2) % NT
                            dve.wait_ge(ih_ready, t - 1)
                            dve.tensor_tensor(il[:, m % 4, :], it[:, m % 2, :], f32(ih[:, m % 4, :]),
                                              ALU.subtract).then_inc(il_ready, 1)
                        if fresh and LAGD < n <= LAGD + PIECES and have(n + 1):
                            silu(tc, n - LAGD - 1)
                        if not fresh and n == LAGD:
                            for piece in range(PIECES):
                                silu(tc, piece)
                    steps_of(step)(dve)

    def kv_phase():
        with ExitStack() as c:
            wk = [sb(f"wk{n}", [P, KT, 2, 2, P], F32R, c) for n in ("h", "l")]
            rot = sb("rot_k_sb", [P, 2, 2, T], F32, c)
            tu = sb("tu", [P, 2, 2, 2, CH], F32, c)
            ab = sb("ab", [P, 2, 2, CH], F32, c)
            kh = sb("kh", [P, 2, 2, CH], F32R, c)
            kl = sb("kl", [P, 2, 2, CH], F32R, c)
            rot_in = sem("rot_in", c)
            wh_done = sem("wh_done", c)
            wl_done = sem("wl_done", c)
            k_ready = sem("k_ready", c)
            k_rot = sem("k_rot", c)
            k_sum = sem("k_sum", c)
            k_hi = sem("k_hi", c)
            k_lo = sem("k_lo", c)
            k_stored = [sem(f"k_stored{n}", c) for n in range(2)]
            wvh_done = sem("wvh_done", c)
            wvl_done = sem("wvl_done", c)
            v_ready = sem("v_ready", c)
            v_done = sem("v_done", c)
            blk = c.enter_context(nc.Block())
            raw = kv_raw[:]
            wvh, wvl = wvh_sb[:], wvl_sb[:]

            def k_view(ap):
                return ap.rearrange("p (g h i e) -> p g e h i", g=2, h=4, e=2)

            @blk.sync
            def _(sp):
                sp.dma_start(rot[:], a["rot_k"]).then_inc(rot_in, 16)
                sp.wait_ge(wide_zero, 1)
                sp.dma_start(wide[0:BS, :, 0:D], a["L0_attn_W_cv"].rearrange("(s d) n -> s d n", s=BS)).then_inc(wcv_in, 16)
                for b in range(B):
                    for half in range(2):
                        cols = slice(half * CH, (half + 1) * CH)
                        for n in range(2):
                            sp.wait_ge(k_lo, 4 * b + 2 * half + n + 1)
                            for part, t in ((0, kh), (1, kl)):
                                dst = k_scr[n, b, part, :, :, cols].rearrange("e p t -> p e t")
                                sp.dma_start(dst, f32(t[:, n])).then_inc(k_stored[n], 16)
                            if b and not half and n == 0:
                                for e in range(2):
                                    sp.dma_start(wc_raw[32 * e:32 * e + 32], wck[e]).then_inc(wck_in, 16)
                for n in range(2):
                    sp.wait_ge(k_stored[n], 2 * 16 * 4)

            @blk.tensor
            def _(pe):
                pe.wait_ge(wl_done, 4)
                for b in range(B):
                    for half in range(2):
                        cols = slice(b * T + half * CH, b * T + (half + 1) * CH)
                        for n in range(2):
                            k4 = 4 * b + 2 * half + n
                            if k4 >= 4:
                                pe.wait_ge(k_rot, k4 - 3)
                            for e in range(2):
                                k = 0
                                for kt in range(KT):
                                    for w, x in three(kt, wk[0][:, kt, n, e, :], wk[1][:, kt, n, e, :],
                                                      xh[:, kt, cols], xl[:, kt, cols]):
                                        ins = pe.matmul(ps[:, 2 * (k4 % 4) + e, :], w, x, start=(k == 0), stop=(k == 5))
                                        k += 1
                            ins.then_inc(k_ready, 1)
                pe.wait_ge(wvl_done, 1)
                for t in range(TB):
                    if t < 8 and t % 2 == 0:
                        pe.wait_ge(k_rot, 5 + t // 2)
                    elif t >= 8:
                        pe.wait_ge(v_done, t - 7)
                    k = 0
                    ts = slice(t * P, (t + 1) * P)
                    for kt in range(KT):
                        for x, w in three(kt, xh[:, kt, ts], xl[:, kt, ts], wvh[:, kt, :], wvl[:, kt, :]):
                            ins = pe.matmul(ps[:, t % 8, :], x, w, start=(k == 0), stop=(k == 5))
                            k += 1
                    ins.then_inc(v_ready, 1)

            @blk.scalar
            def _(act):
                act.wait_ge(kv_in, 32)
                for kt in range(KT):
                    for n in range(2):
                        act.activation(wk[0][:, kt, n].rearrange("p e (h i) -> p e h i", h=4), k_view(raw[:, 0, kt, :])[:, n],
                                       ACT.Copy).then_inc(wh_done, 1)
                for k in range(8):
                    act.wait_ge(k_sum, k + 1)
                    if k >= 2:
                        act.wait_ge(k_stored[k % 2], 32 * (k // 2))
                    act.activation(kh[:, k % 2], ab[:, k % 2], ACT.Copy).then_inc(k_hi, 1)
                    if k == 1:
                        act.wait_ge(wl_done, 4)
                        act.activation(wvh, raw[:, 1], ACT.Copy).then_inc(wvh_done, 1)
                    if k == 3:
                        act.wait_ge(wcv_in, 16)
                        act.activation(wide[BS:P, :, D:P], wide[0:BS, :, 0:D], ACT.Copy).then_inc(wide_done, 1)
                    for t in {5: (0, 1), 6: (2, 3), 7: range(4, TB)}.get(k, ()):
                        act.wait_ge(v_ready, t + 1)
                        act.activation(v_all[:, t, :], ps[:, t % 8, :], ACT.Copy).then_inc(v_done, 1)

            @blk.gpsimd
            def _(pool):
                pool.memset(wide[:], 0.0).then_inc(wide_zero, 1)
                for k in range(8):
                    pool.wait_ge(k_rot, k + 1)
                    if k >= 2:
                        pool.wait_ge(k_lo, k - 1)
                    pool.tensor_tensor(ab[:, k % 2], tu[:, k % 2, 0], tu[:, k % 2, 1], ALU.add).then_inc(k_sum, 1)

            @blk.vector
            def _(dve):
                for kt in range(KT):
                    for n in range(2):
                        dve.wait_ge(wh_done, 2 * kt + n + 1)
                        dve.tensor_tensor(wk[1][:, kt, n].rearrange("p e (h i) -> p e h i", h=4),
                                          k_view(raw[:, 0, kt, :])[:, n],
                                          f32(wk[0][:, kt, n]).rearrange("p e (h i) -> p e h i", h=4),
                                          ALU.subtract).then_inc(wl_done, 1)
                dve.wait_ge(rot_in, 16)

                def low(k):
                    dve.wait_ge(k_hi, k + 1)
                    dve.tensor_tensor(kl[:, k % 2], ab[:, k % 2], f32(kh[:, k % 2]), ALU.subtract).then_inc(k_lo, 1)

                for k in range(8):
                    cols = slice(k // 2 % 2 * CH, (k // 2 % 2 + 1) * CH)
                    dve.wait_ge(k_ready, k + 1)
                    if k >= 2:
                        dve.wait_ge(k_sum, k - 1)
                    for e in range(2):
                        ins = dve.tensor_tensor(tu[:, k % 2, e], ps[:, 2 * (k % 4) + e, :].unsqueeze(1).broadcast_to([P, 2, CH]),
                                                rot[:, e, :, cols], ALU.mult)
                    ins.then_inc(k_rot, 1)
                    if k:
                        low(k - 1)
                    if k == 2:
                        dve.wait_ge(wvh_done, 1)
                        dve.tensor_tensor(wvl, raw[:, 1], f32(wvh), ALU.subtract).then_inc(wvl_done, 1)
                low(7)

    def compress_phase():
        NK = NBLK * B * HKV
        with ExitStack() as c:
            kx = sb("kx", [P, B * HKV, T], F32R, c)
            wc = sb("wc", [P, 2, BS, D], F32R, c)
            vct = sb("vct", [P, P], F32, c)
            vcn = sb("vcn", [P, 2, D], F32, c)
            x_in = sem("kx_in", c)
            vc_ready = sem("vc_ready", c)
            wch_done = sem("wch_done", c)
            wcl_done = sem("wcl_done", c)
            kc_ready = sem("kc_ready", c)
            kc_hi = sem("kc_hi", c)
            kc_lo = sem("kc_lo", c)
            vct_done = sem("vct_done", c)
            vc_turned = sem("vc_turned", c)
            vcn_done = sem("vcn_done", c)
            vc_stored = sem("vc_stored", c)
            blk = c.enter_context(nc.Block())

            @blk.sync
            def _(sp):
                for g in range(HKV):
                    for b in range(B):
                        src = k_scr[g // 4, b, :, :, 32 * (g % 4):32 * (g % 4) + 32, :].rearrange("l e i t -> (l e) i t")
                        sp.dma_start(f32(kx[:, 2 * g + b, :]), src).then_inc(x_in, 16)
                sp.wait_ge(wcl_done, 1)
                sp.dma_start(wq_raw[:], a["L0_attn_W_q"].rearrange("(k p) n -> p k n", p=P)).then_inc(wq_in, 16)
                sp.wait_ge(vcn_done, 1)
                sp.dma_start(vc_scr.rearrange("m p d -> (m p) d").rearrange("(p two) d -> p two d", two=2), vcn[:]).then_inc(vc_stored, 16)
                sp.wait_ge(vc_stored, 16)

            @blk.tensor
            def _(pe):
                pe.wait_ge(wide_done, 1)
                for d in range(D):
                    xs = v_all[:].rearrange("p t (g d) -> p g t d", d=D)[:, :, :, d]
                    ins = pe.matmul(ps[:, 6, 0:P], wide[:, d, :], xs, start=(d == 0), stop=(d == D - 1))
                ins.then_inc(vc_ready, 1)
                pe.wait_ge(vct_done, 1)
                pe.transpose(ps[:, 6, P:2 * P], vct[:], ident[:]).then_inc(vc_turned, 1)
                pe.wait_ge(wcl_done, 1)
                pe.wait_ge(x_in, 16 * B * HKV)
                for s in range(BS):
                    xs = kx[:].rearrange("p g (n s) -> p (g n) s", s=BS)[:, :, s]
                    for n in range(2):
                        ins = pe.matmul(ps[0:D, 7, 0:NK], wc[:, n, s, :], xs, start=(s == 0 and n == 0),
                                        stop=(s == BS - 1 and n == 1))
                ins.then_inc(kc_ready, 1)

            @blk.scalar
            def _(act):
                act.wait_ge(wck_in, 32)
                act.activation(wc_raw[D:P], wc_raw[0:D], ACT.Copy).then_inc(wck_done, 1)
                act.wait_ge(vc_ready, 1)
                act.activation(vct[:], ps[:, 6, 0:P], ACT.Copy).then_inc(vct_done, 1)
                act.wait_ge(wck_done, 1)
                src = wc_raw[:].rearrange("p s (i e) -> p s e i", e=2)
                for n in range(4):
                    rows = slice(16 * n, 16 * n + 16)
                    act.activation(wc[:, 0, rows].rearrange("p s (e i) -> p s e i", e=2), src[:, rows], ACT.Copy)\
                        .then_inc(wch_done, 1)
                act.wait_ge(vc_turned, 1)
                act.activation(vcn[:], ps[:, 6, P:2 * P].rearrange("p (two d) -> p two d", two=2), ACT.Copy).then_inc(vcn_done, 1)

            @blk.vector
            def _(dve):
                src = wc_raw[:].rearrange("p s (i e) -> p s e i", e=2)
                for n in range(4):
                    dve.wait_ge(wch_done, n + 1)
                    rows = slice(16 * n, 16 * n + 16)
                    ins = dve.tensor_tensor(wc[:, 1, rows].rearrange("p s (e i) -> p s e i", e=2), src[:, rows],
                                            f32(wc[:, 0, rows]).rearrange("p s (e i) -> p s e i", e=2), ALU.subtract)
                ins.then_inc(wcl_done, 1)
                dve.wait_ge(kc_ready, 1)
                for e in range(2):
                    for h in range(4):
                        dve.tensor_copy(kc_all[32 * h:32 * h + 32, e, 0, :], ps[32 * e:32 * e + 32, 7, 0:NK]).then_inc(kc_hi, 1)
                for e in range(2):
                    for h in range(4):
                        dve.wait_ge(kc_hi, 4 * e + h + 1)
                        dve.tensor_tensor(kc_all[32 * h:32 * h + 32, e, 1, :], ps[32 * e:32 * e + 32, 7, 0:NK],
                                          f32(kc_all[32 * h:32 * h + 32, e, 0, :]), ALU.subtract).then_inc(kc_lo, 1)

    def query_phase():
        NJ = HKV * 4
        with ExitStack() as c:
            sb("room_below_wq", [P, 2, KT, HKV * D], F32, c)
            sb("room_of_wq", [P, KT, H * D], F32, c)
            raw = wq_raw
            wq = [sb(f"wq{n}", [P, 2, KT, 2, P], F32R, c) for n in ("h", "l")]
            rot = sb("rot_q_sb", [P, 2, 2, T], F32, c)
            tu = sb("q_tu", [P, 2, 2, 2, CH], F32, c)
            ab = sb("q_ab", [P, 2, 2, CH], F32, c)
            qh = sb("qh", [P, 4, 2, CH], F32R, c)
            ql = sb("ql", [P, 4, 2, CH], F32R, c)
            kcb = sb("kcb", [P, B, 2, 2, D], F32R, c)
            lc = sb("lc", [P, 2, CH], F32, c)
            mc = sb("mc", [P, 3, 16], F32, c)
            ec = sb("ec", [P, 16, 16], F32, c)
            prob_c = sb("prob_c", [P, 2, 4, P], F32, c)
            pc = sb("pc", [D, 2, CH], F32, c)
            q_in = sem("q_in", c)
            zeroed = sem("kcb_zeroed", c)
            wqh_done = sem("wqh_done", c)
            wql_done = sem("wql_done", c)
            q_ready = sem("q_ready", c)
            q_rot = sem("q_rot", c)
            q_sum = sem("q_sum", c)
            q_hi = sem("q_hi", c)
            q_lo = sem("q_lo", c)
            q_stored = [sem(f"q_stored{n}", c) for n in range(4)]
            kcb_ready = sem("kcb_ready", c)
            lc_ready = sem("lc_ready", c)
            lc_out = sem("lc_out", c)
            lt_ready = sem("lt_ready", c)
            c_max = sem("c_max", c)
            c_shift = sem("c_shift", c)
            c_exp = sem("c_exp", c)
            c_chain = sem("c_chain", c)
            c_prob = sem("c_prob", c)
            pt_ready = sem("pt_ready", c)
            pc_out = sem("pc_out", c)
            pc_stored = [sem(f"pc_stored{n}", c) for n in range(2)]
            blk = c.enter_context(nc.Block())
            L_SPLIT, L_COMP, L_MAX, L_PROB, L_BACK = 1, 2, 3, 4, 5

            def steps(eng, step):
                for k in range(8):
                    step(0, k, lambda lag, k=k: k >= lag)
                with eng.Fori(1, NJ // 8 - 1) as it:
                    for k in range(8):
                        step(it, k, lambda lag: True)
                for k in range(8):
                    step(NJ // 8 - 1, k, lambda lag: True)
                for k in range(L_BACK):
                    step(NJ // 8, k, lambda lag, k=k: k < lag)

            def place(it, k, lag):
                j, m = 8 * it + k - lag, (k - lag) % 8
                first = isinstance(it, int) and it == 0
                return j, m, 2 * it + (k - lag) // 4, m // 2 % 2, m % 2, (lambda n: not first or k - lag >= n)

            @blk.sync
            def _(sp):
                sp.dma_start(rot[:], a["rot_q"]).then_inc(q_in, 16)

                def step(it, k, on):
                    if on(L_SPLIT):
                        j, m, g, b, half, _ = place(it, k, L_SPLIT)
                        cols = slice(half * CH, (half + 1) * CH)
                        for part, t, done in ((0, qh, q_hi), (1, ql, q_lo)):
                            sp.wait_ge(done, j + 1)
                            dst = q_scr[bass.ds(g, 1), b, part, :, :, cols].rearrange("g e p t -> p (g e) t")
                            sp.dma_start(dst, f32(t[:, m % 4])).then_inc(q_stored[m % 4], 16)
                    if on(L_BACK):
                        j, m, g, b, half, _ = place(it, k, L_BACK)
                        sp.wait_ge(pc_out, j + 1)
                        dst = pc_scr[bass.ds(g, 1), D * b:D * b + D, half * CH:(half + 1) * CH].rearrange("g p t -> (g p) t")
                        sp.dma_start(dst, pc[:, m % 2]).then_inc(pc_stored[m % 2], 16)
                steps(sp, step)
                for n in range(4):
                    sp.wait_ge(q_stored[n], 2 * 16 * (NJ // 4))
                for n in range(2):
                    sp.wait_ge(pc_stored[n], 16 * (NJ // 2))

            @blk.tensor
            def _(pe):
                def step(it, k, on):
                    if on(0):
                        j, m, g, b, half, past = place(it, k, 0)
                        if k % 4 == 0:
                            pe.wait_ge(wql_done, g + 1)
                        if past(2):
                            pe.wait_ge(q_rot, j - 1)
                        cols = slice(b * T + half * CH, b * T + (half + 1) * CH)
                        for e in range(2):
                            n = 0
                            for kt in range(KT):
                                for w, x in three(kt, wq[0][:, k // 4, kt, e, :], wq[1][:, k // 4, kt, e, :],
                                                  xh[:, kt, cols], xl[:, kt, cols]):
                                    ins = pe.matmul(ps[:, 2 * (k % 2) + e, :], w, x, start=(n == 0), stop=(n == 5))
                                    n += 1
                        ins.then_inc(q_ready, 1)
                    if on(L_COMP):
                        j, m, g, b, half, past = place(it, k, L_COMP)
                        pe.wait_ge(q_lo, j + 1)
                        pe.wait_ge(kcb_ready, 4 * (4 * it + (k - L_COMP) // 2 + 1))
                        if past(2):
                            pe.wait_ge(lc_out, j - 1)
                        n = 0
                        for e in range(2):
                            for w, x in ((0, qh), (1, qh), (0, ql)):
                                ins = pe.matmul(ps[0:D, 4 + m % 2, :], kcb[:, b, e, w, :], x[:, m % 4, e, :],
                                                start=(n == 0), stop=(n == 5))
                                n += 1
                        ins.then_inc(lc_ready, 1)
                    if on(L_MAX):
                        j, m, g, b, half, past = place(it, k, L_MAX)
                        if not past(1):
                            pe.wait_ge(zeroed, 3)
                        pe.wait_ge(lc_out, j + 1)
                        if past(1):
                            pe.wait_ge(c_shift, j)
                        for t in range(4):
                            ins = pe.transpose(ps[:, 6, t * P:(t + 1) * P], lc[:, m % 2, t * P:(t + 1) * P], ident[:])
                        ins.then_inc(lt_ready, 1)
                    if on(L_BACK):
                        j, m, g, b, half, past = place(it, k, L_BACK)
                        pe.wait_ge(c_prob, j + 1)
                        if past(1):
                            pe.wait_ge(pc_out, j)
                        for t in range(4):
                            ins = pe.transpose(ps[:, 7, t * P:(t + 1) * P], prob_c[:, m % 2, t, :], ident[:])
                        ins.then_inc(pt_ready, 1)
                steps(pe, step)

            def w_view(g, kt):
                return raw[:, kt, bass.ds(g * REP * D, REP * D)].rearrange("p (h i e) -> p e h i", h=REP, e=2)

            def splits(it, k, on):
                return on(0) and k % 4 == 2 and not (isinstance(it, int) and it == NJ // 8 - 1 and k == 6)

            @blk.gpsimd
            def _(pool):
                pool.memset(f32(kcb[:]), 0.0).then_inc(zeroed, 1)
                pool.memset(prob_c[:, :, :, D:P], 0.0).then_inc(zeroed, 1)
                pool.wait_ge(zeroed, 2)
                pool.memset(lc[D:P], 0.0).then_inc(zeroed, 1)
                pool.wait_ge(zeroed, 3)

                def w_low(g, n):
                    pool.wait_ge(wqh_done, g + 1)
                    for kt in range(KT):
                        ins = pool.tensor_tensor(wq[1][:, n, kt].rearrange("p e (h i) -> p e h i", h=REP), w_view(g, kt),
                                                f32(wq[0][:, n, kt]).rearrange("p e (h i) -> p e h i", h=REP), ALU.subtract)
                    ins.then_inc(wql_done, 1)
                w_low(0, 0)

                def step(it, k, on):
                    if not on(0):
                        return
                    j, m, g, b, half, past = place(it, k, 0)
                    if half == 0:
                        if past(4):
                            pool.wait_ge(lc_ready, j - 2)
                        for h in range(4):
                            src = kc_all[32 * h:32 * h + 32, :, :, bass.ds((2 * g + b) * NBLK, NBLK)]
                            pool.tensor_copy(kcb[32 * h:32 * h + 32, b, :, :, NBLK * h:NBLK * h + NBLK], f32(src))\
                                .then_inc(kcb_ready, 1)
                            pool.wait_ge(kcb_ready, 4 * (2 * g + b) + h + 1)
                    pool.wait_ge(q_rot, j + 1)
                    if past(2):
                        pool.wait_ge(q_lo, j - 1)
                    pool.tensor_tensor(ab[:, k % 2], tu[:, k % 2, 0], tu[:, k % 2, 1], ALU.add).then_inc(q_sum, 1)
                    if splits(it, k, on):
                        w_low(g + 1, (k // 4 + 1) % 2)
                steps(pool, step)

            def buffer_free(eng, j, m, n4, past):
                if past(4):
                    eng.wait_ge(q_stored[m % 4], 32 * n4)
                    eng.wait_ge(lc_ready, j - 3)

            @blk.scalar
            def _(act):
                act.wait_ge(wq_in, 16)

                def w_high(g, n):
                    for kt in range(KT):
                        ins = act.activation(wq[0][:, n, kt].rearrange("p e (h i) -> p e h i", h=REP), w_view(g, kt), ACT.Copy)
                    ins.then_inc(wqh_done, 1)
                w_high(0, 0)

                def step(it, k, on):
                    if splits(it, k, on):
                        j, m, g, b, half, past = place(it, k, 0)
                        if past(4):
                            act.wait_ge(q_ready, j - 2)
                        w_high(g + 1, (k // 4 + 1) % 2)
                    if on(L_COMP):
                        j, m, g, b, half, past = place(it, k, L_COMP)
                        act.wait_ge(lc_ready, j + 1)
                        if past(2):
                            act.wait_ge(lt_ready, j - 1)
                        act.activation(lc[0:D, m % 2], ps[0:D, 4 + m % 2, :], ACT.Copy).then_inc(lc_out, 1)
                    if on(L_SPLIT):
                        j, m, g, b, half, past = place(it, k, L_SPLIT)
                        act.wait_ge(q_sum, j + 1)
                        buffer_free(act, j, m, 2 * it + (k - L_SPLIT) // 4, past)
                        act.activation(qh[:, m % 4], ab[:, m % 2], ACT.Copy).then_inc(q_hi, 1)
                    if on(L_MAX):
                        j, m, g, b, half, past = place(it, k, L_MAX)
                        act.wait_ge(c_shift, j + 1)
                        act.activation(ec[:], ec[:], ACT.Exp).then_inc(c_exp, 1)
                    if on(L_BACK):
                        j, m, g, b, half, past = place(it, k, L_BACK)
                        act.wait_ge(pt_ready, j + 1)
                        if past(2):
                            act.wait_ge(pc_stored[m % 2], 16 * (4 * it + (k - L_BACK) // 2))
                        act.activation(pc[:, m % 2], ps[0:D, 7, :], ACT.Copy).then_inc(pc_out, 1)
                steps(act, step)

            @blk.vector
            def _(dve):
                ch = Chain(dve, c_chain)

                def step(it, k, on):
                    if on(L_PROB):
                        j, m, g, b, half, past = place(it, k, L_PROB)
                        dve.wait_ge(c_exp, j + 1)
                        ch.n, ch.base = 0, 3 * j
                        ch.link(dve.tensor_reduce(mc[:, 1, :], ec[:], X, ALU.add))
                        ch.link(dve.reciprocal(mc[:, 2, :], mc[:, 1, :]))
                        gc = gate_c[:, TJ * b + 4 * half:TJ * b + 4 * half + 4].unsqueeze(2).broadcast_to([P, 4, REP])
                        ch.link(dve.tensor_tensor(mc[:, 1, :].rearrange("p (t h) -> p t h", t=4),
                                                  mc[:, 2, :].rearrange("p (t h) -> p t h", t=4), gc, ALU.mult))
                        if past(2):
                            dve.wait_ge(pt_ready, j - 1)
                        dve.tensor_tensor(prob_c[:, m % 2, :, 0:D].rearrange("p t (h n) -> p t h n", h=REP),
                                          ec[:].rearrange("p (t h) n -> p t h n", t=4),
                                          mc[:, 1, :].rearrange("p (t h) -> p t h", t=4).unsqueeze(3).broadcast_to([P, 4, REP, NBLK]),
                                          ALU.mult).then_inc(c_prob, 1)
                    if on(0):
                        j, m, g, b, half, past = place(it, k, 0)
                        if not past(1):
                            dve.wait_ge(q_in, 16)
                        dve.wait_ge(q_ready, j + 1)
                        if past(2):
                            dve.wait_ge(q_sum, j - 1)
                        for e in range(2):
                            ins = dve.tensor_tensor(tu[:, k % 2, e], ps[:, 2 * (k % 2) + e, :].unsqueeze(1).broadcast_to([P, 2, CH]),
                                                    rot[:, e, :, half * CH:(half + 1) * CH], ALU.mult)
                        ins.then_inc(q_rot, 1)
                    if on(L_MAX):
                        j, m, g, b, half, past = place(it, k, L_MAX)
                        dve.wait_ge(lt_ready, j + 1)
                        lt = ps[:, 6, :].rearrange("p (t r h n) -> p t r h n", t=4, r=2, h=REP)[:, :, 0]
                        nm = mc[:, 0, :].rearrange("p (t h) -> p t h", t=4)
                        dve.tensor_reduce(nm, lt, X, ALU.max, negate=True).then_inc(c_max, 1)
                        dve.wait_ge(c_max, j + 1)
                        if past(1):
                            dve.wait_ge(c_prob, j)
                        dve.tensor_tensor(ec[:].rearrange("p (t h) n -> p t h n", t=4), lt,
                                          nm.unsqueeze(3).broadcast_to([P, 4, REP, NBLK]), ALU.add).then_inc(c_shift, 1)
                    if on(L_SPLIT):
                        j, m, g, b, half, past = place(it, k, L_SPLIT)
                        dve.wait_ge(q_hi, j + 1)
                        buffer_free(dve, j, m, 2 * it + (k - L_SPLIT) // 4, past)
                        dve.tensor_tensor(ql[:, m % 4], ab[:, m % 2], f32(qh[:, m % 4]), ALU.subtract).then_inc(q_lo, 1)
                steps(dve, step)

    def attention_phase():
        NP = 4 * HKV
        NQ = TJ
        with ExitStack() as c:
            qa = sb("qa", [P, 4, 2, T], F32R, c)
            qb = sb("qb", [P, 2, 2, 2, T], F32R, c)
            k_hh = sb("k_hh", [P, B, T], F32R, c)
            k_ll = sb("k_ll", [P, B, T], F32R, c)
            k_l1 = sb("k_l1", [P, B, T], F32R, c)
            v_s = sb("v_s", [P, B, TJ, D], F32, c)
            pct = sb("pct", [P, T], F32, c)
            vcp = sb("vcp", [P, 4, P], F32, c)
            prob = sb("prob", [P, 2, 2, T], F32, c)
            prob_w = sb("prob_w", [P, 2, 2, WW], F32, c)
            wl = sb("wl", [P, 2, TJ, WW], F32, c)
            junk = sb("junk", [P, T], BF16, c)
            nmax = sb("nmax", [P, 2, 2 * TJ], F32, c)
            sums = sb("sums", [P, 2, 2 * TJ], F32, c)
            lns = sb("lns", [P, 2, 2 * TJ], F32, c)
            shift = sb("shift", [P, 2, 2, 2 * TJ], F32, c)
            shift_r = sb("shift_r", [P, P // (4 * TJ), 2, 2 * TJ], F32R, c)
            o_t = sb("o_t", [P, 2, T], F32, c)
            mask_a = sb("mask_a_sb", [P, WW], F32, c)
            mask_b = sb("mask_b_sb", [P, WW], F32, c)
            pick = sb("pick_sb", [D, 4, TJ], F32, c)
            const_in = sem("m_const_in", c)
            ones_ok = sem("ones_ok", c)
            qa_in = [sem(f"qa_in{n}", c) for n in range(4)]
            qb_in = [sem(f"qb_in{n}", c) for n in range(2)]
            k_in = [sem(f"k_in{n}", c) for n in range(2)]
            k_l1_in = [sem(f"k_l1_in{n}", c) for n in range(2)]
            pc_in = sem("pc_in", c)
            v_ok = sem("v_ok", c)
            a_ready = sem("a_ready", c)
            b_ready = sem("b_ready", c)
            w_ready = sem("w_ready5", c)
            t_ready = sem("t_ready", c)
            pv_done = sem("pv_done", c)
            a_exp = sem("a_exp", c)
            b_exp = sem("b_exp", c)
            wb_exp = sem("wb_exp", c)
            w_masked = sem("w_masked", c)
            w_exp = sem("w_exp", c)
            ln_done = sem("ln_done", c)
            o_out = sem("o_out", c)
            a_max = sem("a_max", c)
            a_win = sem("a_win", c)
            w_max = sem("w_max", c)
            w_shift = sem("w_shift", c)
            w_sum = sem("w_sum", c)
            m_chain = sem("m_chain", c)
            st_ready = sem("st_ready", c)
            aug_done = sem("aug_done", c)
            o_stored = [sem(f"o_stored{n}", c) for n in range(2)]
            blk = c.enter_context(nc.Block())
            OB = 6

            def stages(stage):
                def run(eng):
                    stage(-1, 3, False, True)
                    for u in range(4):
                        stage(0, u, True, True)
                    with eng.Fori(1, HKV - 1) as it:
                        for u in range(4):
                            stage(it, u, True, True)
                    for u in range(4):
                        stage(HKV - 1, u, True, u < 3)
                return run

            def early(it, u, n):
                return isinstance(it, int) and 4 * it + u < n

            def after(it, u, n=1):
                return it + (u + n) // 4, (u + n) % 4

            PE_ORDER = ("B0 B1 A A A V0 W B0 W B1 A A A V1 A V0 A B0 A V1 B1 A B0 A V0 W B1 W A A A V1 V0 B0 A B1 A V1 "
                        "V0 W B0 W B1 V1 B0 W B1 V0 W B0 V1 V0 B1 T V1 V0 V1").split()
            ACT_ORDER = ("O B0 B1 A A A W B0 W B1 A A A A A B0 A B1 B0 A A W B1 W X0 A A A B0 B1 A A W B0 W B1 X1 B0 W B1 "
                        "L W B0 B1").split()
            DVE_ORDER = ("A A A K A A A A A K A M A A K A A A K S A A M K K S K C K G G G G").split()

            def jobs(order, b_on, a_on):
                of_b = ("B0", "B1", "W", "V0", "V1", "O", "K")
                seen, seq = {}, []
                for what in order:
                    if b_on if what in of_b else a_on:
                        seq.append((what, seen.setdefault(what, 0)))
                        seen[what] += 1
                return seq

            @blk.sync
            def _(sp):
                sp.dma_start(mask_a[:], a["mask_a"]).then_inc(const_in, 16)
                sp.dma_start(mask_b[:], a["mask_b"]).then_inc(const_in, 16)
                sp.dma_start(pick[:], a["pick"]).then_inc(const_in, 16)

                def load_k(g, b):
                    def rows(part):
                        src = k_scr[bass.ds(g // 4, 1), b, part, :, bass.ds(32 * (g % 4), 32), :]
                        return src.rearrange("g e i t -> (g e) i t")
                    for dst, part in ((k_hh[0:D, b], 0), (k_hh[D:P, b], 0), (k_ll[0:D, b], 1), (k_ll[D:P, b], 1)):
                        sp.dma_start(f32(dst), rows(part)).then_inc(k_in[b], 16)

                def load_k_l1(g, b):
                    src = k_scr[bass.ds(g // 4, 1), b, 1, :, bass.ds(32 * (g % 4), 32), :].rearrange("g e i t -> (g e) i t")
                    sp.dma_start(f32(k_l1[0:D, b]), src).then_inc(k_l1_in[b], 16)

                def load_qa(it, u):
                    for h in range(2):
                        r = 32 * (2 * (u % 2) + h)
                        src = q_scr[bass.ds(it, 1), u // 2, :, :, r:r + 32, :].rearrange("g l e i t -> (g l e) i t")
                        sp.dma_start(f32(qa[:, u, h]), src).then_inc(qa_in[u], 16)

                def load_qb(it, u):
                    for br in range(2):
                        for h in range(2):
                            r = 32 * (2 * (u % 2) + h)
                            src = q_scr[bass.ds(it, 1), u // 2, 0, :, r:r + 32, :].rearrange("g e i t -> (g e) i t")
                            sp.dma_start(f32(qb[0:D, u % 2, br, h]), src).then_inc(qb_in[u % 2], 16)

                def load_pc(it):
                    sp.dma_start(pct[:], pc_scr[bass.ds(it, 1)].rearrange("g p t -> (g p) t")).then_inc(pc_in, 16)
                    vc = vc_scr.rearrange("m p d -> (m p) d")
                    for b in range(B):
                        for h in range(REP):
                            r = D * b + NBLK * h
                            sp.dma_start(vcp[r:r + NBLK, 2 * b + h // 2, D * (h % 2):D * (h % 2) + D],
                                         vc[bass.ds((2 * it + b) * NBLK, NBLK), :]).then_inc(pc_in, 16)

                def stage(it, u, b_on, a_on):
                    if not b_on:
                        load_k(0, 0)
                        load_qa(0, 0)
                        load_k_l1(0, 0)
                        load_qb(0, 0)
                        load_qa(0, 1)
                        load_k(0, 1)
                        load_k_l1(0, 1)
                        sp.wait_ge(ones_ok, 3)
                        load_pc(0)
                        load_qb(0, 1)
                        sp.dma_start(wo_raw[:], a["L0_attn_W_o"].rearrange("(k p) n -> p k n", p=P)).then_inc(wo_in, 16)
                        return
                    pr = 4 * it + u
                    last = isinstance(it, int) and it == HKV - 1
                    if u == 0 and not early(it, u, 1):
                        sp.wait_ge(pv_done, 8 * pr)
                        load_k(it, 1)
                        load_k_l1(it, 1)
                    if u == 2 and not last:
                        sp.wait_ge(pv_done, 8 * pr)
                        load_k(it + 1, 0)
                        load_k_l1(it + 1, 0)
                    if not (last and u >= 2):
                        if not early(it, u, 2):
                            sp.wait_ge(pv_done, 8 * (pr - 1))
                        load_qa(*after(it, u, 2))
                    if not early(it, u, 1):
                        store_o(*after(it, u, -1))
                    if u == 3 and not last:
                        sp.wait_ge(pv_done, 8 * pr + 1)
                        load_pc(it + 1)
                    if not (last and u >= 2):
                        sp.wait_ge(pv_done, 8 * (pr + 1))
                        load_qb(*after(it, u, 2))

                def store_o(it, u):
                    sp.wait_ge(o_out, 4 * it + u + 1)
                    b, row = u // 2, (u % 2) * P
                    sp.dma_start(o_scr[b, bass.ds(it * (REP * D) + row, P), :], o_t[:, u % 2]).then_inc(o_stored[u % 2], 16)

                stages(stage)(sp)
                store_o(HKV - 1, 3)
                for n in range(2):
                    sp.wait_ge(o_stored[n], 16 * NP // 2)

            @blk.tensor
            def _(pe):
                pe.wait_ge(ones_ok, 3)
                ring = {"n": 0, "used": [None] * 3}

                def slot(*used):
                    n = ring["n"] % 3
                    if ring["used"][n] is not None:
                        for s_, f_ in ring["used"][n]:
                            pe.wait_ge(s_, f_)
                    ring["used"][n] = used
                    ring["n"] += 1
                    return 2 * n

                def stage(it, u, b_on, a_on):
                    pr = 4 * it + u
                    ita, ua = after(it, u)
                    x = 4 * ita + ua
                    b, ba = u // 2, ua // 2

                    def job_a(n):
                        h, j = n // TJ, n % TJ
                        if n == 0:
                            pe.wait_ge(qa_in[ua], 32 * (ita + 1))
                            pe.wait_ge(k_in[ba], 64 * (ita + 1))
                        s0 = slot((a_exp, 16 * x + n + 1))
                        lhs = qa[:, ua, h, j * P:(j + 1) * P]
                        for half in range(2):
                            cols = slice(half * CH, (half + 1) * CH)
                            pe.matmul(ps[:, s0 + half, :], lhs, k_hh[:, ba, cols], start=True, stop=False)
                            ins = pe.matmul(ps[:, s0 + half, :], lhs, k_ll[:, ba, cols], start=False, stop=True)
                        ins.then_inc(a_ready, 1)

                    def job_b(cc, h):
                        if cc == 0:
                            if h == 0:
                                pe.wait_ge(qb_in[u % 2], 64 * (2 * it + u // 2 + 1))
                                pe.wait_ge(k_l1_in[b], 16 * (it + 1))
                            pe.wait_ge(aug_done, 4 * pr + h + 1)
                        s0 = slot((b_exp, 16 * pr + 2 * cc + h + 1))
                        ks = slice(cc * P, (cc + 1) * P)
                        for half in range(2):
                            cols = slice(half * CH, (half + 1) * CH)
                            pe.matmul(ps[:, s0 + half, :], k_hh[:, b, ks], qa[:, u, h, cols], start=True, stop=False)
                            ins = pe.matmul(ps[:, s0 + half, :], k_l1[:, b, ks], qb[:, u % 2, 0, h, cols], start=False, stop=True)
                        ins.then_inc(b_ready, 1)

                    def job_w(cc):
                        if cc == 0:
                            pe.wait_ge(aug_done, 4 * pr + 4)
                        n = min(WW, T - cc * P)
                        s0 = slot((wb_exp, 8 * pr + cc + 1))
                        ks, ts = slice(cc * P, (cc + 1) * P), slice(cc * P, cc * P + n)
                        dst = ps[:, s0, 0:2 * n].rearrange("p (h n) -> p h n", h=2)
                        pe.matmul(dst, k_hh[:, b, ks], qa[:, u, :, ts], start=True, stop=False)
                        pe.matmul(dst, k_l1[:, b, ks], qb[:, u % 2, 1, :, ts], start=False, stop=True).then_inc(w_ready, 1)

                    def job_t():
                        s0 = slot((aug_done, 4 * x + 4))
                        ring["n"] += 1
                        pe.wait_ge(st_ready, x + 1)
                        pe.transpose(ps[:, s0, 0:P], f32(shift_r[:]).rearrange("p l r n -> p (l r n)"), ident[:]).then_inc(t_ready, 1)

                    def job_v(cc, half):
                        if cc == 0 and half == 0:
                            pe.wait_ge(pc_in, 144 * (it + 1))
                            pe.wait_ge(v_ok, 2 * it + b + 1)
                            if not early(it, u, 1):
                                pe.wait_ge(o_out, pr)
                            for hf in range(2):
                                pe.matmul(ps[:, OB + hf, :], vcp[:, u, :], pct[:, hf * CH:(hf + 1) * CH],
                                          start=True, stop=False, skip_group_check=True)
                        lastc = cc == TJ - 1
                        v = v_s[:, b, cc, :]
                        if half == 0:
                            pe.wait_ge(b_exp, 16 * pr + 2 * cc + 2)
                        for h in range(2):
                            pe.matmul(ps[D * h:D * h + D, OB + half, :], v, prob[:, cc % 2, h, half * CH:(half + 1) * CH],
                                      start=False, stop=lastc and half == 0, skip_group_check=True)
                        if half == 0:
                            return
                        pe.wait_ge(w_masked, 8 * pr + cc + 1)
                        n = min(WW, T - cc * P)
                        for t0, t1 in ([(0, P), (P, WW)] if cc == 3 else [(0, n)]):
                            t = cc * P + t0
                            for h in range(2):
                                ins = pe.matmul(ps[D * h:D * h + D, OB + t // CH, t % CH:t % CH + t1 - t0], v,
                                                prob_w[:, cc % 2, h, t0:t1], start=False, stop=lastc, skip_group_check=True)
                        ins.then_inc(pv_done, 1)

                    for what, n in jobs(PE_ORDER, b_on, a_on):
                        if what == "A":
                            job_a(n)
                        elif what[0] == "B":
                            job_b(n, int(what[1]))
                        elif what == "W":
                            job_w(n)
                        elif what == "T":
                            job_t()
                        else:
                            job_v(n, int(what[1]))

                stage(-1, 3, False, True)
                ring["n"] += -ring["n"] % 3
                for u in range(4):
                    stage(0, u, True, True)
                assert (ring["n"]) % 3 == 0
                with pe.Fori(1, HKV - 1) as it:
                    def moved(entry, by):
                        return [(s_, f_ + (it - 1) * by[s_.name]) for s_, f_ in entry]
                    per = {a_exp.name: 64, b_exp.name: 64, wb_exp.name: 32, aug_done.name: 16}
                    ring["used"] = [moved(e, per) for e in ring["used"]]
                    for u in range(4):
                        stage(it, u, True, True)
                total = {a_exp.name: 64 * (HKV - 1) + 16, b_exp.name: 64 * (HKV - 1),
                         wb_exp.name: 32 * (HKV - 1), aug_done.name: 16 * (HKV - 1) + 4}
                ring["used"] = [[(s_, total[s_.name]) for s_, _ in e] for e in ring["used"]]
                for u in range(4):
                    stage(HKV - 1, u, True, u < 3)

            def slots_of(b_on, a_on, n0):
                out, n = {}, n0
                for what, k in jobs(PE_ORDER, b_on, a_on):
                    if what[0] != "V":
                        out[(what, k)] = 2 * (n % 3)
                        n += 1 + (what == "T")
                return out, n

            slot_maps = [slots_of(False, True, 0)[0]]
            n_ = 0
            for u_ in range(4):
                m_, n_ = slots_of(True, True, n_)
                slot_maps.append(m_)
            last3 = slots_of(True, False, slots_of(True, True, slots_of(True, True, slots_of(True, True, 0)[1])[1])[1])[0]

            def slot_map(u, b_on, a_on):
                return slot_maps[0] if not b_on else slot_maps[1 + u] if a_on else last3

            @blk.scalar
            def _(act):
                def stage(it, u, b_on, a_on):
                    pr = 4 * it + u
                    ita, ua = after(it, u)
                    x = 4 * ita + ua
                    first_a = isinstance(it, int) and x == 0
                    where = slot_map(u, b_on, a_on)
                    for what, n in jobs(ACT_ORDER, b_on, a_on):
                        if what == "A":
                            s0 = where[("A", n)]
                            act.wait_ge(a_win, 16 * x + n + 1)
                            if n == 0 and not first_a:
                                act.wait_ge(ln_done, x)
                            src = ps[:, s0:s0 + 2, :].rearrange("p a n -> p (a n)")
                            if n or not first_a:
                                act.wait_ge(a_exp, 16 * x + n)
                            act.activation(junk[:], src, ACT.Exp, bias=nmax[:, 0, n:n + 1],
                                           accum_out=sums[:, 0, n:n + 1]).then_inc(a_exp, 1)
                        elif what[0] == "B":
                            h = int(what[1])
                            s0 = where[(what, n)]
                            act.wait_ge(b_ready, 16 * pr + 2 * n + h + 1)
                            if not early(it, u, 1) or n >= 2:
                                act.wait_ge(pv_done, 8 * pr + n - 1)
                            act.activation(prob[:, n % 2, h], ps[:, s0:s0 + 2, :].rearrange("p a n -> p (a n)"), ACT.Exp)\
                                .then_inc(b_exp, 1)
                        elif what == "W":
                            s0 = where[("W", n)]
                            w = min(WW, T - n * P)
                            act.wait_ge(w_ready, 8 * pr + n + 1)
                            if not early(it, u, 1) or n >= 2:
                                act.wait_ge(pv_done, 8 * pr + n - 1)
                            act.activation(prob_w[:, n % 2, :, 0:w], ps[:, s0, 0:2 * w].rearrange("p (h n) -> p h n", h=2), ACT.Exp)\
                                .then_inc(wb_exp, 1)
                        elif what[0] == "X":
                            h = int(what[1])
                            act.wait_ge(w_shift, 2 * x + h + 1)
                            act.activation(wl[:, h], wl[:, h], ACT.Exp).then_inc(w_exp, 1)
                        elif what == "L":
                            act.wait_ge(w_sum, 2 * x + 2)
                            act.wait_ge(a_exp, 16 * x + 16)
                            if not first_a:
                                act.wait_ge(st_ready, x)
                            act.activation(lns[:], sums[:], ACT.Ln).then_inc(ln_done, 1)
                        elif not early(it, u, 1):
                            out_o(*after(it, u, -1))

                def out_o(it, u):
                    pr = 4 * it + u
                    act.wait_ge(pv_done, 8 * pr + 8)
                    if not early(it, u, 2):
                        act.wait_ge(o_stored[u % 2], 16 * (2 * it + u // 2))
                    act.activation(o_t[:, u % 2].rearrange("p (a n) -> p a n", a=2), ps[:, OB:OB + 2, :], ACT.Copy).then_inc(o_out, 1)

                stages(stage)(act)
                out_o(HKV - 1, 3)

            @blk.gpsimd
            def _(pool):
                pool.memset(f32(k_l1[D:P]), 1.0).then_inc(ones_ok, 1)
                pool.wait_ge(ones_ok, 1)
                pool.memset(f32(shift_r[:, 2:]), 0.0).then_inc(ones_ok, 1)
                pool.memset(vcp[:], 0.0).then_inc(ones_ok, 1)

                def copy_v(g, b):
                    pool.tensor_copy(v_s[:, b], v_all[:, TJ * b:TJ * b + TJ, bass.ds(g * D, D)]).then_inc(v_ok, 1)

                def stage(it, u, b_on, a_on):
                    ita, ua = after(it, u)
                    x = 4 * ita + ua
                    if a_on:
                        for h in range(2):
                            pool.wait_ge(w_max, 2 * x + h + 1)
                            nm = nmax[:, 1, TJ * h:TJ * h + TJ].unsqueeze(2).broadcast_to([P, TJ, WW])
                            pool.tensor_tensor(wl[:, h], wl[:, h], nm, ALU.add).then_inc(w_shift, 1)
                    if not b_on:
                        copy_v(0, 0)
                        copy_v(0, 1)
                    elif u == 0 and not early(it, u, 1):
                        pool.wait_ge(pv_done, 8 * (4 * it))
                        copy_v(it, 1)
                    elif u == 2 and not (isinstance(it, int) and it == HKV - 1):
                        pool.wait_ge(pv_done, 8 * (4 * it + 2))
                        copy_v(it + 1, 0)
                stages(stage)(pool)

            @blk.vector
            def _(dve):
                ch = Chain(dve, m_chain)
                dve.wait_ge(const_in, 48)

                def stage(it, u, b_on, a_on):
                    ita, ua = after(it, u)
                    x = 4 * ita + ua
                    first_a = isinstance(it, int) and x == 0
                    ba = ua // 2
                    where = slot_map(u, b_on, a_on)

                    def job_a(n):
                        h, j = n // TJ, n % TJ
                        s0 = where[("A", n)]
                        if j == 0:
                            if not first_a:
                                dve.wait_ge(w_sum, 2 * (x - 1) + h + 1)
                                dve.wait_ge(st_ready, x)
                            dve.memset(wl[:, h, 0, 0:WIN], NEG)
                        dve.wait_ge(a_ready, 16 * x + n + 1)
                        src = ps[:, s0:s0 + 2, :].rearrange("p a n -> p (a n)")
                        dve.tensor_reduce(nmax[:, 0, n:n + 1], src, X, ALU.max, negate=True).then_inc(a_max, 1)
                        lo = WIN if j == 0 else 0
                        dve.tensor_tensor(wl[:, h, j, lo:WW], src[:, P * j - WIN + lo:P * j + P], mask_a[:, lo:WW], ALU.add)\
                            .then_inc(a_win, 1)

                    def win_max(h):
                        dve.wait_ge(a_win, 16 * x + TJ * h + TJ)
                        dve.tensor_reduce(nmax[:, 1, TJ * h:TJ * h + TJ], wl[:, h], X, ALU.max, negate=True).then_inc(w_max, 1)

                    def win_sum(h):
                        dve.wait_ge(w_exp, 2 * x + h + 1)
                        dve.tensor_reduce(sums[:, 1, TJ * h:TJ * h + TJ], wl[:, h], X, ALU.add).then_inc(w_sum, 1)

                    def shifts():
                        dve.wait_ge(ln_done, x + 1)
                        ch.n, ch.base = 0, 3 * x
                        ch.link(dve.tensor_tensor(shift[:, 0], nmax[:], lns[:], ALU.subtract))
                        lg = ln_gate[:, :, TJ * ba:TJ * ba + TJ].unsqueeze(2).broadcast_to([P, 2, 2, TJ])
                        ch.link(dve.tensor_tensor(shift[:, 1].rearrange("p r (h j) -> p r h j", h=2),
                                                  shift[:, 0].rearrange("p r (h j) -> p r h j", h=2), lg, ALU.add))
                        ch.link(dve.tensor_copy(shift_r[:, 0], shift[:, 1]))
                        dve.tensor_tensor(shift_r[:, 1], shift[:, 1], f32(shift_r[:, 0]), ALU.subtract).then_inc(st_ready, 1)

                    def aug(n):
                        if n == 0:
                            dve.wait_ge(t_ready, x + 1)
                            if not early(ita, ua, 2):
                                dve.wait_ge(pv_done, 8 * (x - 1))
                        s0 = where[("T", 0)]
                        dst = qb[D:P, ua % 2, n // 2, n % 2].rearrange("p (j n) -> p j n", j=TJ)
                        dve.tensor_tensor(dst, ps[0:D, s0, 0:P].unsqueeze(1).broadcast_to([D, TJ, P]),
                                          pick[:, n, :].unsqueeze(2).broadcast_to([D, TJ, P]), ALU.mult)\
                            .then_inc(aug_done, 1)

                    def masked(n):
                        w = min(WW, T - n * P)
                        pw = prob_w[:, n % 2, :, 0:w]
                        dve.wait_ge(wb_exp, 8 * (4 * it + u) + n + 1)
                        dve.tensor_tensor(pw, pw, mask_b[:, 0:w].unsqueeze(1).broadcast_to([P, 2, w]), ALU.min).then_inc(w_masked, 1)

                    for what, n in jobs(DVE_ORDER, b_on, a_on):
                        {"A": job_a, "K": masked, "M": win_max, "S": win_sum, "C": lambda _: shifts(), "G": aug}[what](n)
                stages(stage)(dve)

    def out_phase():
        NH = H * D // P
        with ExitStack() as c:
            raw = wo_raw
            wh = sb("woh", [P, NH, DM], F32R, c)
            wl_ = sb("wol", [P, NH, DM], F32R, c)
            o = sb("o", [P, 4, CH], F32, c)
            oh = sb("oh", [P, 4, CH], F32R, c)
            ol = sb("ol", [P, 4, CH], F32R, c)
            xr = sb("xr", [P, 2, 4, DM], F32, c)
            y = sb("y", [P, 2, CH], F32, c)
            yo = sb("yo", [P, 2, 4, DM], F32, c)
            o_in = [sem(f"o_in{n}", c) for n in range(4)]
            xr_in = [sem(f"xr_in{n}", c) for n in range(2)]
            woh_done = sem("woh_done", c)
            wol_done = sem("wol_done", c)
            oh_done = sem("oh_done", c)
            ol_done = sem("ol_done", c)
            s_part = sem("s_part", c)
            y_done = sem("y_done", c)
            y_turned = sem("y_turned", c)
            yo_done = sem("yo_done", c)
            stored = [sem(f"stored{n}", c) for n in range(2)]
            blk = c.enter_context(nc.Block())
            out_tok = out.rearrange("b (n p) d -> p (b n) d", p=P)

            @blk.sync
            def _(sp):
                for tc in range(NC):
                    for n in range(NH):
                        k = tc * NH + n
                        if k >= 4:
                            sp.wait_ge(ol_done, k - 3)
                        sp.dma_start(o[:, n % 4], o_scr[tc // 2, n * P:(n + 1) * P, (tc % 2) * CH:(tc % 2) * CH + CH]).then_inc(o_in[n % 4], 16)
                        if n == 0:
                            if tc >= 2:
                                sp.wait_ge(yo_done, tc - 1)
                            sp.dma_start(xr[:, tc % 2], x_tok[:, 4 * tc:4 * tc + 4, :]).then_inc(xr_in[tc % 2], 16)
                        if n == 15 and tc:
                            sp.wait_ge(yo_done, tc)
                            sp.dma_start(out_tok[:, 4 * tc - 4:4 * tc, :], yo[:, (tc - 1) % 2]).then_inc(stored[(tc - 1) % 2], 16)
                sp.wait_ge(yo_done, NC)
                sp.dma_start(out_tok[:, 4 * NC - 4:4 * NC, :], yo[:, (NC - 1) % 2]).then_inc(stored[(NC - 1) % 2], 16)
                for n in range(2):
                    sp.wait_ge(stored[n], 16 * NC // 2)

            @blk.tensor
            def _(pe):
                def turn(tc):
                    pe.wait_ge(y_done, tc + 1)
                    for t in range(4):
                        for ht in range(2):
                            ins = pe.transpose(ps[:, 4 + t // 2, (2 * (t % 2) + ht) * P:(2 * (t % 2) + ht + 1) * P],
                                               y[:, ht, t * P:(t + 1) * P], ident[:])
                    ins.then_inc(y_turned, 1)
                for tc in range(NC):
                    if tc >= 2:
                        pe.wait_ge(y_done, tc - 1)
                    for n in range(NH):
                        if tc == 0 and n % 4 == 0:
                            pe.wait_ge(wol_done, n // 4 + 1)
                        pe.wait_ge(ol_done, tc * NH + n + 1)
                        for ht in range(2):
                            hs = slice(ht * P, (ht + 1) * P)
                            prods = three(0, wh[:, n, hs], wl_[:, n, hs], oh[:, n % 4], ol[:, n % 4])
                            for k, (w, x) in enumerate(prods):
                                ins = pe.matmul(ps[:, 2 * (tc % 2) + ht, :], w, x, start=(n == 0 and k == 0),
                                                stop=(n == NH - 1 and k == 2))
                        ins.then_inc(s_part, 1)
                        if n == 6 and tc:
                            turn(tc - 1)
                turn(NC - 1)

            @blk.scalar
            def _(act):
                act.wait_ge(wo_in, 16)
                for n in range(4):
                    act.activation(wh[:, 4 * n:4 * n + 4], raw[:, 4 * n:4 * n + 4], ACT.Copy).then_inc(woh_done, 1)
                for k in range(NC * NH):
                    act.wait_ge(o_in[k % 4], 16 * (k // 4 + 1))
                    if k >= 4:
                        act.wait_ge(s_part, k - 3)
                    act.activation(oh[:, k % 4], o[:, k % 4], ACT.Copy).then_inc(oh_done, 1)

            @blk.vector
            def _(dve):
                def w_low(n):
                    rows = slice(4 * n, 4 * n + 4)
                    dve.wait_ge(woh_done, n + 1)
                    dve.tensor_tensor(wl_[:, rows], raw[:, rows], f32(wh[:, rows]), ALU.subtract).then_inc(wol_done, 1)

                def gated(tc):
                    dve.wait_ge(s_part, (tc + 1) * NH)
                    if tc:
                        dve.wait_ge(y_turned, tc)
                    dve.tensor_tensor(y[:], ps[:, 2 * (tc % 2):2 * (tc % 2) + 2, :], g_t[:, :, tc * CH:(tc + 1) * CH], ALU.mult)\
                        .then_inc(y_done, 1)

                def finish(tc):
                    dve.wait_ge(y_turned, tc + 1)
                    dve.wait_ge(xr_in[tc % 2], 16 * (tc // 2 + 1))
                    if tc >= 2:
                        dve.wait_ge(stored[tc % 2], 16 * (tc // 2))
                    yt = ps[:, 4:6, :].rearrange("p a (t d) -> p (a t) d", d=DM)
                    dve.tensor_tensor(yo[:, tc % 2], yt, xr[:, tc % 2], ALU.add).then_inc(yo_done, 1)
                for tc in range(NC):
                    for n in range(NH):
                        k = tc * NH + n
                        if tc == 0 and n % 4 == 0:
                            w_low(n // 4)
                        dve.wait_ge(oh_done, k + 1)
                        dve.tensor_tensor(ol[:, k % 4], o[:, k % 4], f32(oh[:, k % 4]), ALU.subtract).then_inc(ol_done, 1)
                        if n == 2 and tc:
                            gated(tc - 1)
                        if n == 10 and tc:
                            finish(tc - 1)
                gated(NC - 1)
                finish(NC - 1)

    with ExitStack() as mlp:
        hi = [mlp.enter_context(nc.sbuf_tensor(f"w_hi{m}", [P, F * DM // P // P, P], F32R)) for m in range(3)]
        lo = [mlp.enter_context(nc.sbuf_tensor(f"w_lo{m}", [P, F * DM // P // P, P], F32R)) for m in range(3)]
        norm_and_weights(hi, lo)
        mlp_phase(hi, lo)
    early_w.close()
    with ExitStack() as pre:
        sb("room", [P, 2, KT, HKV * D], F32, pre)
        wq_raw = sb("wq_raw", [P, KT, H * D], F32, pre)
        sb("room_kx", [P, B * HKV, T], F32, pre)
        wide = sb("wc_wide", [P, D, P], F32, pre)
    wide_zero = sem("wide_zero")
    wcv_in = sem("wcv_in")
    wide_done = sem("wide_done")
    wck_done = sem("wck_done")
    wq_in = sem("wq_in")
    with ExitStack() as comp:
        wvh_sb, wvl_sb = (sb(f"wv{n}", [P, KT, HKV * D], F32R, comp) for n in ("h", "l"))
        wc_raw = sb("wc_raw", [P, BS, D], F32, comp)
        kv_phase()
        compress_phase()
    query_phase()
    dense.close()
    wo_raw = sb("wo_raw", [P, H * D // P, DM], F32)
    wo_in = sem("wo_in")
    attention_phase()
    out_phase()


def constants():
    inv = 1.0 / 10000.0 ** (np.arange(0, D, 2, dtype=np.float32) / D)
    ang = np.outer(np.arange(T, dtype=np.float32), inv).T
    cos, sin = np.tile(np.cos(ang), (4, 1)), np.tile(np.sin(ang), (4, 1))
    rot = np.stack([np.stack([cos, sin], 1), np.stack([-sin, cos], 1)], 1).astype(np.float32)
    row = np.arange(P)[:, None]
    col = np.arange(WW)[None]
    mask_a = np.where((col > row) & (col <= row + WIN), 0.0, NEG).astype(np.float32)
    mask_b = np.where((col >= row) & (col < row + WIN), -NEG, 0.0).astype(np.float32)
    pick = np.tile(np.eye(4 * TJ, dtype=np.float32).reshape(4 * TJ, 4, TJ), (2, 1, 1))
    return {"mask_a": mask_a, "mask_b": mask_b, "pick": pick, "ident": np.eye(P, dtype=np.float32), "rot_k": rot, "rot_q": rot * np.float32(0.125)}


_INS = ['L0_attn_x', 'L0_attn_W_q', 'L0_attn_W_k', 'L0_attn_W_v', 'L0_attn_W_o', 'L0_attn_W_ck', 'L0_attn_W_cv',
        'L0_attn_W_gate', 'L0_ffn_gate_W_packed', 'L0_ffn_gate_scales', 'L0_ffn_up_W_packed',
        'L0_ffn_up_scales', 'L0_ffn_down_W_packed', 'L0_ffn_down_scales']


def kernel(**inputs):
    import numpy as _np
    import concourse.bacc as _bacc
    from concourse import mybir as _mybir
    from concourse.bass_utils import run_bass_kernel_spmd as _run

    nc = _bacc.Bacc("TRN2", target_bir_lowering=False, num_devices=1)
    arrays = {name: _np.ascontiguousarray(inputs[name]) for name in _INS}
    arrays.update(constants())
    args = {n: nc.dram_tensor(f"in_{n}", v.shape, _mybir.dt.from_np(v.dtype), kind="ExternalInput").ap()
            for n, v in arrays.items()}
    out = nc.dram_tensor("out_0", (B, T, DM), F32, kind="ExternalOutput").ap()
    build(nc, args, out)
    r = _run(nc, [{f"in_{n}": v for n, v in arrays.items()}], core_ids=[0])
    return r.results[0]["out_0"]
```
